# Optimizing a Trainium2 kernel written in Bass

```python
import numpy as np
import jax
import jax.numpy as jnp

def _softmax(x, axis=-1):
    return jax.nn.softmax(x, axis=axis)

def _gelu(x):
    return jax.nn.gelu(x, approximate=True)

def _silu(x):
    return jax.nn.silu(x)

def _sigmoid(x):
    return jax.nn.sigmoid(x)

def _layernorm(x, axis=-1, eps=1e-05):
    m = jnp.mean(x, axis=axis, keepdims=True)
    v = jnp.var(x, axis=axis, keepdims=True)
    return (x - m) / jnp.sqrt(v + eps)

def _scatter_add(tgt, idx, src, axis=0):
    return tgt.at[idx].add(src)

def _segment_sum(src, seg, n):
    return jax.ops.segment_sum(src, seg, n)
kernel_name = 'mk_gnn_resnorm_d4_gnn_r8_bc9730'

def setup_inputs(seed: int=0):
    np.random.seed(seed)
    _w = jnp.asarray

    def _rec_inputs():
        import jax
        import jax.numpy as jnp
        _gk = jax.random.key(seed)
        x = -0.000202 + 1 * jax.random.normal(jax.random.fold_in(_gk, 1), (12500, 64), jnp.float32)
        src = jax.random.randint(jax.random.fold_in(_gk, 2), (200000,), 0, 12500, jnp.int32)
        dst = jnp.minimum((12500 * jax.random.uniform(jax.random.fold_in(_gk, 3), (200000,)) ** 2.0).astype(jnp.int32), 99999)
        _o = jnp.argsort(dst, stable=True)
        src = src[_o]
        dst = dst[_o]
        edge_attr_2 = jax.random.uniform(jax.random.fold_in(_gk, 12), (200000, 2), jnp.float32, 0.0, 1)
        edge_type_16 = jax.random.randint(jax.random.fold_in(_gk, 14), (200000,), 0, 16, jnp.int32)
        return (x, src, dst, edge_attr_2, edge_type_16)
    x, src, dst, edge_attr_2, edge_type_16 = _rec_inputs()

    def _L0_gnn_setup():
        import jax, jax.numpy as jnp
        import numpy as np
        N_NODES = 12500
        N_EDGES = 200000
        IN_DIM = 64
        HID_DIM = 64
        OUT_DIM = 64

        def _glorot(key, shape):
            fan_in, fan_out = (shape[1], shape[0])
            lim = float(np.sqrt(6.0 / (fan_in + fan_out)))
            return jax.random.uniform(key, shape, jnp.float32, -lim, lim)

        def _graph_conv(x, src, dst, W_rel, b_rel, W_root):
            agg = jax.ops.segment_sum(x[src], dst, num_segments=N_NODES)
            return agg @ W_rel.T + b_rel + x @ W_root.T
        key = jax.random.key(seed)
        ks = jax.random.split(key, 8)
        x = jax.random.normal(ks[0], (N_NODES, IN_DIM), jnp.float32)
        edge_index = jax.random.randint(ks[1], (2, N_EDGES), 0, N_NODES, jnp.int64)
        return {'x': x, 'edge_index': edge_index, 'W_rel1': _glorot(ks[2], (HID_DIM, IN_DIM)), 'b_rel1': jnp.zeros((HID_DIM,), jnp.float32), 'W_root1': _glorot(ks[3], (HID_DIM, IN_DIM)), 'W_rel2': _glorot(ks[4], (OUT_DIM, HID_DIM)), 'b_rel2': jnp.zeros((OUT_DIM,), jnp.float32), 'W_root2': _glorot(ks[5], (OUT_DIM, HID_DIM))}
    _L0_gnn_all = _L0_gnn_setup()
    _L0_gnn_in = {k: v for k, v in _L0_gnn_all.items() if k in ('W_rel1', 'b_rel1', 'W_root1', 'W_rel2', 'b_rel2', 'W_root2')}
    del _L0_gnn_all

    def _L1_gnn_setup():
        import jax, jax.numpy as jnp
        import numpy as np
        N_NODES = 12500
        N_EDGES = 125000
        IN_DIM = 64
        OUT_DIM = 64
        BN_EPS = 1e-05
        key = jax.random.key(seed)
        ks = jax.random.split(key, 8)
        x = jax.random.normal(ks[0], (N_NODES, IN_DIM), dtype=jnp.float32)
        edge_index = jax.random.randint(ks[1], (2, N_EDGES), 0, N_NODES, dtype=jnp.int64)
        s1 = 1.0 / np.sqrt(IN_DIM)
        s2 = 1.0 / np.sqrt(OUT_DIM)
        W1 = jax.random.uniform(ks[2], (IN_DIM, OUT_DIM), jnp.float32, -s1, s1)
        b1 = jax.random.uniform(ks[3], (OUT_DIM,), jnp.float32, -s1, s1)
        W2 = jax.random.uniform(ks[4], (OUT_DIM, OUT_DIM), jnp.float32, -s2, s2)
        b2 = jax.random.uniform(ks[5], (OUT_DIM,), jnp.float32, -s2, s2)
        gamma = jnp.ones((OUT_DIM,), jnp.float32)
        beta = jnp.zeros((OUT_DIM,), jnp.float32)
        return {'x': x, 'edge_index': edge_index, 'W1': W1, 'b1': b1, 'W2': W2, 'b2': b2, 'gamma': gamma, 'beta': beta}
    _L1_gnn_all = _L1_gnn_setup()
    _L1_gnn_in = {k: v for k, v in _L1_gnn_all.items() if k in ('W1', 'b1', 'W2', 'b2', 'gamma', 'beta')}
    del _L1_gnn_all

    def _L2_gnn_setup():
        import jax, jax.numpy as jnp
        import numpy as np
        N_NODES = 12500
        N_EDGES = 125000
        IN_FEAT = 64
        OUT_FEAT = 64
        NUM_RELS = 16
        key = jax.random.key(seed)
        ks = jax.random.split(key, 7)
        xavier = np.sqrt(2.0) * np.sqrt(6.0 / (IN_FEAT + OUT_FEAT))
        feat = jax.random.normal(ks[0], (N_NODES, IN_FEAT), dtype=jnp.float32)
        weight = jax.random.uniform(ks[1], (NUM_RELS, IN_FEAT, OUT_FEAT), dtype=jnp.float32, minval=-xavier, maxval=xavier)
        h_bias = jnp.zeros((OUT_FEAT,), dtype=jnp.float32)
        loop_weight = jax.random.uniform(ks[2], (IN_FEAT, OUT_FEAT), dtype=jnp.float32, minval=-xavier, maxval=xavier)
        src = jax.random.randint(ks[3], (N_EDGES,), 0, N_NODES, dtype=jnp.int32)
        dst = jax.random.randint(ks[4], (N_EDGES,), 0, N_NODES, dtype=jnp.int32)
        etype = jax.random.randint(ks[5], (N_EDGES,), 0, NUM_RELS, dtype=jnp.int32)
        return {'feat': feat, 'weight': weight, 'h_bias': h_bias, 'loop_weight': loop_weight, 'src': src, 'dst': dst, 'etype': etype}
    _L2_gnn_all = _L2_gnn_setup()
    _L2_gnn_in = {k: v for k, v in _L2_gnn_all.items() if k in ('weight', 'h_bias', 'loop_weight')}
    del _L2_gnn_all

    def _L3_gnn_setup():
        import jax, jax.numpy as jnp
        import numpy as np
        K = 5

        def spline_conv(x, edge_index, pseudo, W, root, bias):
            N = x.shape[0]
            src, dst = (edge_index[0], edge_index[1])
            xk = jnp.einsum('ni,kio->nko', x, W)
            v = pseudo * (K - 1)
            bot = jnp.floor(v)
            frac = v - bot
            bot = bot.astype(jnp.int32)
            msg = jnp.zeros((src.shape[0], W.shape[2]), dtype=x.dtype)
            for s0 in (0, 1):
                for s1 in (0, 1):
                    b0 = frac[:, 0] if s0 else 1.0 - frac[:, 0]
                    b1 = frac[:, 1] if s1 else 1.0 - frac[:, 1]
                    basis = b0 * b1
                    idx = jnp.clip(bot[:, 0] + s0, 0, K - 1) + K * jnp.clip(bot[:, 1] + s1, 0, K - 1)
                    msg = msg + basis[:, None] * xk[src, idx]
            agg = jax.ops.segment_max(msg, dst, num_segments=N)
            agg = jnp.where(jnp.isfinite(agg), agg, jnp.zeros_like(agg))
            return agg + x @ root + bias
        key = jax.random.key(seed)
        ks = jax.random.split(key, 8)
        N, E, C = (6250, 200000, 64)
        Cin = C
        s = 1.0 / np.sqrt(25 * Cin)
        return {'x': jax.random.normal(ks[0], (N, C), dtype=jnp.float32), 'edge_index': jax.random.randint(ks[1], (2, E), 0, N, dtype=jnp.int32), 'edge_attr': jax.random.uniform(ks[2], (E, 2), dtype=jnp.float32), 'W1': jax.random.normal(ks[3], (25, C, C), dtype=jnp.float32) * s, 'root1': jax.random.normal(ks[4], (C, C), dtype=jnp.float32) / np.sqrt(C), 'bias1': jnp.zeros((C,), dtype=jnp.float32), 'W2': jax.random.normal(ks[5], (25, C, C), dtype=jnp.float32) * s, 'root2': jax.random.normal(ks[6], (C, C), dtype=jnp.float32) / np.sqrt(C), 'bias2': jnp.zeros((C,), dtype=jnp.float32)}
    _L3_gnn_all = _L3_gnn_setup()
    _L3_gnn_in = {k: v for k, v in _L3_gnn_all.items() if k in ('W1', 'root1', 'bias1', 'W2', 'root2', 'bias2')}
    del _L3_gnn_all
    return {'x': x, 'src': src, 'dst': dst, 'edge_attr_2': edge_attr_2, 'edge_type_16': edge_type_16, 'L0_gnn_W_rel1': _L0_gnn_in['W_rel1'], 'L0_gnn_b_rel1': _L0_gnn_in['b_rel1'], 'L0_gnn_W_root1': _L0_gnn_in['W_root1'], 'L0_gnn_W_rel2': _L0_gnn_in['W_rel2'], 'L0_gnn_b_rel2': _L0_gnn_in['b_rel2'], 'L0_gnn_W_root2': _L0_gnn_in['W_root2'], 'L1_gnn_W1': _L1_gnn_in['W1'], 'L1_gnn_b1': _L1_gnn_in['b1'], 'L1_gnn_W2': _L1_gnn_in['W2'], 'L1_gnn_b2': _L1_gnn_in['b2'], 'L1_gnn_gamma': _L1_gnn_in['gamma'], 'L1_gnn_beta': _L1_gnn_in['beta'], 'L2_gnn_weight': _L2_gnn_in['weight'], 'L2_gnn_h_bias': _L2_gnn_in['h_bias'], 'L2_gnn_loop_weight': _L2_gnn_in['loop_weight'], 'L3_gnn_W1': _L3_gnn_in['W1'], 'L3_gnn_root1': _L3_gnn_in['root1'], 'L3_gnn_bias1': _L3_gnn_in['bias1'], 'L3_gnn_W2': _L3_gnn_in['W2'], 'L3_gnn_root2': _L3_gnn_in['root2'], 'L3_gnn_bias2': _L3_gnn_in['bias2']}

def reference(x, src, dst, edge_attr_2, edge_type_16, L0_gnn_W_rel1, L0_gnn_b_rel1, L0_gnn_W_root1, L0_gnn_W_rel2, L0_gnn_b_rel2, L0_gnn_W_root2, L1_gnn_W1, L1_gnn_b1, L1_gnn_W2, L1_gnn_b2, L1_gnn_gamma, L1_gnn_beta, L2_gnn_weight, L2_gnn_h_bias, L2_gnn_loop_weight, L3_gnn_W1, L3_gnn_root1, L3_gnn_bias1, L3_gnn_W2, L3_gnn_root2, L3_gnn_bias2):
    import jax
    import jax.numpy as jnp

    def _L0_gnn_ref(x, edge_index, W_rel1, b_rel1, W_root1, W_rel2, b_rel2, W_root2):
        import jax, jax.numpy as jnp
        import numpy as np
        N_NODES = 12500
        N_EDGES = 200000
        IN_DIM = 64
        HID_DIM = 64
        OUT_DIM = 64

        def _glorot(key, shape):
            fan_in, fan_out = (shape[1], shape[0])
            lim = float(np.sqrt(6.0 / (fan_in + fan_out)))
            return jax.random.uniform(key, shape, jnp.float32, -lim, lim)

        def _graph_conv(x, src, dst, W_rel, b_rel, W_root):
            agg = jax.ops.segment_sum(x[src], dst, num_segments=N_NODES)
            return agg @ W_rel.T + b_rel + x @ W_root.T
        src, dst = (edge_index[0], edge_index[1])
        h = jax.nn.relu(_graph_conv(x, src, dst, W_rel1, b_rel1, W_root1))
        return _graph_conv(h, src, dst, W_rel2, b_rel2, W_root2)

    def _L1_gnn_ref(x, edge_index, W1, b1, W2, b2, gamma, beta):
        import jax, jax.numpy as jnp
        import numpy as np
        N_NODES = 12500
        N_EDGES = 125000
        IN_DIM = 64
        OUT_DIM = 64
        BN_EPS = 1e-05
        src, dst = (edge_index[0], edge_index[1])
        agg = jax.ops.segment_sum(x[src], dst, num_segments=N_NODES)
        h = x + agg
        h = jax.nn.relu(h @ W1 + b1) @ W2 + b2
        mean = jnp.mean(h, axis=0)
        var = jnp.var(h, axis=0)
        h = (h - mean) * jax.lax.rsqrt(var + BN_EPS) * gamma + beta
        return jax.nn.relu(h)

    def _L2_gnn_ref(feat, weight, h_bias, loop_weight, src, dst, etype):
        import jax, jax.numpy as jnp
        import numpy as np
        N_NODES = 12500
        N_EDGES = 125000
        IN_FEAT = 64
        OUT_FEAT = 64
        NUM_RELS = 16
        xproj = jnp.einsum('ni,rio->rno', feat, weight)
        m = xproj[etype, src]
        agg = jax.ops.segment_sum(m, dst, num_segments=feat.shape[0])
        return agg + h_bias + feat @ loop_weight

    def _L3_gnn_ref(x, edge_index, edge_attr, W1, root1, bias1, W2, root2, bias2):
        import jax, jax.numpy as jnp
        import numpy as np
        K = 5

        def spline_conv(x, edge_index, pseudo, W, root, bias):
            N = x.shape[0]
            src, dst = (edge_index[0], edge_index[1])
            xk = jnp.einsum('ni,kio->nko', x, W)
            v = pseudo * (K - 1)
            bot = jnp.floor(v)
            frac = v - bot
            bot = bot.astype(jnp.int32)
            msg = jnp.zeros((src.shape[0], W.shape[2]), dtype=x.dtype)
            for s0 in (0, 1):
                for s1 in (0, 1):
                    b0 = frac[:, 0] if s0 else 1.0 - frac[:, 0]
                    b1 = frac[:, 1] if s1 else 1.0 - frac[:, 1]
                    basis = b0 * b1
                    idx = jnp.clip(bot[:, 0] + s0, 0, K - 1) + K * jnp.clip(bot[:, 1] + s1, 0, K - 1)
                    msg = msg + basis[:, None] * xk[src, idx]
            agg = jax.ops.segment_max(msg, dst, num_segments=N)
            agg = jnp.where(jnp.isfinite(agg), agg, jnp.zeros_like(agg))
            return agg + x @ root + bias
        h = jax.nn.relu(spline_conv(x, edge_index, edge_attr, W1, root1, bias1))
        out = spline_conv(h, edge_index, edge_attr, W2, root2, bias2)
        return out
    edge_index = jnp.stack([src, dst])
    x = _layernorm(x + _L0_gnn_ref(x, edge_index, L0_gnn_W_rel1, L0_gnn_b_rel1, L0_gnn_W_root1, L0_gnn_W_rel2, L0_gnn_b_rel2, L0_gnn_W_root2), axis=-1)
    x = _layernorm(x + _L1_gnn_ref(x, edge_index, L1_gnn_W1, L1_gnn_b1, L1_gnn_W2, L1_gnn_b2, L1_gnn_gamma, L1_gnn_beta), axis=-1)
    x = _layernorm(x + _L2_gnn_ref(x, L2_gnn_weight, L2_gnn_h_bias, L2_gnn_loop_weight, src, dst, edge_type_16), axis=-1)
    x = _layernorm(x + _L3_gnn_ref(x, edge_index, edge_attr_2, L3_gnn_W1, L3_gnn_root1, L3_gnn_bias1, L3_gnn_W2, L3_gnn_root2, L3_gnn_bias2), axis=-1)
    return x

_drawn_inputs = setup_inputs


def setup_inputs(seed=0):
    import zlib

    import numpy as np

    out = dict(_drawn_inputs(seed))
    spreads = {'L0_gnn_b_rel1': (0.0, 0.1),
     'L0_gnn_b_rel2': (0.0, 0.8),
     'L1_gnn_gamma': (1.0, 0.2),
     'L1_gnn_beta': (0.0, 0.1),
     'L2_gnn_h_bias': (0.0, 0.537),
     'L3_gnn_bias1': (0.0, 0.1),
     'L3_gnn_bias2': (0.0, 0.1)}
    factors = {'L1_gnn_b1': 21.519, 'L1_gnn_b2': 64.0}
    for name, (base, spread) in spreads.items():
        noise = np.random.default_rng([zlib.crc32(name.encode()), seed]).standard_normal(out[name].shape)
        drawn = base * np.exp(spread * noise) if base else spread * noise
        out[name] = jnp.asarray(drawn.astype(out[name].dtype))
    for name, factor in factors.items():
        out[name] = (out[name] * factor).astype(out[name].dtype)
    return out
```

```python
from contextlib import ExitStack

import concourse.bass as bass
from concourse import mybir

F32 = mybir.dt.float32
BF16 = mybir.dt.bfloat16
I32 = mybir.dt.int32
U32 = mybir.dt.uint32
ALU = mybir.AluOpType
ACT = mybir.ActivationFunctionType
AX = mybir.AxisListType

P = 128
D = 64
N = 12500
E = 200000
RELS = 16
K = 5
CELLS = (K - 1) * (K - 1)
CORNERS = 4
EPS = 1e-5
BIG = 3.3e38

GT = 4
GROUPS = -(-E // (2 * GT * P))
GROUPS += GROUPS % 2
GP = GROUPS // 2
HALF = GROUPS * GT * P
EP = 2 * HALF
TILES = EP // P
NBLK = -(-TILES // P)
NAT = NBLK * P
FULLBLK = E // (P * P)
RESTROWS = (E - FULLBLK * P * P) // P
RESTCOLS = E % P

NT = -(-N // P)
NP = NT * P
LASTROWS = N - (NT - 1) * P
BT = 7
BATCHES = NT // BT
BP = BATCHES // 2
BW = BT * D
HIS = NT
BOX = GT * 2

CONVS = 6
SUM, MAX = 0, 1
MODE = [SUM, SUM, SUM, SUM, MAX, MAX]
CORNER_OF = [1, 1, 1, 1, CORNERS, CORNERS]
PRE_STEPS = 3
LN_STEPS = 7
POST_STEPS = [2, 2 + LN_STEPS, 1, 2 + LN_STEPS, 2, 2 + LN_STEPS]
BN_STEPS = 3 + LN_STEPS

TAB_STORES = [q * NT // 2 for q in range(4)]


def wait_for(eng, sem, value):
    if isinstance(value, int) and value <= 0:
        return
    eng.wait_ge(sem, value)


def build(nc, a, out):
    with ExitStack() as ctx:
        def sb(name, shape, dt):
            return ctx.enter_context(nc.sbuf_tensor(name, shape, dt))

        def sem(name):
            return ctx.enter_context(nc.semaphore(name))

        def pair(name):
            return [sem(f"{name}{k}") for k in range(2)]

        def dram(name, shape, dt=F32):
            return nc.dram_tensor(name, shape, dt, kind="Internal").ap()

        rows = dram("scanned_rows", [EP, D])
        h_table = dram("h_table", [NP, D])
        x1_table = dram("x1_table", [NP, D])
        rel_table = dram("rel_table", [NP * RELS, D])
        cell_table = dram("cell_table", [NP * CELLS, CORNERS * D])
        keep_sum = dram("keep_sum", [EP], BF16)
        keep_max = dram("keep_max", [EP], BF16)

        idx = [sb(f"idx{n}", [P, GROUPS, 2, GT], I32) for n in range(3)]
        basis = sb("basis", [P, GROUPS, BOX, CORNERS], F32)
        hi_t = sb("hi_t", [P, GROUPS, BOX], BF16)
        lo_t = sb("lo_t", [P, GROUPS, BOX], BF16)
        X = sb("X", [P, NT * D], F32)
        H = sb("H", [P, NT * D], F32)
        ident = sb("ident", [P, P], F32)
        ones = sb("ones", [P, P], F32)
        upto = sb("upto", [P, P], F32)
        iota_row = sb("iota_row", [P, P], BF16)
        iota_i = sb("iota_i", [P, P], I32)
        node_id = sb("node_id", [P, NT], F32)
        node_i = sb("node_i", [P, NT], I32)
        valid = sb("valid", [P, 1], F32)
        cut_dst_i = sb("cut_dst_i", [P, 2], I32)
        cut_dst = sb("cut_dst", [P, 2], F32)
        cnt = sb("cnt", [P, NT], F32)
        tot = sb("tot", [P, NT], F32)
        cum = sb("cum", [P, NT], F32)
        end_row = sb("end_row", [P, NT], I32)
        nonempty = sb("nonempty", [P, NT], F32)
        straddle = sb("straddle", [P, NT], F32)
        straddle_max = sb("straddle_max", [P, NT], F32)
        carry = sb("carry", [P, D], F32)
        w_pair = [sb(f"w_pair{c}", [P, D], F32) for c in range(CONVS)]
        w_raw = sb("w_raw", [D, 2, 2, D], F32)
        w2 = sb("w2", [D, D], F32)
        bias_in = ["L0_gnn_b_rel1", "L0_gnn_b_rel2", "L1_gnn_b2", "L2_gnn_h_bias", "L3_gnn_bias1", "L3_gnn_bias2"]
        bias = [sb(f"bias{c}", [P, D], F32) for c in range(CONVS)]
        gamma = sb("gamma", [P, D], F32)
        beta = sb("beta", [P, D], F32)
        b1_col = sb("b1_col", [D, 1], F32)
        w_table = sb("w_table", [D, K * K * D], F32)
        mean = sb("mean", [P, D], F32)
        rstd = sb("rstd", [P, D], F32)
        part = sb("part", [P, D], F32)
        scanned = sb("scanned", [P, 2, GT * P], F32)
        turned_rows = sb("turned_rows", [P, 2, 2, GT * D], F32)
        keep = sb("keep", [P, 2, GT * P], BF16)
        idx_now = sb("idx_now", [P, 2, 2, GT], I32)
        end_now = sb("end_now", [P, 2, BT], I32)
        agg = sb("agg", [P, 2, BW], F32)
        plain_rows = sb("plain_rows", [P, 2, BOX * D], F32)
        pre_a = sb("pre_a", [P, BW], F32)
        pre_b = sb("pre_b", [P, BW], F32)
        tmp_a = sb("tmp_a", [P, BW], F32)
        tmp_b = sb("tmp_b", [P, BW], F32)
        ln_c = sb("ln_c", [P, BW], F32)
        ln_s = sb("ln_s", [P, BT], F32)
        ln_m = sb("ln_m", [P, BT], F32)
        ln_v = sb("ln_v", [P, BT], F32)
        ln_e = sb("ln_e", [P, BT], F32)
        ln_d = sb("ln_d", [P, BT], F32)
        ln_r = sb("ln_r", [P, BT], F32)

        SLOT = BOX * CORNERS * D
        arena = sb("arena", [P, 4 * SLOT + 4 * BT * P], F32)
        at = [0]

        def carve(n):
            v = arena[:, at[0]:at[0] + n]
            at[0] += n
            return v

        gathered = [carve(SLOT) for _ in range(2)]
        weighted = [carve(SLOT) for _ in range(2)]
        table_out = [arena[:, 2 * k * SLOT:2 * (k + 1) * SLOT] for k in range(2)]
        zin = [carve(BT * P) for _ in range(2)]
        zt = [carve(BT * P) for _ in range(2)]
        onehot = [w.bitcast(BF16) for w in weighted]
        hi_hot = [o[:, 0:BOX * HIS].rearrange("p (t v) -> p t v", v=HIS) for o in onehot]
        lo_hot = [o[:, BOX * HIS:BOX * (HIS + P)].rearrange("p (t v) -> p t v", v=P) for o in onehot]
        nats = [arena[:, n * NAT:(n + 1) * NAT] for n in range(7)] + [H[:, n * NAT:(n + 1) * NAT] for n in range(3)]
        nats += [X[:, n * NAT:(n + 1) * NAT] for n in (1, 2)]
        keep_nat = [X[:, n * NAT // 2:(n + 1) * NAT // 2].bitcast(BF16) for n in range(2)]
        xs, xt = zin, zt
        u_t = [w[0:D, 0:BT * P] for w in weighted]

        PS = ctx.enter_context(nc.psum_tensor("PS", [P, 8, 512], F32))
        turn_ps = [PS[:, k, :] for k in range(2)]
        back_ps = [PS[:, 2 + k, :] for k in range(2)]
        hist_ps = PS[:, 4, 0:HIS]
        flip_ps = [PS[:, 5 + k, :] for k in range(2)]
        scratch_ps = PS[:, 7, :]
        zt_ps = [PS[:, 2 * k:2 * k + 2, :].rearrange("p a b -> p (a b)")[:, 0:BT * P] for k in range(2)]
        y_ps = [PS[:, 4 + k, 0:BW] for k in range(2)]
        u_ps = PS[0:D, 6:8, 0:BW]
        xt_ps = PS[0:D, 0:2, :].rearrange("p a b -> p (a b)")[:, 0:BT * P]
        rel_ps = [PS[:, 2 + h, :] for h in range(2)]
        knot_ps = [PS[:, 2 + r, 0:K * D] for r in range(K)]

        s_pads = sem("pads_set")
        s_src = sem("src_in")
        s_nat = sem("edge_arrays_in")
        s_consts = sem("constants")
        s_weights = sem("weights_in")
        s_x = sem("x_in")
        s_xpad = sem("x_pad")
        s_setup = sem("setup_steps")
        s_marks = sem("segment_marks")
        s_array = sem("edge_values_ready")
        s_flip = sem("flipped")
        s_flipped = sem("flip_taken")
        s_keep_dram = sem("keep_in_dram")
        s_wt = sem("weights_turned")
        s_wt_taken = sem("turned_weights_taken")
        s_idx = pair("idx_staged")
        s_rows_in = [pair("rows_gathered_a"), pair("rows_gathered_b")]
        s_weighted = pair("rows_weighted")
        s_turned = pair("rows_turned")
        s_keep = pair("keep_in")
        s_scanned = pair("scanned")
        s_back = pair("turned_back")
        s_taken = pair("back_taken")
        s_stored = pair("rows_stored")
        s_onehot = pair("onehots")
        s_hist = pair("counted")
        s_histz = sem("counts_cleared")
        s_find = sem("last_edges_steps")
        s_pref = sem("prefix_sums")
        s_found = sem("last_edges_found")
        s_carry = sem("carry_in")
        s_end = pair("end_rows_staged")
        s_agg = pair("aggregates_in")
        s_pre_step = sem("pre_steps")
        s_pre = pair("aggregate_fixed")
        s_zx = pair("node_part")
        s_zt = pair("batch_turned")
        s_ztc = pair("turned_batch_taken")
        s_u = sem("hidden")
        s_uc = sem("hidden_taken")
        s_mm = pair("products")
        s_post_step = sem("post_steps")
        s_var = sem("variance")
        s_std = sem("deviation")
        s_post = pair("batch_done")
        s_out = sem("batches_stored")
        s_bn = sem("batch_norm_steps")
        s_bnp = sem("batch_norm_sums")
        s_x2 = sem("normed_batches")
        s_wtab = sem("table_weights_in")
        s_xs = pair("batch_staged")
        s_xt = sem("table_batch_turned")
        s_bnt = sem("batch_norm_totals")
        s_bnv = sem("batch_norm_variance")
        s_bns = sem("batch_norm_deviation")
        s_xtc = pair("table_batch_taken")
        s_tab = pair("table_half")
        s_tabc = pair("table_half_taken")
        s_tabd = [sem(f"table_stored{k}") for k in range(2)]
        block = ctx.enter_context(nc.Block())

        rows_w = rows.rearrange("(h g p j) c -> p h g (j c)", h=2, g=GROUPS, p=P)
        keeps = [k.rearrange("(h g c) -> h g c", h=2, g=GROUPS) for k in (keep_sum, keep_max)]
        cell_v = cell_table.rearrange("(t p r) c -> t p (r c)", p=P, r=CELLS)
        rel_v = rel_table.rearrange("(t p r) c -> t p (r c)", p=P, r=RELS)
        h_v = h_table.rearrange("(t p) c -> p t c", p=P)
        x1_v = x1_table.rearrange("(t p) c -> p t c", p=P)
        tables = [a["x"], h_table, x1_table, rel_table, cell_table, cell_table]
        idx_of = [idx[0], idx[0], idx[0], idx[1], idx[2], idx[2]]
        x3d = X[:, :].rearrange("p (t c) -> p t c", c=D)
        TABLE_OF = {3: 0, 4: 1, 5: 2}
        NORMED = {1: 0, "bn": 1, 3: 2, 5: 3}
        KNOT_ROWS = [(0, 1, 2), (3, 4)]
        SRC_OF = [X, X, H]
        NODE_OF = [X, H, X, X, X, H]
        RES_OF = [H, X, H, X, H, X]

        def edge_use(c, i):
            return c * GP + i

        def max_use(c, i):
            return (c - MODE.index(MAX)) * GP + i

        def node_use(c, i):
            return c * BP + i

        def groups(eng, body):
            for k in range(2):
                body(0, k)
            with eng.Fori(1, GP - 1) as i:
                for k in range(2):
                    body(i, k)
            for k in range(2):
                body(GP - 1, k)

        def batches(eng, body):
            for k in range(2):
                body(0, k)
            with eng.Fori(1, BP - 1) as i:
                for k in range(2):
                    body(i, k)
            for k in range(2):
                body(BP - 1, k)

        def before(i, k):
            return (i, 0) if k == 1 else (i - 1, 1)

        def cols(i, k, width):
            return bass.ds((2 * i + k) * width, width)

        WEIGHT_DMAS = 2 + 4 + 3 + 3 + CONVS + 3

        def by_tile(dst):
            return dst.rearrange("p g (h j) -> p g h j", h=2)

        FLIPS = [(nats[6], idx[0]), (nats[2], by_tile(hi_t)), (nats[1], by_tile(lo_t)), (nats[3], idx[1]), (nats[6], idx[2])]
        FLIPS += [(nats[n], by_tile(basis[:, :, :, s])) for s, n in enumerate((7, 8, 9, 10))]
        CHUNKS = [(b, min(4, NBLK - b)) for b in range(0, NBLK, 4)]

        def take_table(eng, copy, mine, q, i, u, h):
            eng.wait_ge(s_tab[h], q * NT + 2 * BT * i + u + 1)
            wait_for(eng, s_tabd[u % 2], 16 * (TAB_STORES[q] + BT * i + u // 2))
            if q == 0:
                copy(table_out[u % 2][:, h * 512:(h + 1) * 512], rel_ps[h]).then_inc(s_tabc[h], 2)
                return
            cells = table_out[u % 2].rearrange("p (b a s c) -> p b a s c", b=K - 1, a=K - 1, s=2)
            done = []
            for r in mine:
                for corner in range(2):
                    if 0 <= r - corner < K - 1:
                        v = knot_ps[r]
                        knots = bass.AP(v.tensor, v.offset, [v.ap[0], [D, K - 1], [1, 2 * D]])
                        done.append(copy(cells[:, r - corner, :, corner, :], knots))
            done[-1].then_inc(s_tabc[h], 1)

        @block.gpsimd
        def _(pool):
            pool.iota(iota_i[:, :], [[1, P]], base=0, channel_multiplier=0).then_inc(s_consts, 1)
            pool.iota(node_i[:, :], [[P, NT]], base=0, channel_multiplier=1).then_inc(s_consts, 1)
            pool.memset(ident[:, :], 0.0).then_inc(s_consts, 1)
            pool.memset(ones[:, :], 1.0).then_inc(s_consts, 1)
            pool.wait_ge(s_consts, 4)
            pool.affine_select(out=ident[:, :], in_=ident[:, :], compare_op=ALU.not_equal, fill=1.0, base=0,
                               pattern=[[-1, P]], channel_multiplier=1).then_inc(s_consts, 1)
            pool.affine_select(out=upto[:, :], in_=ones[:, :], compare_op=ALU.is_ge, fill=0.0, base=0,
                               pattern=[[1, P]], channel_multiplier=-1).then_inc(s_consts, 1)
            pool.affine_select(out=valid[:, :], in_=ones[:, 0:1], compare_op=ALU.is_ge, fill=0.0, base=LASTROWS - 1,
                               pattern=[[0, 1]], channel_multiplier=-1).then_inc(s_consts, 1)

            for c in range(CONVS):
                width = CORNER_OF[c] * D
                if c in (1, 2):
                    pool.wait_ge(s_out, 16 * BATCHES * c)
                if c in TABLE_OF:
                    n = TABLE_OF[c]
                    for k in range(2):
                        pool.wait_ge(s_tabd[k], 16 * TAB_STORES[n + 1])

                def gather_group(i, k):
                    n = edge_use(c, i)
                    pool.wait_ge(s_idx[k], n + 1)
                    if MODE[c] == SUM:
                        wait_for(pool, s_turned[k], n)
                    else:
                        wait_for(pool, s_weighted[k], max_use(c, i))
                    pool.nop(nofuse=True)
                    for j in range(GT):
                        for h in range(2):
                            t = 2 * j + h
                            into = plain_rows[:, k, :] if MODE[c] == SUM else gathered[k]
                            pool.indirect_dma_start(
                                into[:, t * width:(t + 1) * width], None, tables[c],
                                bass.IndirectOffsetOnAxis(ap=idx_now[:, k, h, j:j + 1].bitcast(U32), axis=0),
                            ).then_inc(s_rows_in[c // 3][k], 16)

                groups(pool, gather_group)
                for k in range(2):
                    pool.wait_ge(s_stored[k], 16 * GP * (c + 1))

                def gather_batch(i, k):
                    m = node_use(c, i)
                    pool.wait_ge(s_end[k], m + 1)
                    wait_for(pool, s_pre[k], m)
                    pool.nop(nofuse=True)
                    for t in range(BT):
                        pool.indirect_dma_start(
                            agg[:, k, t * D:(t + 1) * D], None, rows,
                            bass.IndirectOffsetOnAxis(ap=end_now[:, k, t:t + 1].bitcast(U32), axis=0),
                        ).then_inc(s_agg[k], 16)

                batches(pool, gather_batch)

        @block.sync
        def _(sp):
            sp.wait_ge(s_pads, 6)
            def load_edges(tile_, src, w, arrived):
                v = tile_.rearrange("p (b c) -> p b c", b=NBLK)
                n = FULLBLK * P * P
                full = src[0:n * w].rearrange("(b r c) -> r b c", r=P, c=P * w)
                sp.dma_start(v[:, 0:FULLBLK, :], full).then_inc(arrived, 16)
                sp.dma_start(v[0:RESTROWS, FULLBLK, :],
                             src[n * w:(n + RESTROWS * P) * w].rearrange("(r c) -> r c", c=P * w)).then_inc(arrived, 16)
                sp.dma_start(v[RESTROWS:RESTROWS + 1, FULLBLK, 0:RESTCOLS * w],
                             src[(n + RESTROWS * P) * w:E * w].rearrange("(r c) -> r c", r=1)).then_inc(arrived, 16)
            load_edges(nats[0].bitcast(I32), a["src"], 1, s_src)
            load_edges(nats[1].bitcast(I32), a["dst"], 1, s_nat)
            v = nats[2].bitcast(I32).rearrange("p (b c) -> p b c", b=NBLK)
            sp.dma_start(v[0:1, 0, 1:P], a["dst"][0:P - 1].rearrange("(r c) -> r c", r=1)).then_inc(s_nat, 16)
            sp.dma_start(v[1:P, 0, :], a["dst"][P - 1:P * P - 1].rearrange("(r c) -> r c", c=P)).then_inc(s_nat, 16)
            sp.dma_start(v[:, 1:FULLBLK, :], a["dst"][P * P - 1:FULLBLK * P * P - 1].rearrange(
                "(b r c) -> r b c", r=P, c=P)).then_inc(s_nat, 16)
            sp.dma_start(v[0:RESTROWS, FULLBLK, :],
                         a["dst"][FULLBLK * P * P - 1:(FULLBLK * P + RESTROWS) * P - 1].rearrange(
                             "(r c) -> r c", c=P)).then_inc(s_nat, 16)
            sp.dma_start(v[RESTROWS:RESTROWS + 1, FULLBLK, 0:RESTCOLS],
                         a["dst"][(FULLBLK * P + RESTROWS) * P - 1:E - 1].rearrange("(r c) -> r c", r=1)).then_inc(s_nat, 16)
            load_edges(nats[3].bitcast(I32), a["edge_type_16"], 1, s_nat)
            load_edges(arena[:, 4 * NAT:6 * NAT], a["edge_attr_2"].rearrange("e c -> (e c)"), 2, s_nat)
            for h in range(2):
                sp.dma_start(cut_dst_i[:, h:h + 1], a["dst"][HALF - 1 + h:HALF + h].rearrange("(r c) -> r c", r=1)
                             .broadcast_to([P, 1])).then_inc(s_weights, 16)
            for n in range(2):
                sp.dma_start(w_raw[:, n, 0, :], a[f"L0_gnn_W_rel{n + 1}"]).then_inc(s_weights, 16)
                sp.dma_start(w_raw[:, n, 1, :], a[f"L0_gnn_W_root{n + 1}"]).then_inc(s_weights, 16)
            sp.dma_start(w_pair[2][0:D, :], a["L1_gnn_W1"]).then_inc(s_weights, 16)
            sp.dma_start(w_pair[2][D:P, :], a["L1_gnn_W1"]).then_inc(s_weights, 16)
            sp.dma_start(w2[:, :], a["L1_gnn_W2"]).then_inc(s_weights, 16)
            for c, name in ((3, "L2_gnn_loop_weight"), (4, "L3_gnn_root1"), (5, "L3_gnn_root2")):
                sp.dma_start(w_pair[c][D:P, :], a[name]).then_inc(s_weights, 16)
            for c in range(CONVS):
                sp.dma_start(bias[c][:, :], a[bias_in[c]].rearrange("(r c) -> r c", r=1)
                             .broadcast_to([P, D])).then_inc(s_weights, 16)
            sp.dma_start(gamma[:, :], a["L1_gnn_gamma"].rearrange("(r c) -> r c", r=1)
                         .broadcast_to([P, D])).then_inc(s_weights, 16)
            sp.dma_start(beta[:, :], a["L1_gnn_beta"].rearrange("(r c) -> r c", r=1)
                         .broadcast_to([P, D])).then_inc(s_weights, 16)
            sp.dma_start(b1_col[:, :], a["L1_gnn_b1"].rearrange("(r c) -> r c", c=1)).then_inc(s_weights, 16)
            sp.wait_ge(s_marks, 1)
            for n in range(2):
                blocks = TILES // P
                v = keep_nat[n].rearrange("p (b c) -> p b c", b=NBLK)
                dst = (keep_sum, keep_max)[n]
                sp.dma_start(dst[0:blocks * P * P].rearrange("(b r c) -> r b c", r=P, c=P),
                             v[:, 0:blocks, :]).then_inc(s_keep_dram, 16)
                sp.dma_start(dst[blocks * P * P:EP].rearrange("(r c) -> r c", c=P),
                             v[0:TILES - blocks * P, blocks, :]).then_inc(s_keep_dram, 16)
            sp.wait_ge(s_keep_dram, 64)
            def table_weights(c):
                n = TABLE_OF[c]
                if n == 0:
                    sp.dma_start(w_table[:, 0:RELS * D].rearrange("i (r o) -> i r o", o=D),
                                 a["L2_gnn_weight"].rearrange("r i o -> i r o")).then_inc(s_wtab, 16)
                else:
                    sp.dma_start(w_table[:, :].rearrange("i (r o) -> i r o", o=D),
                                 a[f"L3_gnn_W{n}"].rearrange("r i o -> i r o")).then_inc(s_wtab, 16)

            for c in range(CONVS):
                marks = keeps[MODE[c]]

                def load_keep(i, k):
                    n = edge_use(c, i)
                    wait_for(sp, s_scanned[k], n)
                    for h in range(2):
                        src = marks[h:h + 1, bass.ds(2 * i + k, 1), :].rearrange("a b c -> (a b) c")
                        sp.dma_start(keep[h * D:(h + 1) * D, k, :], src.broadcast_to([D, GT * P])).then_inc(s_keep[k], 16)

                def store_rows(i, k):
                    n = edge_use(c, i)
                    sp.wait_ge(s_taken[k], n + 1)
                    sp.dma_start(rows_w[:, :, bass.ds(2 * i + k, 1), :].rearrange("p h g c -> p h (g c)"),
                                 turned_rows[:, k, :, :]).then_inc(s_stored[k], 16)

                if c + 1 in TABLE_OF:
                    table_weights(c + 1)
                for k in range(2):
                    load_keep(0, k)
                with sp.Fori(1, GP) as i:
                    for k in range(2):
                        store_rows(i - 1, k)
                        load_keep(i, k)
                for k in range(2):
                    store_rows(GP - 1, k)
                for k in range(2):
                    sp.wait_ge(s_stored[k], 16 * GP * (c + 1))
                sp.dma_start(carry[:, :], rows[HALF - 1:HALF, :].broadcast_to([P, D])).then_inc(s_carry, 16)
                if c in (0, 1, 5):
                    res = RES_OF[c][:, :].rearrange("p (t c) -> p t c", c=D)
                    def store_batch(i, k):
                        m = node_use(c, i)
                        sp.wait_ge(s_post[k], m + 1)
                        t = bass.ds((2 * i + k) * BT, BT)
                        dst = h_v if c == 0 else x1_v
                        if c < 5:
                            sp.dma_start(dst[:, t, :], res[:, t, :]).then_inc(s_out, 16)
                        elif isinstance(i, int) and (i, k) == (BP - 1, 1):
                            t0 = NT - BT
                            sp.dma_start(out[t0 * P:(NT - 1) * P, :].rearrange("(t p) c -> p t c", p=P),
                                         res[:, t0:NT - 1, :]).then_inc(s_out, 16)
                            sp.dma_start(out[(NT - 1) * P:N, :], res[0:LASTROWS, NT - 1, :]).then_inc(s_out, 16)
                        else:
                            sp.dma_start(out[bass.ds((2 * i + k) * BT * P, BT * P), :].rearrange("(t p) c -> p t c", p=P),
                                         res[:, t, :]).then_inc(s_out, 16)
                    batches(sp, store_batch)
                if c + 1 in TABLE_OF:
                    q = TABLE_OF[c + 1]

                    def store_table(i, u):
                        for h in range(2):
                            sp.wait_ge(s_tabc[h], 2 * (q * NT + 2 * BT * i + u + 1))
                        tile_, t = table_out[u % 2], bass.ds(2 * BT * i + u, 1)
                        if q == 0:
                            sp.dma_start(rel_v[t].rearrange("t p c -> (t p) c"),
                                         tile_[:, 0:RELS * D]).then_inc(s_tabd[u % 2], 16)
                        else:
                            sp.dma_start(cell_v[t].rearrange("t p c -> (t p) c"), tile_).then_inc(s_tabd[u % 2], 16)

                    with sp.Fori(0, BP) as i:
                        for u in range(2 * BT):
                            store_table(i, u)
            sp.wait_ge(s_out, 16 * (3 * BATCHES + 1))

        @block.scalar
        def _(act):
            def take_flips(n):
                for q, (b, nb) in enumerate(CHUNKS):
                    f = n * len(CHUNKS) + q
                    act.wait_ge(s_flip, f + 1)
                    done = []
                    for h in range(2):
                        t0, t1 = max(b * P, h * TILES // 2), min((b + nb) * P, (h + 1) * TILES // 2)
                        if t0 < t1:
                            g0, g1 = (t0 - h * TILES // 2) // GT, (t1 - h * TILES // 2) // GT
                            done.append(nc.scalar.copy(
                                FLIPS[n][1][:, g0:g1, h, :],
                                flip_ps[f % 2][:, t0 - b * P:t1 - b * P].rearrange("p (g j) -> p g j", j=GT)))
                    done[-1].then_inc(s_flipped, 1)

            def stage_rows(c, i, k):
                if c == 3 and isinstance(i, int) and i == 0:
                    act.wait_ge(s_rows_in[0][k], 16 * BOX * edge_use(3, 0))
                else:
                    wait_for(act, s_rows_in[c // 3][k], 16 * BOX * edge_use(c % 3, i))
                act.nop(nofuse=True)
                nc.scalar.copy(idx_now[:, k, :, :],
                               idx_of[c][:, bass.ds(2 * i + k, 1), :, :].rearrange("p g h j -> p (g h) j")
                               ).then_inc(s_idx[k], 1)

            take_flips(0)
            act.wait_ge(s_flipped, len(CHUNKS))
            for k in range(2):
                stage_rows(0, 0, k)
            for n in range(1, len(FLIPS)):
                take_flips(n)
            act.wait_ge(s_xpad, 1)
            act.dma_start(x3d[:, 0:NT - 1, :], a["x"][0:(NT - 1) * P, :].rearrange("(t p) c -> p t c", p=P)).then_inc(s_x, 16)
            act.dma_start(x3d[0:LASTROWS, NT - 1, :], a["x"][(NT - 1) * P:N, :]).then_inc(s_x, 16)

            for c in range(CONVS):
                def take_back(i, k):
                    n = edge_use(c, i)
                    act.wait_ge(s_back[k], n + 1)
                    wait_for(act, s_stored[k], 16 * n)
                    nc.scalar.copy(turned_rows[:, k, :, :].rearrange("p h (j c) -> p j h c", j=GT),
                                   back_ps[k].rearrange("p (j h c) -> p j h c", j=GT, h=2)).then_inc(s_taken[k], 1)

                def edge_step(i, k):
                    if not (isinstance(i, int) and i == GP - 1):
                        stage_rows(c, i + 1, k)
                    if not (isinstance(i, int) and (i, k) == (0, 0)):
                        take_back(*before(i, k))

                if c > 0:
                    for k in range(2):
                        stage_rows(c, 0, k)
                groups(act, edge_step)
                take_back(GP - 1, 1)

                def stage_ends(i, k):
                    m = node_use(c, i)
                    wait_for(act, s_agg[k], 16 * BT * m)
                    act.nop(nofuse=True)
                    nc.scalar.copy(end_now[:, k, :], end_row[:, cols(i, k, BT)]).then_inc(s_end[k], 1)

                def deviation():
                    nc.scalar.activation(ln_d[:, :], ln_e[:, :], ACT.Sqrt).then_inc(s_std, 1)

                def norm_count(c_, i, k):
                    return c_ * BATCHES + 2 * i + k

                def node_step(i, k):
                    m = node_use(c, i)
                    wait_for(act, s_zt[k], m)
                    act.nop(nofuse=True)
                    nc.scalar.copy(zin[k].rearrange("p (t c) -> p t c", c=P)[:, :, D:P],
                                   NODE_OF[c][:, cols(i, k, BW)].rearrange("p (t c) -> p t c", c=D)).then_inc(s_zx[k], 1)
                    if not (isinstance(i, int) and i == BP - 1):
                        stage_ends(i + 1, k)
                    act.wait_ge(s_zt[k], m + 1)
                    wait_for(act, s_mm[k], m)
                    nc.scalar.copy(zt[k], zt_ps[k]).then_inc(s_ztc[k], 1)
                    if c == 2:
                        b = 2 * i + k
                        act.wait_ge(s_u, b + 1)
                        nc.scalar.activation(u_t[k].rearrange("p (a b) -> p a b", a=2), u_ps, ACT.Relu,
                                             bias=b1_col[:, 0:1]).then_inc(s_uc, 1)
                    if c in NORMED and not (isinstance(i, int) and (i, k) == (0, 0)):
                        act.wait_ge(s_var, norm_count(NORMED[c], *before(i, k)) + 1)
                        deviation()

                if c == 0:
                    act.wait_ge(s_found, 1)
                    act.wait_ge(s_x, 32)
                for k in range(2):
                    stage_ends(0, k)
                batches(act, node_step)
                if c in NORMED:
                    act.wait_ge(s_var, norm_count(NORMED[c], BP - 1, 1) + 1)
                    deviation()
                if c == 2:
                    act.wait_ge(s_bnv, 1)
                    nc.scalar.activation(part[:, :], rstd[:, :], ACT.Sqrt).then_inc(s_bns, 1)
                if c + 1 in TABLE_OF:
                    q = TABLE_OF[c + 1]
                    for k in range(2):
                        act.wait_ge(s_post[k], BP * (c + 1))

                    def table_step(i, k):
                        r = q * BP + i
                        if q == 0:
                            act.wait_ge(s_var, norm_count(NORMED["bn"], i, k) + 1)
                            deviation()
                            act.wait_ge(s_x2, 2 * i + k + 1)
                        wait_for(act, s_xt, 2 * r + k - 1)
                        act.nop(nofuse=True)
                        nc.scalar.copy(xs[k][:, 0:BW], SRC_OF[q][:, cols(i, k, BW)]).then_inc(s_xs[k], 1)
                        act.wait_ge(s_xt, 2 * r + k + 1)
                        nc.scalar.copy(xt[k][0:D, :], xt_ps).then_inc(s_xtc[k], 1)
                        for t in range(BT):
                            for h in range(2):
                                take_table(act, nc.scalar.copy, ((1,), (3,))[h], q, i, k * BT + t, h)

                    batches(act, table_step)

        @block.tensor
        def _(pe):
            pe.wait_ge(s_consts, 7)
            for n in range(len(FLIPS)):
                pe.wait_ge(s_array, n + 1)
                for q, (b, nb) in enumerate(CHUNKS):
                    f = n * len(CHUNKS) + q
                    if f >= 2:
                        pe.wait_ge(s_flipped, f - 1)
                    for j in range(nb):
                        last = nc.tensor.transpose(flip_ps[f % 2][:, j * P:(j + 1) * P],
                                                   FLIPS[n][0][:, (b + j) * P:(b + j + 1) * P], ident[:, :])
                    last.then_inc(s_flip, 1)
            pe.wait_ge(s_weights, 16 * WEIGHT_DMAS)
            for n in range(2):
                last = nc.tensor.transpose(scratch_ps[:, n * D:(n + 1) * D],
                                           w_raw[:, n, :, :].rearrange("o a i -> o (a i)"), ident[0:D, 0:D])
            last.then_inc(s_wt, 1)

            for c in range(CONVS):
                def turn(i, k):
                    n = edge_use(c, i)
                    if MODE[c] == SUM:
                        pe.wait_ge(s_rows_in[c // 3][k], 16 * BOX * (edge_use(c % 3, i) + 1))
                    else:
                        pe.wait_ge(s_weighted[k], max_use(c, i) + 1)
                    wait_for(pe, s_scanned[k], n)
                    pe.nop(nofuse=True)
                    if MODE[c] == SUM:
                        v = plain_rows[:, k, :].rearrange("p (j q) -> p j q", j=GT)
                        for j in range(GT):
                            last = nc.tensor.transpose(turn_ps[k][:, j * P:(j + 1) * P], v[:, j, :], ident[:, :])
                        last.then_inc(s_turned[k], 1)
                    else:
                        v = weighted[k].rearrange("p (j s q) -> p j s q", j=GT, s=CORNERS)
                        for j in range(GT):
                            for s in range(CORNERS):
                                last = nc.tensor.matmul(turn_ps[k][:, j * P:(j + 1) * P], v[:, j, s, :],
                                                        ident[:, :], start=(s == 0), stop=(s == CORNERS - 1))
                        last.then_inc(s_turned[k], 1)

                def count(i, k):
                    pe.wait_ge(s_onehot[k], i + 1)
                    first, end = isinstance(i, int) and (i, k) == (0, 0), isinstance(i, int) and (i, k) == (GP - 1, 1)
                    for t in range(BOX):
                        last = nc.tensor.matmul(hist_ps, lo_hot[k][:, t, :], hi_hot[k][:, t, :],
                                                start=first and t == 0, stop=end and t == BOX - 1,
                                                skip_group_check=True)
                    last.then_inc(s_hist[k], 1)

                def turn_back(i, k):
                    n = edge_use(c, i)
                    pe.wait_ge(s_scanned[k], n + 1)
                    wait_for(pe, s_taken[k], n)
                    pe.nop(nofuse=True)
                    v = scanned[:, k, :].rearrange("q (p j) -> q j p", j=GT)
                    for j in range(GT):
                        last = nc.tensor.transpose(back_ps[k][:, j * P:(j + 1) * P], v[:, j, :], ident[:, :])
                    last.then_inc(s_back[k], 1)

                def edge_step(i, k):
                    turn(i, k)
                    if c == 0:
                        count(i, k)
                    if not (isinstance(i, int) and (i, k) == (0, 0)):
                        turn_back(*before(i, k))

                groups(pe, edge_step)
                turn_back(GP - 1, 1)

                if c == 0:
                    pe.wait_ge(s_wt_taken, 1)
                    pe.wait_ge(s_find, 1)
                    nc.tensor.matmul(scratch_ps[:, 0:NT], upto[:, :], cnt[:, :], start=True, stop=True)
                    nc.tensor.matmul(scratch_ps[:, P:P + NT], ones[:, :], cnt[:, :], start=True,
                                     stop=True).then_inc(s_pref, 1)

                def node_step(i, k):
                    m = node_use(c, i)
                    pe.wait_ge(s_pre[k], m + 1)
                    pe.wait_ge(s_zx[k], m + 1)
                    wait_for(pe, s_ztc[k], m)
                    pe.nop(nofuse=True)
                    for t in range(BT):
                        last = nc.tensor.transpose(zt_ps[k][:, t * P:(t + 1) * P], zin[k][:, t * P:(t + 1) * P],
                                                   ident[:, :])
                    last.then_inc(s_zt[k], 1)
                    pe.wait_ge(s_ztc[k], m + 1)
                    wait_for(pe, s_post[k], m)
                    pe.nop(nofuse=True)
                    lhs, rhs = zt[k], w_pair[c]
                    if c == 2:
                        for g in range(2):
                            last = nc.tensor.matmul(u_ps[:, g, :], w_pair[2][:, :], zt[k][:, g * BW:(g + 1) * BW],
                                                    start=True, stop=True)
                        last.then_inc(s_u, 1)
                        pe.wait_ge(s_uc, 2 * i + k + 1)
                        pe.nop(nofuse=True)
                        lhs, rhs = u_t[k], w2
                    for t in range(BT):
                        last = nc.tensor.matmul(y_ps[k][:, t * D:(t + 1) * D], lhs[:, t * P:(t + 1) * P], rhs[:, :],
                                                start=True, stop=True)
                    last.then_inc(s_mm[k], 1)

                batches(pe, node_step)

                if c == 2:
                    for n in range(2):
                        pe.wait_ge(s_bnp, n + 1)
                        nc.tensor.matmul(scratch_ps[:, n * P:n * P + D], ones[:, :], part[:, :], start=True,
                                         stop=True).then_inc(s_bnt, 1)

                if c + 1 in TABLE_OF:
                    q = TABLE_OF[c + 1]

                    def table_step(i, k):
                        r = q * BP + i
                        pe.wait_ge(s_xs[k], r + 1)
                        wait_for(pe, s_xtc[1 - k], r + k)
                        pe.nop(nofuse=True)
                        for t in range(BT):
                            last = nc.tensor.transpose(xt_ps[:, t * P:(t + 1) * P], xs[k][:, t * D:(t + 1) * D],
                                                       ident[:, :])
                        last.then_inc(s_xt, 1)
                        pe.wait_ge(s_xtc[k], r + 1)
                        if isinstance(i, int) and (i, k) == (0, 0):
                            pe.wait_ge(s_wtab, 16 * (q + 1))
                        for t in range(BT):
                            for h in range(2):
                                wait_for(pe, s_tabc[h], 2 * (q * NT + 2 * BT * i + k * BT + t))
                                pe.nop(nofuse=True)
                                turned = xt[k][0:D, t * P:(t + 1) * P]
                                if q == 0:
                                    last = nc.tensor.matmul(rel_ps[h], turned, w_table[:, h * 512:(h + 1) * 512],
                                                            start=True, stop=True)
                                else:
                                    for r in KNOT_ROWS[h]:
                                        last = nc.tensor.matmul(knot_ps[r], turned,
                                                                w_table[:, r * K * D:(r + 1) * K * D],
                                                                start=True, stop=True)
                                last.then_inc(s_tab[h], 1)

                    batches(pe, table_step)

        @block.vector
        def _(dve):
            steps = [0]

            def link(ins):
                steps[0] += 1
                ins.then_inc(s_setup, 1)
                dve.wait_ge(s_setup, steps[0])

            published = [0]

            def publish(ins):
                published[0] += 1
                ins.then_inc(s_array, 1)
                dve.wait_ge(s_array, published[0])

            V = nc.vector
            tail = slice(FULLBLK * P, NAT)
            V.memset(nats[0].bitcast(I32)[:, tail], 0).then_inc(s_pads, 1)
            V.memset(nats[1].bitcast(I32)[:, tail], 1 << 20).then_inc(s_pads, 1)
            V.memset(nats[2].bitcast(I32)[:, tail], -1).then_inc(s_pads, 1)
            V.memset(nats[2].bitcast(I32)[:, 0:1], -1).then_inc(s_pads, 1)
            V.memset(nats[3].bitcast(I32)[:, tail], 0).then_inc(s_pads, 1)
            V.memset(arena[:, 4 * NAT + 2 * FULLBLK * P:6 * NAT], 0.0).then_inc(s_pads, 1)

            src_i, dst_i, prev_i, typ_i = (nats[n].bitcast(I32) for n in range(4))
            attr = arena[:, 4 * NAT:6 * NAT].rearrange("p (e a) -> p e a", a=2)
            dve.wait_ge(s_src, 48)
            publish(V.tensor_copy(nats[6], src_i))
            dve.wait_ge(s_nat, 14 * 16)
            link(V.tensor_tensor(nats[7], dst_i, prev_i, ALU.is_equal))
            link(V.tensor_copy(keep_nat[0], nats[7]))
            link(V.tensor_scalar(nats[8], nats[7], 0.5, BIG, ALU.subtract, ALU.mult))
            link(V.tensor_tensor(keep_nat[1], nats[8], nats[8], ALU.add))
            dve.sem_inc(s_marks, 1)
            link(V.tensor_scalar(prev_i, dst_i, 7, None, ALU.logical_shift_right))
            link(V.tensor_copy(nats[7], prev_i))
            publish(V.tensor_copy(nats[2], nats[7]))
            link(V.tensor_scalar(dst_i, dst_i, P - 1, None, ALU.bitwise_and))
            link(V.tensor_copy(nats[8], dst_i))
            publish(V.tensor_copy(nats[1], nats[8]))
            link(V.tensor_copy(nats[9], typ_i))
            publish(V.scalar_tensor_tensor(out=nats[3], in0=nats[6], scalar=float(RELS), in1=nats[9], op0=ALU.mult,
                                           op1=ALU.add))
            cell, off = [None, None], [None, None]
            for d in range(2):
                v, f, g = nats[7], nats[8 + d], nats[10]
                link(V.tensor_scalar(v, attr[:, :, d], float(K - 1), 0.0, ALU.mult, ALU.max))
                link(V.tensor_scalar(v, v, float(K - 1), None, ALU.min))
                link(V.tensor_copy(nats[11].bitcast(I32), v))
                link(V.tensor_copy(f, nats[11].bitcast(I32)))
                link(V.tensor_tensor(g, f, v, ALU.is_gt))
                link(V.tensor_tensor(f, f, g, ALU.subtract))
                link(V.tensor_scalar(f, f, float(K - 2), None, ALU.min))
                o = nats[0] if d == 0 else nats[11]
                link(V.tensor_tensor(o, v, f, ALU.subtract))
                cell[d], off[d] = f, o
            link(V.scalar_tensor_tensor(out=nats[7], in0=cell[1], scalar=float(K - 1), in1=cell[0], op0=ALU.mult,
                                        op1=ALU.add))
            dve.wait_ge(s_flipped, len(CHUNKS))
            publish(V.scalar_tensor_tensor(out=nats[6], in0=nats[6], scalar=float(CELLS), in1=nats[7], op0=ALU.mult,
                                           op1=ALU.add))
            in_a, in_b = nats[4], nats[5]
            link(V.tensor_scalar(in_a, off[0], -1.0, 1.0, ALU.mult, ALU.add))
            link(V.tensor_scalar(in_b, off[1], -1.0, 1.0, ALU.mult, ALU.add))
            for s, (first, second) in enumerate(((in_a, in_b), (off[0], in_b), (in_a, off[1]), (off[0], off[1]))):
                publish(V.tensor_tensor(FLIPS[5 + s][0], first, second, ALU.mult))
            dve.wait_ge(s_consts, 7)
            link(V.tensor_copy(iota_row[:, :], iota_i[:, :]))
            link(V.tensor_copy(node_id[:, :], node_i[:, :]))
            dve.wait_ge(s_weights, 16 * WEIGHT_DMAS)
            link(V.tensor_copy(cut_dst[:, :], cut_dst_i[:, :]))
            for c in range(3, CONVS):
                link(V.tensor_copy(w_pair[c][0:D, :], ident[0:D, 0:D]))
            dve.wait_ge(s_wt, 1)
            for n in range(2):
                last = V.tensor_copy(w_pair[n][:, :], scratch_ps[:, n * D:(n + 1) * D])
            last.then_inc(s_wt_taken, 1)
            dve.wait_ge(s_keep_dram, 64)
            dve.wait_ge(s_flipped, len(CHUNKS) * len(FLIPS))
            V.memset(x3d[:, NT - 1, :], 0.0).then_inc(s_xpad, 1)
            dve.wait_ge(s_wt_taken, 1)

            pre_base, post_base = [0], [0]
            norms = [0]

            def per_node(v):
                return v.rearrange("p (t c) -> p t c", c=D)

            def over_features(v):
                return v.unsqueeze(2).broadcast_to([P, BT, D])

            def over_nodes(v, n=BT):
                return v.unsqueeze(1).broadcast_to([P, n, D])

            def chained(base, per, b):
                done = [0]

                def step(ins):
                    done[0] += 1
                    ins.then_inc(s_post_step if base is post_base else s_pre_step, 1)
                    dve.wait_ge(s_post_step if base is post_base else s_pre_step, base[0] + per * b + done[0])
                    assert done[0] <= per
                return step

            def layer_norm(step, y, res, norm_no):
                step(V.tensor_reduce(ln_s[:, :], per_node(y), AX.X, ALU.add))
                step(V.tensor_scalar(ln_m[:, :], ln_s[:, :], 1.0 / D, None, ALU.mult))
                step(V.tensor_tensor(per_node(ln_c[:, :]), per_node(y), over_features(ln_m[:, :]), ALU.subtract))
                step(V.tensor_tensor(tmp_b[:, :], ln_c[:, :], ln_c[:, :], ALU.mult))
                step(V.tensor_reduce(ln_v[:, :], per_node(tmp_b[:, :]), AX.X, ALU.add))
                V.tensor_scalar(ln_e[:, :], ln_v[:, :], 1.0 / D, EPS, ALU.mult, ALU.add).then_inc(s_var, 1)
                dve.wait_ge(s_std, norm_no + 1)
                step(V.reciprocal(ln_r[:, :], ln_d[:, :]))
                step(V.tensor_tensor(per_node(res), per_node(ln_c[:, :]), over_features(ln_r[:, :]), ALU.mult))

            for c in range(CONVS):
                def hot(i, k):
                    wait_for(dve, s_hist[k], i)
                    g = bass.ds(2 * i + k, 1)
                    for hot_, val, w in ((hi_hot, hi_t, HIS), (lo_hot, lo_t, P)):
                        last = V.tensor_tensor(hot_[k], val[:, g, :].rearrange("p g t -> p (g t)").unsqueeze(2)
                                               .broadcast_to([P, BOX, w]),
                                               iota_row[:, 0:w].unsqueeze(1).broadcast_to([P, BOX, w]), ALU.is_equal)
                    last.then_inc(s_onehot[k], 1)

                def weigh(i, k):
                    n = edge_use(c, i)
                    dve.wait_ge(s_rows_in[c // 3][k], 16 * BOX * (edge_use(c % 3, i) + 1))
                    wait_for(dve, s_turned[k], n)
                    w = basis[:, bass.ds(2 * i + k, 1), :, :].rearrange("p g (h j) s -> p h (g j) s", h=2)
                    rows_ = gathered[k].rearrange("p (j h s c) -> p h j s c", j=GT, h=2, s=CORNERS)
                    dst = weighted[k].rearrange("p (j s h c) -> p h j s c", j=GT, h=2, s=CORNERS)
                    for h in range(2):
                        last = V.tensor_tensor(dst[:, h], rows_[:, h],
                                               w[:, h].unsqueeze(3).broadcast_to([P, GT, CORNERS, D]), ALU.mult)
                    last.then_inc(s_weighted[k], 1)

                def scan(i, k):
                    n = edge_use(c, i)
                    first = isinstance(i, int) and (i, k) == (0, 0)
                    dve.wait_ge(s_turned[k], n + 1)
                    dve.wait_ge(s_keep[k], 32 * (n + 1))
                    wait_for(dve, s_back[k], n)
                    if not first:
                        j, l = before(i, k)
                        dve.wait_ge(s_scanned[l], edge_use(c, j) + 1)
                    init = ((0.0 if MODE[c] == SUM else -BIG) if first
                            else scanned[:, 1 - k, GT * P - 1:GT * P])
                    ops = (ALU.mult, ALU.add) if MODE[c] == SUM else (ALU.min, ALU.max)
                    V.tensor_tensor_scan(scanned[:, k, :], keep[:, k, :], turn_ps[k], init, *ops
                                         ).then_inc(s_scanned[k], 1)

                def edge_step(i, k):
                    if c == 0:
                        hot(i, k)
                    if MODE[c] == MAX:
                        weigh(i, k)
                    if not (isinstance(i, int) and (i, k) == (0, 0)):
                        scan(*before(i, k))

                groups(dve, edge_step)
                scan(GP - 1, 1)

                if c == 0:
                    for k in range(2):
                        dve.wait_ge(s_hist[k], GP)
                    found = [1]

                    def find(ins):
                        found[0] += 1
                        ins.then_inc(s_find, 1)
                        dve.wait_ge(s_find, found[0])

                    V.tensor_copy(cnt[:, :], hist_ps).then_inc(s_find, 1)
                    dve.wait_ge(s_pref, 1)
                    find(V.tensor_copy(tot[:, :], scratch_ps[:, P:P + NT]))
                    find(V.tensor_tensor_scan(cum[:, :], ones[:, 0:NT], tot[:, :], 0.0, ALU.mult, ALU.add))
                    find(V.tensor_tensor(cum[:, :], cum[:, :], tot[:, :], ALU.subtract))
                    find(V.tensor_tensor(cum[:, :], cum[:, :], scratch_ps[:, 0:NT], ALU.add))
                    find(V.tensor_scalar(cum[:, :], cum[:, :], 1.0, 0.0, ALU.subtract, ALU.max))
                    find(V.tensor_copy(end_row[:, :], cum[:, :]))
                    find(V.tensor_scalar(nonempty[:, :], cnt[:, :], 0.0, None, ALU.is_gt))
                    find(V.tensor_scalar(tot[:, :], node_id[:, :], cut_dst[:, 0:1], None, ALU.is_equal))
                    find(V.scalar_tensor_tensor(out=straddle[:, :], in0=node_id[:, :], scalar=cut_dst[:, 1:2],
                                                in1=tot[:, :], op0=ALU.is_equal, op1=ALU.mult))
                    find(V.tensor_scalar(straddle_max[:, :], straddle[:, :], 1.0, BIG, ALU.subtract, ALU.mult))
                    dve.sem_inc(s_found, 1)
                    dve.wait_ge(s_x, 32)

                def fix_aggregate(i, k):
                    m = node_use(c, i)
                    step = chained(pre_base, PRE_STEPS - 1, 2 * i + k)
                    dve.wait_ge(s_agg[k], 16 * BT * (m + 1))
                    if not (isinstance(i, int) and (i, k) == (0, 0)):
                        j, l = before(i, k)
                        dve.wait_ge(s_pre[l], node_use(c, j) + 1)
                    t = cols(i, k, BT)
                    step(V.tensor_tensor(per_node(pre_a[:, :]), per_node(agg[:, k, :]), over_features(nonempty[:, t]),
                                         ALU.mult))
                    at_cut = (straddle if MODE[c] == SUM else straddle_max)[:, t]
                    step(V.tensor_tensor(per_node(pre_b[:, :]), over_nodes(carry[:, :]), over_features(at_cut),
                                         ALU.mult if MODE[c] == SUM else ALU.add))
                    wait_for(dve, s_zt[k], m)
                    V.tensor_tensor(zin[k].rearrange("p (t c) -> p t c", c=P)[:, :, 0:D], per_node(pre_a[:, :]),
                                    per_node(pre_b[:, :]), ALU.add if MODE[c] == SUM else ALU.max
                                    ).then_inc(s_pre[k], 1)

                def finish_batch(i, k):
                    m, b = node_use(c, i), 2 * i + k
                    step = chained(post_base, POST_STEPS[c], b)
                    dve.wait_ge(s_mm[k], m + 1)
                    y, res = y_ps[k], RES_OF[c][:, cols(i, k, BW)]
                    if c == 2:
                        step(V.tensor_tensor(per_node(res), per_node(y), over_nodes(bias[c][:, :]), ALU.add))
                    else:
                        step(V.tensor_tensor(per_node(tmp_a[:, :]), per_node(y), over_nodes(bias[c][:, :]), ALU.add))
                    if c in (0, 4):
                        step(V.tensor_scalar(res, tmp_a[:, :], 0.0, None, ALU.max))
                    if c in NORMED:
                        step(V.tensor_tensor(tmp_a[:, :], tmp_a[:, :], X[:, cols(i, k, BW)], ALU.add))
                        layer_norm(step, tmp_a[:, :], res, NORMED[c] * BATCHES + b)
                    dve.sem_inc(s_post[k], 1)

                def node_step(i, k):
                    fix_aggregate(i, k)
                    if not (isinstance(i, int) and (i, k) == (0, 0)):
                        finish_batch(*before(i, k))

                dve.wait_ge(s_carry, 16 * (c + 1))
                batches(dve, node_step)
                finish_batch(BP - 1, 1)
                pre_base[0] += (PRE_STEPS - 1) * BATCHES
                post_base[0] += POST_STEPS[c] * BATCHES

                if c == 2:
                    last_tile = H[:, (NT - 1) * D:NT * D]
                    by_feature = H[:, :].rearrange("p (t c) -> p c t", c=D)
                    square = arena[:, 0:NT * D]
                    bn = [0]

                    def norm_step(ins, signal=None):
                        bn[0] += 1
                        ins.then_inc(s_bn, 1)
                        dve.wait_ge(s_bn, bn[0])

                    norm_step(V.tensor_scalar(last_tile, last_tile, valid[:, 0:1], None, ALU.mult))
                    V.tensor_reduce(part[:, :], by_feature, AX.X, ALU.add).then_inc(s_bnp, 1)
                    dve.wait_ge(s_bnt, 1)
                    norm_step(V.tensor_scalar(mean[:, :], scratch_ps[:, 0:D], 1.0 / N, None, ALU.mult))
                    norm_step(V.tensor_tensor(per_node(H[:, :]), per_node(H[:, :]), over_nodes(mean[:, :], NT),
                                              ALU.subtract))
                    norm_step(V.tensor_scalar(last_tile, last_tile, valid[:, 0:1], None, ALU.mult))
                    norm_step(V.tensor_tensor(square, H[:, :], H[:, :], ALU.mult))
                    V.tensor_reduce(part[:, :], square.rearrange("p (t c) -> p c t", c=D), AX.X,
                                    ALU.add).then_inc(s_bnp, 1)
                    dve.wait_ge(s_bnt, 2)
                    V.tensor_scalar(rstd[:, :], scratch_ps[:, P:P + D], 1.0 / N, EPS, ALU.mult,
                                    ALU.add).then_inc(s_bnv, 1)
                    dve.wait_ge(s_bns, 1)
                    norm_step(V.reciprocal(rstd[:, :], part[:, :]))
                    norm_step(V.tensor_tensor(mean[:, :], rstd[:, :], gamma[:, :], ALU.mult))

                    def normed_batch(i, k):
                        b = 2 * i + k
                        step = chained(post_base, BN_STEPS, b)
                        step(V.tensor_tensor(per_node(tmp_a[:, :]), per_node(H[:, cols(i, k, BW)]),
                                             over_nodes(mean[:, :]), ALU.mult))
                        step(V.tensor_tensor(per_node(tmp_a[:, :]), per_node(tmp_a[:, :]), over_nodes(beta[:, :]),
                                             ALU.add))
                        step(V.scalar_tensor_tensor(out=tmp_a[:, :], in0=tmp_a[:, :], scalar=0.0,
                                                    in1=X[:, cols(i, k, BW)], op0=ALU.max, op1=ALU.add))
                        layer_norm(step, tmp_a[:, :], X[:, cols(i, k, BW)], NORMED["bn"] * BATCHES + b)
                        dve.sem_inc(s_x2, 1)

                    batches(dve, normed_batch)
                    post_base[0] += BN_STEPS * BATCHES

                if c + 1 in TABLE_OF and TABLE_OF[c + 1] > 0:
                    q = TABLE_OF[c + 1]

                    def table_step(i, k):
                        for t in range(BT):
                            for h in range(2):
                                take_table(dve, V.tensor_copy, ((0, 2), (4,))[h], q, i, k * BT + t, h)

                    batches(dve, table_step)


_INS = ['x', 'src', 'dst', 'edge_attr_2', 'edge_type_16', 'L0_gnn_W_rel1', 'L0_gnn_b_rel1', 'L0_gnn_W_root1',
        'L0_gnn_W_rel2', 'L0_gnn_b_rel2', 'L0_gnn_W_root2', 'L1_gnn_W1', 'L1_gnn_b1', 'L1_gnn_W2', 'L1_gnn_b2',
        'L1_gnn_gamma', 'L1_gnn_beta', 'L2_gnn_weight', 'L2_gnn_h_bias', 'L2_gnn_loop_weight', 'L3_gnn_W1',
        'L3_gnn_root1', 'L3_gnn_bias1', 'L3_gnn_W2', 'L3_gnn_root2', 'L3_gnn_bias2']


def kernel(**inputs):
    import numpy as _np
    import concourse.bacc as _bacc
    from concourse import mybir as _mybir
    from concourse.bass_utils import run_bass_kernel_spmd as _run

    nc = _bacc.Bacc("TRN2", target_bir_lowering=False, num_devices=1)
    arrays, args = {}, {}
    for name in _INS:
        a = _np.ascontiguousarray(inputs[name])
        arrays[f"in_{name}_dram"] = a
        args[name] = nc.dram_tensor(f"in_{name}_dram", a.shape, _mybir.dt.from_np(a.dtype), kind="ExternalInput").ap()
    out = nc.dram_tensor("out_0_dram", inputs["x"].shape, _mybir.dt.float32, kind="ExternalOutput").ap()
    build(nc, args, out)
    r = _run(nc, [arrays], core_ids=[0])
    return r.results[0]["out_0_dram"]
```

```python
from contextlib import ExitStack

import concourse.bass as bass
from concourse import mybir

F32 = mybir.dt.float32
BF16 = mybir.dt.bfloat16
I32 = mybir.dt.int32
U32 = mybir.dt.uint32
ALU = mybir.AluOpType
ACT = mybir.ActivationFunctionType
AX = mybir.AxisListType

P = 128
D = 64
N = 12500
E = 200000
RELS = 16
K = 5
KNOTS = K * K
RUN = K + 2
CORNERS = 4
EPS = 1e-5
BIG = 3.3e38

GT = 4
GROUPS = -(-E // (2 * GT * P))
GROUPS += GROUPS % 2
GP = GROUPS // 2
HALF = GROUPS * GT * P
EP = 2 * HALF
TILES = EP // P
NBLK = -(-TILES // P)
NAT = NBLK * P
FULLBLK = E // (P * P)
RESTROWS = (E - FULLBLK * P * P) // P
RESTCOLS = E % P

NT = -(-N // P)
NP = NT * P
LASTROWS = N - (NT - 1) * P
BT = 7
BATCHES = NT // BT
BP = BATCHES // 2
BW = BT * D
HIS = NT
BOX = GT * 2

CONVS = 6
SUM, MAX = 0, 1
MODE = [SUM, SUM, SUM, SUM, MAX, MAX]
ALONG = (3, 4)
RUN_OF = [1, 1, 1, 1, RUN, RUN]
PRE_STEPS = 3
LN_STEPS = 7
POST_STEPS = [2, 2 + LN_STEPS, 1, 2 + LN_STEPS, 2, 2 + LN_STEPS]
BN_STEPS = 4 + LN_STEPS

RING = 14
KNOT_ROWS = [(0, 1, 2), (3, 4)]
PIECE = len(KNOT_ROWS[0]) * K * D
PIECES_PER_SLOT = 4 * BT // RING
RELW = RELS * D // 2


def wait_for(eng, sem, value):
    if isinstance(value, int) and value <= 0:
        return
    eng.wait_ge(sem, value)


def build(nc, a, out):
    with ExitStack() as ctx:
        def sb(name, shape, dt):
            return ctx.enter_context(nc.sbuf_tensor(name, shape, dt))

        def sem(name):
            return ctx.enter_context(nc.semaphore(name))

        def pair(name):
            return [sem(f"{name}{k}") for k in range(2)]

        def dram(name, shape, dt=F32):
            return nc.dram_tensor(name, shape, dt, kind="Internal").ap()

        rows = dram("scanned_rows", [EP, D])
        h_table = dram("h_table", [NP, D])
        x1_table = dram("x1_table", [NP, D])
        rel_table = dram("rel_table", [NP * RELS, D])
        knot_table = dram("knot_table", [NP * KNOTS, D])
        keep_sum = dram("keep_sum", [EP], BF16)
        keep_max = dram("keep_max", [EP], BF16)

        idx = [sb(f"idx{n}", [P, GROUPS, 2, GT], I32) for n in range(3)]
        basis = sb("basis", [P, GROUPS, BOX, CORNERS], F32)
        X = sb("X", [P, NT * D], F32)
        H = sb("H", [P, NT * D], F32)
        hi_t, lo_t = (H[:, NT * D - (n + 1) * TILES // 2:NT * D - n * TILES // 2].bitcast(BF16)
                      .rearrange("p (g t) -> p g t", t=BOX) for n in range(2))
        ident = sb("ident", [P, P], F32)
        ones = sb("ones", [P, P], F32)
        upto = sb("upto", [P, P], F32)
        iota_row = sb("iota_row", [P, P], BF16)
        node_id = sb("node_id", [P, NT], F32)
        valid = sb("valid", [P, 1], F32)
        cut_dst_i = sb("cut_dst_i", [P, 2], I32)
        cut_dst = sb("cut_dst", [P, 2], F32)
        cnt = sb("cnt", [P, NT], F32)
        tot = sb("tot", [P, NT], F32)
        cum = sb("cum", [P, NT], F32)
        end_row = sb("end_row", [P, NT], I32)
        nonempty = sb("nonempty", [P, NT], F32)
        straddle = sb("straddle", [P, NT], F32)
        straddle_max = sb("straddle_max", [P, NT], F32)
        carry = sb("carry", [P, D], F32)
        w_pair = [sb(f"w_pair{c}", [P, D], F32) for c in range(CONVS)]
        w2 = sb("w2", [D, D], F32)
        bias_in = ["L0_gnn_b_rel1", "L0_gnn_b_rel2", "L1_gnn_b2", "L2_gnn_h_bias", "L3_gnn_bias1", "L3_gnn_bias2"]
        bias = [sb(f"bias{c}", [P, D], F32) for c in range(CONVS)]
        cols_in = ["L1_gnn_b1", "L1_gnn_b2", "L1_gnn_gamma"]
        b1_col, b2_col, gamma_col = (sb(f"col{n}", [D, 1], F32) for n in range(3))
        beta = sb("beta", [P, D], F32)
        w_parts = sb("w_parts", [P, 3, K * K * D], BF16)
        ident_h = sb("ident_h", [P, P], BF16)
        bn_part = sb("bn_part", [D, 2 * BATCHES, 6], F32)
        bn_all = sb("bn_all", [D, 2], F32)
        bn_col = sb("bn_col", [D, 4], F32)
        bn_row = sb("bn_row", [P, 2, D], F32)
        scanned = sb("scanned", [P, 2, GT * P], F32)
        turned_rows = sb("turned_rows", [P, 2, 2, GT * D], F32)
        keep = sb("keep", [P, 2, GT * P], BF16)
        idx_now = sb("idx_now", [P, 2, 2, GT], I32)
        end_now = sb("end_now", [P, 2, BT], I32)
        plain_rows = sb("plain_rows", [P, 2, BOX * D], F32)
        agg = plain_rows[:, :, 0:BW]
        tmp_a = sb("tmp_a", [P, BW], F32)
        tmp_b = sb("tmp_b", [P, BW], F32)
        pre_a, pre_b = tmp_a, tmp_b
        ln_c = sb("ln_c", [P, BW], F32)
        bn_wide = ln_c[0:D, 0:2 * P].rearrange("p (n c) -> p n c", n=2)
        rest = ln_c
        iota_i = tmp_a[:, 0:P].bitcast(I32)
        node_i = tmp_a[:, P:P + NT].bitcast(I32)
        w_raw = ln_c[0:D, 0:4 * D].rearrange("p (n a c) -> p n a c", n=2, a=2)
        ln_s = sb("ln_s", [P, BT], F32)
        ln_m = sb("ln_m", [P, BT], F32)
        ln_v = sb("ln_v", [P, BT], F32)
        ln_e = sb("ln_e", [P, BT], F32)
        ln_d = sb("ln_d", [P, BT], F32)
        ln_r = sb("ln_r", [P, BT], F32)

        arena = sb("arena", [P, RING * PIECE + 4 * BW + 4 * BT * P], F32)
        at = [0]

        def carve(n):
            v = arena[:, at[0]:at[0] + n]
            at[0] += n
            return v

        gathered = [carve(BOX * RUN * D) for _ in range(2)]
        weighted = [carve(BOX * CORNERS * D) for _ in range(2)]
        at = [0]
        ring = [carve(PIECE) for _ in range(RING)]
        x_parts = [carve(2 * BW).bitcast(BF16).rearrange("p (t s c) -> p t s c", s=4, c=D) for _ in range(2)]
        zin = [carve(BT * P) for _ in range(2)]
        zt = [carve(BT * P) for _ in range(2)]
        onehot = [w.bitcast(BF16) for w in weighted]
        hi_hot = [o[:, 0:BOX * HIS].rearrange("p (t v) -> p t v", v=HIS) for o in onehot]
        lo_hot = [o[:, BOX * HIS:BOX * (HIS + P)].rearrange("p (t v) -> p t v", v=P) for o in onehot]
        nats = [arena[:, n * NAT:(n + 1) * NAT] for n in range(9)] + [H[:, n * NAT:(n + 1) * NAT] for n in range(2)]
        nats += [X[:, n * NAT:(n + 1) * NAT] for n in (1, 2)]
        keep_nat = [X[:, n * NAT // 2:(n + 1) * NAT // 2].bitcast(BF16) for n in range(2)]
        xt = [v[:, 0:2 * BW].bitcast(BF16).rearrange("p (t s c) -> p t s c", s=2, c=P) for v in
              (scanned.rearrange("p a b -> p (a b)"), turned_rows.rearrange("p a b c -> p (a b c)"))]
        u_t = [w[0:D, 0:BT * P] for w in weighted]

        PS = ctx.enter_context(nc.psum_tensor("PS", [P, 8, 512], F32))
        turn_ps = [PS[:, k, :] for k in range(2)]
        back_ps = [PS[:, 2 + k, :] for k in range(2)]
        hist_ps = PS[:, 4, 0:HIS]
        flip_ps = [PS[:, 5 + k, :] for k in range(2)]
        scratch_ps = PS[:, 7, :]
        zt_ps = [PS[:, 2 * k:2 * k + 2, :].rearrange("p a b -> p (a b)")[:, 0:BT * P] for k in range(2)]
        y_ps = [PS[:, 4 + k, 0:BW] for k in range(2)]
        zt_ps_of = [[zt_ps[0], zt_ps[0]] if c in ALONG else zt_ps for c in range(CONVS)]
        y_ps_of = [[PS[:, 7, 0:BW]] * 2 if c in ALONG else y_ps for c in range(CONVS)]
        u_ps = PS[0:D, 6:8, 0:BW]
        xt_ps = PS[:, 0:2, :].rearrange("p a b -> p (a b)")[:, 0:2 * BW].bitcast(BF16).rearrange(
            "p (t s c) -> p t s c", s=2, c=P)
        rel_ps = [PS[:, 2 + h, :] for h in range(2)]
        knot_ps = [PS[:, 2 + r, 0:K * D] for r in range(K)]
        part_ps = [[rel_ps[h].unsqueeze(1), PS[:, 2 + KNOT_ROWS[h][0]:3 + KNOT_ROWS[h][-1], 0:K * D]] for h in range(2)]

        s_pads = sem("pads_set")
        s_src = sem("src_in")
        s_nat = sem("edge_arrays_in")
        s_consts = sem("constants")
        s_weights = sem("weights_in")
        s_x = sem("x_in")
        s_xpad = sem("x_pad")
        s_setup = sem("setup_steps")
        s_marks = sem("segment_marks")
        s_array = sem("edge_values_ready")
        s_flip = sem("flipped")
        s_flipped = sem("flip_taken")
        s_keep_dram = sem("keep_in_dram")
        s_wt = sem("weights_turned")
        s_wt_taken = sem("turned_weights_taken")
        s_idx = pair("idx_staged")
        s_rows_in = [pair("rows_gathered_a"), pair("rows_gathered_b")]
        s_weighted = pair("rows_weighted")
        s_turned = pair("rows_turned")
        s_keep = pair("keep_in")
        s_scanned = pair("scanned")
        s_back = pair("turned_back")
        s_taken = pair("back_taken")
        s_stored = pair("rows_stored")
        s_onehot = pair("onehots")
        s_hist = pair("counted")
        s_find = sem("last_edges_steps")
        s_pref = sem("prefix_sums")
        s_found = sem("last_edges_found")
        s_carry = sem("carry_in")
        s_end = pair("end_rows_staged")
        s_agg = pair("aggregates_in")
        s_pre_step = sem("pre_steps")
        s_pre = pair("aggregate_fixed")
        s_zx = pair("node_part")
        s_zt = pair("batch_turned")
        s_ztc = pair("turned_batch_taken")
        s_u = sem("hidden")
        s_uc = sem("hidden_taken")
        s_mm = pair("products")
        s_post_step = sem("post_steps")
        s_var = sem("variance")
        s_std = sem("deviation")
        s_post = pair("batch_done")
        s_out = sem("batches_stored")
        s_bn = sem("batch_norm_steps")
        s_bst = sem("batch_statistics")
        s_x2 = sem("normed_batches")
        s_wtab = sem("table_weights_in")
        s_wsplit_step = sem("weight_split_steps")
        s_wsplit = sem("weights_split")
        s_split_step = sem("split_steps")
        s_xs = sem("batch_split")
        s_xt = sem("table_batch_turned")
        s_bnt = sem("batch_norm_totals")
        s_bnv = sem("batch_norm_variance")
        s_bns = sem("batch_norm_deviation")
        s_bnw = sem("batch_norm_columns")
        s_xtc = pair("table_batch_taken")
        s_tab = pair("table_half")
        s_tabc = pair("table_half_taken")
        s_tabd = [sem(f"table_stored{v}") for v in range(RING)]
        block = ctx.enter_context(nc.Block())

        rows_w = rows.rearrange("(h g p j) c -> p h g (j c)", h=2, g=GROUPS, p=P)
        keeps = [k.rearrange("(h g c) -> h g c", h=2, g=GROUPS) for k in (keep_sum, keep_max)]
        knot_v = knot_table.rearrange("(t p r) c -> t p (r c)", p=P, r=KNOTS)
        rel_v = rel_table.rearrange("(t p r) c -> t p (r c)", p=P, r=RELS)
        h_v = h_table.rearrange("(t p) c -> p t c", p=P)
        x1_v = x1_table.rearrange("(t p) c -> p t c", p=P)
        tables = [a["x"], h_table, x1_table, rel_table, knot_table, knot_table]
        idx_of = [idx[0], idx[0], idx[0], idx[1], idx[2], idx[2]]
        x3d = X[:, :].rearrange("p (t c) -> p t c", c=D)
        TABLE_OF = {3: 0, 4: 1, 5: 2}
        TABLE_COLS = [RELS * D, KNOTS * D, KNOTS * D]
        NORMED = {1: 0, "bn": 1, 3: 2, 5: 3}
        PARTS = [[(0, RELW), (RELW, RELW)]] + 2 * [[(rows_[0] * K * D, len(rows_) * K * D) for rows_ in KNOT_ROWS]]
        SRC_OF = [X, X, H]
        NODE_OF = [X, H, X, X, X, H]
        RES_OF = [H, X, H, X, H, X]

        def edge_use(c, i):
            return c * GP + i

        def max_use(c, i):
            return (c - MODE.index(MAX)) * GP + i

        def node_use(c, i):
            return c * BP + i

        def pairs(eng, body, c, n):
            start = 1 if c else 2
            for i in range(start):
                for k in range(2):
                    body(i, k)
            with eng.Fori(start, n - 1) as i:
                for k in range(2):
                    body(i, k)
            for k in range(2):
                body(n - 1, k)

        def before(i, k):
            return (i, 0) if k == 1 else (i - 1, 1)

        def cols(i, k, width):
            return bass.ds((2 * i + k) * width, width)

        WEIGHT_DMAS = 2 + 4 + 3 + 3 + CONVS + 1 + 3

        def by_tile(dst):
            return dst.rearrange("p g (h j) -> p g h j", h=2)

        FLIPS = [(nats[6], idx[0]), (nats[2], by_tile(hi_t)), (nats[1], by_tile(lo_t)), (nats[3], idx[1]), (nats[6], idx[2])]
        FLIPS += [(nats[n], by_tile(basis[:, :, :, s])) for s, n in enumerate((7, 8, 9, 10))]
        CHUNKS = [(b, min(4, NBLK - b)) for b in range(0, NBLK, 4)]

        def slot_free(eng, q, i, v):
            wait_for(eng, s_tabd[v % RING], 16 * (PIECES_PER_SLOT * (q * BP + i) + v // RING))

        @block.gpsimd
        def _(pool):
            pool.iota(iota_i[:, :], [[1, P]], base=0, channel_multiplier=0).then_inc(s_consts, 1)
            pool.iota(node_i[:, :], [[P, NT]], base=0, channel_multiplier=1).then_inc(s_consts, 1)
            pool.memset(ident[:, :], 0.0).then_inc(s_consts, 1)
            pool.memset(ones[:, :], 1.0).then_inc(s_consts, 1)
            pool.wait_ge(s_consts, 4)
            pool.affine_select(out=ident[:, :], in_=ident[:, :], compare_op=ALU.not_equal, fill=1.0, base=0,
                               pattern=[[-1, P]], channel_multiplier=1).then_inc(s_consts, 1)
            pool.affine_select(out=upto[:, :], in_=ones[:, :], compare_op=ALU.is_ge, fill=0.0, base=0,
                               pattern=[[1, P]], channel_multiplier=-1).then_inc(s_consts, 1)
            pool.affine_select(out=valid[:, :], in_=ones[:, 0:1], compare_op=ALU.is_ge, fill=0.0, base=LASTROWS - 1,
                               pattern=[[0, 1]], channel_multiplier=-1).then_inc(s_consts, 1)

            for c in range(CONVS):
                width = RUN_OF[c] * D
                if c in (1, 2):
                    pool.wait_ge(s_out, 16 * BATCHES * c)
                if c in TABLE_OF:
                    n = TABLE_OF[c]
                    for v in range(RING):
                        pool.wait_ge(s_tabd[v], 16 * PIECES_PER_SLOT * BP * (n + 1))

                def gather_group(i, k):
                    n = edge_use(c, i)
                    pool.wait_ge(s_idx[k], n + 1)
                    if MODE[c] == SUM:
                        wait_for(pool, s_turned[k], n)
                    else:
                        wait_for(pool, s_weighted[k], max_use(c, i))
                    pool.nop(nofuse=True)
                    for j in range(GT):
                        for h in range(2):
                            t = 2 * j + h
                            into = plain_rows[:, k, :] if MODE[c] == SUM else gathered[k]
                            pool.indirect_dma_start(
                                into[:, t * width:(t + 1) * width], None, tables[c],
                                bass.IndirectOffsetOnAxis(ap=idx_now[:, k, h, j:j + 1].bitcast(U32), axis=0),
                            ).then_inc(s_rows_in[c // 3][k], 16)

                pairs(pool, gather_group, c, GP)
                for k in range(2):
                    pool.wait_ge(s_stored[k], 16 * GP * (c + 1))

                def gather_batch(i, k):
                    m = node_use(c, i)
                    pool.wait_ge(s_end[k], m + 1)
                    wait_for(pool, s_pre[k], m)
                    pool.nop(nofuse=True)
                    for t in range(BT):
                        pool.indirect_dma_start(
                            agg[:, k, t * D:(t + 1) * D], None, rows,
                            bass.IndirectOffsetOnAxis(ap=end_now[:, k, t:t + 1].bitcast(U32), axis=0),
                        ).then_inc(s_agg[k], 16)

                pairs(pool, gather_batch, c, BP)

        @block.sync
        def _(sp):
            sp.wait_ge(s_pads, 6)
            def load_edges(tile_, src, w, arrived):
                v = tile_.rearrange("p (b c) -> p b c", b=NBLK)
                n = FULLBLK * P * P
                full = src[0:n * w].rearrange("(b r c) -> r b c", r=P, c=P * w)
                sp.dma_start(v[:, 0:FULLBLK, :], full).then_inc(arrived, 16)
                sp.dma_start(v[0:RESTROWS, FULLBLK, :],
                             src[n * w:(n + RESTROWS * P) * w].rearrange("(r c) -> r c", c=P * w)).then_inc(arrived, 16)
                sp.dma_start(v[RESTROWS:RESTROWS + 1, FULLBLK, 0:RESTCOLS * w],
                             src[(n + RESTROWS * P) * w:E * w].rearrange("(r c) -> r c", r=1)).then_inc(arrived, 16)
            load_edges(nats[0].bitcast(I32), a["src"], 1, s_src)
            load_edges(nats[1].bitcast(I32), a["dst"], 1, s_nat)
            v = nats[2].bitcast(I32).rearrange("p (b c) -> p b c", b=NBLK)
            sp.dma_start(v[0:1, 0, 1:P], a["dst"][0:P - 1].rearrange("(r c) -> r c", r=1)).then_inc(s_nat, 16)
            sp.dma_start(v[1:P, 0, :], a["dst"][P - 1:P * P - 1].rearrange("(r c) -> r c", c=P)).then_inc(s_nat, 16)
            sp.dma_start(v[:, 1:FULLBLK, :], a["dst"][P * P - 1:FULLBLK * P * P - 1].rearrange(
                "(b r c) -> r b c", r=P, c=P)).then_inc(s_nat, 16)
            sp.dma_start(v[0:RESTROWS, FULLBLK, :],
                         a["dst"][FULLBLK * P * P - 1:(FULLBLK * P + RESTROWS) * P - 1].rearrange(
                             "(r c) -> r c", c=P)).then_inc(s_nat, 16)
            sp.dma_start(v[RESTROWS:RESTROWS + 1, FULLBLK, 0:RESTCOLS],
                         a["dst"][(FULLBLK * P + RESTROWS) * P - 1:E - 1].rearrange("(r c) -> r c", r=1)).then_inc(s_nat, 16)
            load_edges(nats[3].bitcast(I32), a["edge_type_16"], 1, s_nat)
            load_edges(arena[:, 4 * NAT:6 * NAT], a["edge_attr_2"].rearrange("e c -> (e c)"), 2, s_nat)
            for h in range(2):
                sp.dma_start(cut_dst_i[:, h:h + 1], a["dst"][HALF - 1 + h:HALF + h].rearrange("(r c) -> r c", r=1)
                             .broadcast_to([P, 1])).then_inc(s_weights, 16)
            for n in range(2):
                sp.dma_start(w_raw[:, n, 0, :], a[f"L0_gnn_W_rel{n + 1}"]).then_inc(s_weights, 16)
                sp.dma_start(w_raw[:, n, 1, :], a[f"L0_gnn_W_root{n + 1}"]).then_inc(s_weights, 16)
            sp.dma_start(w_pair[2][0:D, :], a["L1_gnn_W1"]).then_inc(s_weights, 16)
            sp.dma_start(w_pair[2][D:P, :], a["L1_gnn_W1"]).then_inc(s_weights, 16)
            sp.dma_start(w2[:, :], a["L1_gnn_W2"]).then_inc(s_weights, 16)
            for c, name in ((3, "L2_gnn_loop_weight"), (4, "L3_gnn_root1"), (5, "L3_gnn_root2")):
                sp.dma_start(w_pair[c][D:P, :], a[name]).then_inc(s_weights, 16)
            for c in range(CONVS):
                sp.dma_start(bias[c][:, :], a[bias_in[c]].rearrange("(r c) -> r c", r=1)
                             .broadcast_to([P, D])).then_inc(s_weights, 16)
            sp.dma_start(beta[:, :], a["L1_gnn_beta"].rearrange("(r c) -> r c", r=1)
                         .broadcast_to([P, D])).then_inc(s_weights, 16)
            for col, name in zip((b1_col, b2_col, gamma_col), cols_in):
                sp.dma_start(col[:, :], a[name].rearrange("(r c) -> r c", c=1)).then_inc(s_weights, 16)
            sp.wait_ge(s_marks, 1)
            for n in range(2):
                blocks = TILES // P
                v = keep_nat[n].rearrange("p (b c) -> p b c", b=NBLK)
                dst = (keep_sum, keep_max)[n]
                sp.dma_start(dst[0:blocks * P * P].rearrange("(b r c) -> r b c", r=P, c=P),
                             v[:, 0:blocks, :]).then_inc(s_keep_dram, 16)
                sp.dma_start(dst[blocks * P * P:EP].rearrange("(r c) -> r c", c=P),
                             v[0:TILES - blocks * P, blocks, :]).then_inc(s_keep_dram, 16)
            sp.wait_ge(s_keep_dram, 64)
            def table_weights(c):
                n = TABLE_OF[c]
                w = a["L2_gnn_weight"] if n == 0 else a[f"L3_gnn_W{n}"]
                if n == 1:
                    sp.wait_ge(s_x2, BATCHES)
                for half in range(2):
                    sp.dma_start(H[half * D:(half + 1) * D, 0:TABLE_COLS[n]].rearrange("i (r o) -> i r o", o=D),
                                 w.rearrange("r i o -> i r o")).then_inc(s_wtab, 16)

            for c in range(CONVS):
                marks = keeps[MODE[c]]

                def load_keep(i, k):
                    n = edge_use(c, i)
                    wait_for(sp, s_scanned[k], n)
                    for h in range(2):
                        src = marks[h:h + 1, bass.ds(2 * i + k, 1), :].rearrange("a b c -> (a b) c")
                        sp.dma_start(keep[h * D:(h + 1) * D, k, :], src.broadcast_to([D, GT * P])).then_inc(s_keep[k], 16)

                def store_rows(i, k):
                    n = edge_use(c, i)
                    sp.wait_ge(s_taken[k], n + 1)
                    sp.dma_start(rows_w[:, :, bass.ds(2 * i + k, 1), :].rearrange("p h g c -> p h (g c)"),
                                 turned_rows[:, k, :, :]).then_inc(s_stored[k], 16)

                if c + 1 in TABLE_OF:
                    table_weights(c + 1)
                for k in range(2):
                    load_keep(0, k)
                with sp.Fori(1, GP) as i:
                    for k in range(2):
                        store_rows(i - 1, k)
                        load_keep(i, k)
                for k in range(2):
                    store_rows(GP - 1, k)
                for k in range(2):
                    sp.wait_ge(s_stored[k], 16 * GP * (c + 1))
                sp.dma_start(carry[:, :], rows[HALF - 1:HALF, :].broadcast_to([P, D])).then_inc(s_carry, 16)
                if c in (0, 1, 5):
                    res = RES_OF[c][:, :].rearrange("p (t c) -> p t c", c=D)
                    def store_batch(i, k):
                        m = node_use(c, i)
                        sp.wait_ge(s_post[k], m + 1)
                        t = bass.ds((2 * i + k) * BT, BT)
                        dst = h_v if c == 0 else x1_v
                        if c < 5:
                            sp.dma_start(dst[:, t, :], res[:, t, :]).then_inc(s_out, 16)
                        elif isinstance(i, int) and (i, k) == (BP - 1, 1):
                            t0 = NT - BT
                            sp.dma_start(out[t0 * P:(NT - 1) * P, :].rearrange("(t p) c -> p t c", p=P),
                                         res[:, t0:NT - 1, :]).then_inc(s_out, 16)
                            sp.dma_start(out[(NT - 1) * P:N, :], res[0:LASTROWS, NT - 1, :]).then_inc(s_out, 16)
                        else:
                            sp.dma_start(out[bass.ds((2 * i + k) * BT * P, BT * P), :].rearrange("(t p) c -> p t c", p=P),
                                         res[:, t, :]).then_inc(s_out, 16)
                    pairs(sp, store_batch, c, BP)
                if c + 1 in TABLE_OF:
                    q = TABLE_OF[c + 1]

                    def store_table(i, u):
                        for h in range(2):
                            sp.wait_ge(s_tabc[h], q * NT + 2 * BT * i + u + 1)
                            piece, done = ring[(2 * u + h) % RING], s_tabd[(2 * u + h) % RING]
                            t = bass.ds(2 * BT * i + u, 1)
                            at_, w = PARTS[q][h]
                            dst = (rel_v if q == 0 else knot_v)[t].rearrange("t p c -> (t p) c")
                            sp.dma_start(dst[:, at_:at_ + w], piece[:, 0:w]).then_inc(done, 16)

                    with sp.Fori(0, BP) as i:
                        for u in range(2 * BT):
                            store_table(i, u)
            sp.wait_ge(s_out, 16 * (3 * BATCHES + 1))

        @block.scalar
        def _(act):
            def take_flips(n):
                for q, (b, nb) in enumerate(CHUNKS):
                    f = n * len(CHUNKS) + q
                    act.wait_ge(s_flip, f + 1)
                    done = []
                    for h in range(2):
                        t0, t1 = max(b * P, h * TILES // 2), min((b + nb) * P, (h + 1) * TILES // 2)
                        if t0 < t1:
                            g0, g1 = (t0 - h * TILES // 2) // GT, (t1 - h * TILES // 2) // GT
                            done.append(nc.scalar.copy(
                                FLIPS[n][1][:, g0:g1, h, :],
                                flip_ps[f % 2][:, t0 - b * P:t1 - b * P].rearrange("p (g j) -> p g j", j=GT)))
                    done[-1].then_inc(s_flipped, 1)

            def stage_rows(c, i, k):
                if c == 3 and isinstance(i, int) and i == 0:
                    act.wait_ge(s_rows_in[0][k], 16 * BOX * edge_use(3, 0))
                else:
                    wait_for(act, s_rows_in[c // 3][k], 16 * BOX * edge_use(c % 3, i))
                act.nop(nofuse=True)
                nc.scalar.copy(idx_now[:, k, :, :],
                               idx_of[c][:, bass.ds(2 * i + k, 1), :, :].rearrange("p g h j -> p (g h) j")
                               ).then_inc(s_idx[k], 1)

            take_flips(0)
            act.wait_ge(s_flipped, len(CHUNKS))
            for k in range(2):
                stage_rows(0, 0, k)
            for n in range(1, len(FLIPS)):
                take_flips(n)
            act.wait_ge(s_xpad, 1)
            act.dma_start(x3d[:, 0:NT - 1, :], a["x"][0:(NT - 1) * P, :].rearrange("(t p) c -> p t c", p=P)).then_inc(s_x, 16)
            act.dma_start(x3d[0:LASTROWS, NT - 1, :], a["x"][(NT - 1) * P:N, :]).then_inc(s_x, 16)

            for c in range(CONVS):
                def take_back(i, k):
                    n = edge_use(c, i)
                    act.wait_ge(s_back[k], n + 1)
                    wait_for(act, s_stored[k], 16 * n)
                    nc.scalar.copy(turned_rows[:, k, :, :].rearrange("p h (j c) -> p j h c", j=GT),
                                   back_ps[k].rearrange("p (j h c) -> p j h c", j=GT, h=2)).then_inc(s_taken[k], 1)

                def edge_step(i, k):
                    if not (isinstance(i, int) and i == GP - 1):
                        stage_rows(c, i + 1, k)
                    if not (isinstance(i, int) and (i, k) == (0, 0)):
                        take_back(*before(i, k))

                if c > 0:
                    for k in range(2):
                        stage_rows(c, 0, k)
                pairs(act, edge_step, c, GP)
                take_back(GP - 1, 1)

                def stage_ends(i, k):
                    m = node_use(c, i)
                    wait_for(act, s_agg[k], 16 * BT * m)
                    act.nop(nofuse=True)
                    nc.scalar.copy(end_now[:, k, :], end_row[:, cols(i, k, BT)]).then_inc(s_end[k], 1)

                def deviation():
                    nc.scalar.activation(ln_d[:, :], ln_e[:, :], ACT.Sqrt).then_inc(s_std, 1)

                def norm_count(c_, i, k):
                    return c_ * BATCHES + 2 * i + k

                q = TABLE_OF.get(c + 1)

                def table_step(i, k):
                    r = q * BP + i
                    act.wait_ge(s_xt, 2 * r + k + 1)
                    nc.scalar.copy(xt[k], xt_ps).then_inc(s_xtc[k], 1)
                    normed = "bn" if q == 0 else c
                    for t in range(BT):
                        if t == 3 and normed in NORMED and not (isinstance(i, int) and (i, k) == (BP - 1, 1)):
                            act.wait_ge(s_var, norm_count(NORMED[normed], i, k) + 2)
                            deviation()
                        for h in range(2):
                            u = k * BT + t
                            act.wait_ge(s_tab[h], q * NT + 2 * BT * i + u + 1)
                            slot_free(act, q, i, 2 * u + h)
                            v, w = part_ps[h][min(q, 1)], PARTS[q][h][1]
                            nc.scalar.copy(ring[(2 * u + h) % RING][:, 0:w].rearrange("p (r c) -> p r c", r=v.shape[1]),
                                           v).then_inc(s_tabc[h], 1)

                def node_step(i, k):
                    m = node_use(c, i)
                    wait_for(act, s_zt[k], m)
                    act.nop(nofuse=True)
                    nc.scalar.copy(zin[k].rearrange("p (t c) -> p t c", c=P)[:, :, D:P],
                                   NODE_OF[c][:, cols(i, k, BW)].rearrange("p (t c) -> p t c", c=D)).then_inc(s_zx[k], 1)
                    if not (isinstance(i, int) and i == BP - 1):
                        stage_ends(i + 1, k)
                    act.wait_ge(s_zt[k], m + 1)
                    wait_for(act, s_mm[k], m)
                    nc.scalar.copy(zt[k], zt_ps_of[c][k]).then_inc(s_ztc[k], 1)
                    if c == 2:
                        b = 2 * i + k
                        act.wait_ge(s_u, b + 1)
                        nc.scalar.activation(u_t[k].rearrange("p (a b) -> p a b", a=2), u_ps, ACT.Relu,
                                             bias=b1_col[:, 0:1]).then_inc(s_uc, 1)
                    if c in NORMED and (isinstance(i, int) and (i, k) == (0, 1) if c in ALONG
                                        else not (isinstance(i, int) and (i, k) == (0, 0))):
                        act.wait_ge(s_var, norm_count(NORMED[c], *before(i, k)) + 1)
                        deviation()
                    if c in ALONG and not (isinstance(i, int) and (i, k) == (0, 0)):
                        table_step(*before(i, k))

                if c == 0:
                    act.wait_ge(s_found, 1)
                    act.wait_ge(s_x, 32)
                for k in range(2):
                    stage_ends(0, k)
                pairs(act, node_step, c, BP)
                if c in NORMED and c not in ALONG:
                    act.wait_ge(s_var, norm_count(NORMED[c], BP - 1, 1) + 1)
                    deviation()
                if c in ALONG:
                    table_step(BP - 1, 1)
                if c == 2:
                    act.wait_ge(s_bnv, 1)
                    nc.scalar.activation(bn_col[:, 1:2], bn_col[:, 0:1], ACT.Sqrt).then_inc(s_bns, 1)
                    act.wait_ge(s_var, norm_count(NORMED["bn"], 0, 0) + 1)
                    deviation()
                    pairs(act, table_step, c, BP)

        @block.tensor
        def _(pe):
            pe.wait_ge(s_consts, 7)
            for n in range(len(FLIPS)):
                pe.wait_ge(s_array, n + 1)
                for q, (b, nb) in enumerate(CHUNKS):
                    f = n * len(CHUNKS) + q
                    if f >= 2:
                        pe.wait_ge(s_flipped, f - 1)
                    for j in range(nb):
                        last = nc.tensor.transpose(flip_ps[f % 2][:, j * P:(j + 1) * P],
                                                   FLIPS[n][0][:, (b + j) * P:(b + j + 1) * P], ident[:, :])
                    last.then_inc(s_flip, 1)
            pe.wait_ge(s_weights, 16 * WEIGHT_DMAS)
            for n in range(2):
                last = nc.tensor.transpose(scratch_ps[:, n * D:(n + 1) * D],
                                           w_raw[:, n, :, :].rearrange("o a i -> o (a i)"), ident[0:D, 0:D])
            last.then_inc(s_wt, 1)

            for c in range(CONVS):
                def turn(i, k):
                    n = edge_use(c, i)
                    if MODE[c] == SUM:
                        pe.wait_ge(s_rows_in[c // 3][k], 16 * BOX * (edge_use(c % 3, i) + 1))
                    else:
                        pe.wait_ge(s_weighted[k], max_use(c, i) + 1)
                    wait_for(pe, s_scanned[k], n)
                    pe.nop(nofuse=True)
                    if MODE[c] == SUM:
                        v = plain_rows[:, k, :].rearrange("p (j q) -> p j q", j=GT)
                        for j in range(GT):
                            last = nc.tensor.transpose(turn_ps[k][:, j * P:(j + 1) * P], v[:, j, :], ident[:, :])
                        last.then_inc(s_turned[k], 1)
                    else:
                        v = weighted[k].rearrange("p (j s q) -> p j s q", j=GT, s=CORNERS)
                        for j in range(GT):
                            for s in range(CORNERS):
                                last = nc.tensor.matmul(turn_ps[k][:, j * P:(j + 1) * P], v[:, j, s, :],
                                                        ident[:, :], start=(s == 0), stop=(s == CORNERS - 1))
                        last.then_inc(s_turned[k], 1)

                def count(i, k):
                    pe.wait_ge(s_onehot[k], i + 1)
                    first, end = isinstance(i, int) and (i, k) == (0, 0), isinstance(i, int) and (i, k) == (GP - 1, 1)
                    for t in range(BOX):
                        last = nc.tensor.matmul(hist_ps, lo_hot[k][:, t, :], hi_hot[k][:, t, :],
                                                start=first and t == 0, stop=end and t == BOX - 1,
                                                skip_group_check=True)
                    last.then_inc(s_hist[k], 1)

                def turn_back(i, k):
                    n = edge_use(c, i)
                    pe.wait_ge(s_scanned[k], n + 1)
                    wait_for(pe, s_taken[k], n)
                    pe.nop(nofuse=True)
                    v = scanned[:, k, :].rearrange("q (p j) -> q j p", j=GT)
                    for j in range(GT):
                        last = nc.tensor.transpose(back_ps[k][:, j * P:(j + 1) * P], v[:, j, :], ident[:, :])
                    last.then_inc(s_back[k], 1)

                def edge_step(i, k):
                    turn(i, k)
                    if c == 0:
                        count(i, k)
                    if not (isinstance(i, int) and (i, k) == (0, 0)):
                        turn_back(*before(i, k))

                pairs(pe, edge_step, c, GP)
                turn_back(GP - 1, 1)

                if c == 0:
                    pe.wait_ge(s_wt_taken, 1)
                    pe.wait_ge(s_find, 1)
                    nc.tensor.matmul(scratch_ps[:, 0:NT], upto[:, :], cnt[:, :], start=True, stop=True)
                    nc.tensor.matmul(scratch_ps[:, P:P + NT], ones[:, :], cnt[:, :], start=True,
                                     stop=True).then_inc(s_pref, 1)

                q = TABLE_OF.get(c + 1)

                def table_step(i, k):
                    r = q * BP + i
                    pe.wait_ge(s_xs, 2 * r + k + 1)
                    wait_for(pe, s_xtc[1 - k], r + k)
                    pe.nop(nofuse=True)
                    for t in range(BT):
                        for s in range(2):
                            last = nc.tensor.transpose(xt_ps[:, t, s, :], x_parts[k][:, t, 2 * s:2 * s + 2, :]
                                                       .rearrange("p s c -> p (s c)"), ident_h[:, :])
                    last.then_inc(s_xt, 1)
                    pe.wait_ge(s_xtc[k], r + 1)
                    if isinstance(i, int) and (i, k) == (0, 0):
                        pe.wait_ge(s_wsplit, q + 1)
                    for t in range(BT):
                        for h in range(2):
                            wait_for(pe, s_tabc[h], q * NT + 2 * BT * i + k * BT + t)
                            pe.nop(nofuse=True)
                            for n in range(3):
                                for r in ((h,) if q == 0 else KNOT_ROWS[h]):
                                    into, w = (rel_ps[h], RELW) if q == 0 else (knot_ps[r], K * D)
                                    last = nc.tensor.matmul(into, xt[k][:, t, n // 2, :],
                                                            w_parts[:, n, r * w:(r + 1) * w],
                                                            start=(n == 0), stop=(n == 2))
                            last.then_inc(s_tab[h], 1)

                def node_step(i, k):
                    m = node_use(c, i)
                    pe.wait_ge(s_pre[k], m + 1)
                    pe.wait_ge(s_zx[k], m + 1)
                    wait_for(pe, s_ztc[k], m)
                    pe.nop(nofuse=True)
                    for t in range(BT):
                        last = nc.tensor.transpose(zt_ps_of[c][k][:, t * P:(t + 1) * P], zin[k][:, t * P:(t + 1) * P],
                                                   ident[:, :])
                    last.then_inc(s_zt[k], 1)
                    pe.wait_ge(s_ztc[k], m + 1)
                    if c not in ALONG:
                        wait_for(pe, s_post[k], m)
                    elif not (isinstance(i, int) and (i, k) == (0, 0)):
                        j, l = before(i, k)
                        pe.wait_ge(s_post[l], node_use(c, j) + 1)
                    pe.nop(nofuse=True)
                    lhs, rhs = zt[k], w_pair[c]
                    if c == 2:
                        wait_for(pe, s_bst, 2 * i + k)
                        for g in range(2):
                            last = nc.tensor.matmul(u_ps[:, g, :], w_pair[2][:, :], zt[k][:, g * BW:(g + 1) * BW],
                                                    start=True, stop=True)
                        last.then_inc(s_u, 1)
                        pe.wait_ge(s_uc, 2 * i + k + 1)
                        pe.nop(nofuse=True)
                        for g in range(2):
                            last = nc.tensor.matmul(u_ps[:, g, :], w2[:, :], u_t[k][:, g * BW:(g + 1) * BW],
                                                    start=True, stop=True)
                        lhs, rhs = u_t[k], w2
                    for t in range(BT):
                        last = nc.tensor.matmul(y_ps_of[c][k][:, t * D:(t + 1) * D], lhs[:, t * P:(t + 1) * P], rhs[:, :],
                                                start=True, stop=True)
                    last.then_inc(s_mm[k], 1)
                    if c in ALONG and not (isinstance(i, int) and (i, k) == (0, 0)):
                        table_step(*before(i, k))

                pairs(pe, node_step, c, BP)
                if c in ALONG:
                    table_step(BP - 1, 1)

                if c == 2:
                    pe.wait_ge(s_bnw, 1)
                    for n in range(2):
                        last = nc.tensor.matmul(scratch_ps[:, n * D:(n + 1) * D], bn_wide[:, n, :], ident[0:D, 0:D],
                                                start=True, stop=True)
                    last.then_inc(s_bnt, 1)
                    pairs(pe, table_step, 0, BP)

        @block.vector
        def _(dve):
            steps = [0]

            def link(ins):
                steps[0] += 1
                ins.then_inc(s_setup, 1)
                dve.wait_ge(s_setup, steps[0])

            published = [0]

            def publish(ins):
                published[0] += 1
                ins.then_inc(s_array, 1)
                dve.wait_ge(s_array, published[0])

            V = nc.vector
            tail = slice(FULLBLK * P, NAT)
            V.memset(nats[0].bitcast(I32)[:, tail], 0).then_inc(s_pads, 1)
            V.memset(nats[1].bitcast(I32)[:, tail], 1 << 20).then_inc(s_pads, 1)
            V.memset(nats[2].bitcast(I32)[:, tail], -1).then_inc(s_pads, 1)
            V.memset(nats[2].bitcast(I32)[:, 0:1], -1).then_inc(s_pads, 1)
            V.memset(nats[3].bitcast(I32)[:, tail], 0).then_inc(s_pads, 1)
            V.memset(arena[:, 4 * NAT + 2 * FULLBLK * P:6 * NAT], 0.0).then_inc(s_pads, 1)

            src_i, dst_i, prev_i, typ_i = (nats[n].bitcast(I32) for n in range(4))
            attr = arena[:, 4 * NAT:6 * NAT].rearrange("p (e a) -> p e a", a=2)
            dve.wait_ge(s_src, 48)
            publish(V.tensor_copy(nats[6], src_i))
            dve.wait_ge(s_nat, 14 * 16)
            link(V.tensor_tensor(nats[7], dst_i, prev_i, ALU.is_equal))
            link(V.tensor_copy(keep_nat[0], nats[7]))
            link(V.tensor_scalar(nats[8], nats[7], 0.5, BIG, ALU.subtract, ALU.mult))
            link(V.tensor_tensor(keep_nat[1], nats[8], nats[8], ALU.add))
            dve.sem_inc(s_marks, 1)
            link(V.tensor_scalar(prev_i, dst_i, 7, None, ALU.logical_shift_right))
            link(V.tensor_copy(nats[7], prev_i))
            publish(V.tensor_copy(nats[2], nats[7]))
            link(V.tensor_scalar(dst_i, dst_i, P - 1, None, ALU.bitwise_and))
            link(V.tensor_copy(nats[8], dst_i))
            publish(V.tensor_copy(nats[1], nats[8]))
            link(V.tensor_copy(nats[9], typ_i))
            publish(V.scalar_tensor_tensor(out=nats[3], in0=nats[6], scalar=float(RELS), in1=nats[9], op0=ALU.mult,
                                           op1=ALU.add))
            v, up, whole = nats[7], nats[10], nats[11].bitcast(I32)
            cell, off = (nats[8], nats[9]), (nats[0], nats[12])
            for d in range(2):
                link(V.tensor_scalar(v, attr[:, :, d], float(K - 1), 0.0, ALU.mult, ALU.max))
                link(V.tensor_scalar(v, v, float(K - 1), None, ALU.min))
                link(V.tensor_copy(whole, v))
                link(V.tensor_copy(cell[d], whole))
                link(V.tensor_tensor(up, cell[d], v, ALU.is_gt))
                link(V.tensor_tensor(cell[d], cell[d], up, ALU.subtract))
                link(V.tensor_scalar(cell[d], cell[d], float(K - 2), None, ALU.min))
                link(V.tensor_tensor(off[d], v, cell[d], ALU.subtract))
            row = nats[10]
            link(V.scalar_tensor_tensor(out=row, in0=cell[1], scalar=float(K), in1=cell[0], op0=ALU.mult, op1=ALU.add))
            dve.wait_ge(s_flipped, len(CHUNKS))
            publish(V.scalar_tensor_tensor(out=nats[6], in0=nats[6], scalar=float(KNOTS), in1=row, op0=ALU.mult,
                                           op1=ALU.add))
            rest_ = (nats[4], nats[5])
            for d in range(2):
                link(V.tensor_scalar(rest_[d], off[d], -1.0, 1.0, ALU.mult, ALU.add))
            for s in range(CORNERS):
                publish(V.tensor_tensor(FLIPS[5 + s][0], (rest_[0], off[0])[s % 2], (rest_[1], off[1])[s // 2],
                                        ALU.mult))
            dve.wait_ge(s_consts, 7)
            link(V.tensor_copy(iota_row[:, :], iota_i[:, :]))
            link(V.tensor_copy(node_id[:, :], node_i[:, :]))
            link(V.tensor_copy(ident_h[:, :], ident[:, :]))
            dve.wait_ge(s_weights, 16 * WEIGHT_DMAS)
            link(V.tensor_copy(cut_dst[:, :], cut_dst_i[:, :]))
            for c in range(3, CONVS):
                link(V.tensor_copy(w_pair[c][0:D, :], ident[0:D, 0:D]))
            dve.wait_ge(s_wt, 1)
            for n in range(2):
                last = V.tensor_copy(w_pair[n][:, :], scratch_ps[:, n * D:(n + 1) * D])
            last.then_inc(s_wt_taken, 1)
            dve.wait_ge(s_keep_dram, 64)
            dve.wait_ge(s_flipped, len(CHUNKS) * len(FLIPS))
            V.memset(x3d[:, NT - 1, :], 0.0).then_inc(s_xpad, 1)
            dve.wait_ge(s_wt_taken, 1)

            pre_base, post_base = [0], [0]
            norms = [0]

            def per_node(v):
                return v.rearrange("p (t c) -> p t c", c=D)

            def over_features(v):
                return v.unsqueeze(2).broadcast_to([P, BT, D])

            def over_nodes(v, n=BT):
                return v.unsqueeze(1).broadcast_to([P, n, D])

            def chained(base, per, b):
                done = [0]

                def step(ins):
                    done[0] += 1
                    ins.then_inc(s_post_step if base is post_base else s_pre_step, 1)
                    dve.wait_ge(s_post_step if base is post_base else s_pre_step, base[0] + per * b + done[0])
                    assert done[0] <= per
                return step

            def layer_norm(step, y, res, norm_no):
                step(V.tensor_reduce(ln_s[:, :], per_node(y), AX.X, ALU.add))
                step(V.tensor_scalar(ln_m[:, :], ln_s[:, :], 1.0 / D, None, ALU.mult))
                step(V.tensor_tensor(per_node(ln_c[:, :]), per_node(y), over_features(ln_m[:, :]), ALU.subtract))
                step(V.tensor_tensor(tmp_b[:, :], ln_c[:, :], ln_c[:, :], ALU.mult))
                step(V.tensor_reduce(ln_v[:, :], per_node(tmp_b[:, :]), AX.X, ALU.add))
                V.tensor_scalar(ln_e[:, :], ln_v[:, :], 1.0 / D, EPS, ALU.mult, ALU.add).then_inc(s_var, 1)
                dve.wait_ge(s_std, norm_no + 1)
                step(V.reciprocal(ln_r[:, :], ln_d[:, :]))
                step(V.tensor_tensor(per_node(res), per_node(ln_c[:, :]), over_features(ln_r[:, :]), ALU.mult))

            for c in range(CONVS):
                def hot(i, k):
                    wait_for(dve, s_hist[k], i)
                    g = bass.ds(2 * i + k, 1)
                    for hot_, val, w in ((hi_hot, hi_t, HIS), (lo_hot, lo_t, P)):
                        last = V.tensor_tensor(hot_[k], val[:, g, :].rearrange("p g t -> p (g t)").unsqueeze(2)
                                               .broadcast_to([P, BOX, w]),
                                               iota_row[:, 0:w].unsqueeze(1).broadcast_to([P, BOX, w]), ALU.is_equal)
                    last.then_inc(s_onehot[k], 1)

                def weigh(i, k):
                    n = edge_use(c, i)
                    dve.wait_ge(s_rows_in[c // 3][k], 16 * BOX * (edge_use(c % 3, i) + 1))
                    wait_for(dve, s_turned[k], n)
                    w = basis[:, bass.ds(2 * i + k, 1), :, :].rearrange("p g (h j) s -> p h (g j) s", h=2)
                    rows_ = gathered[k].rearrange("p (j h s c) -> p h j s c", j=GT, h=2, s=RUN)
                    dst = weighted[k].rearrange("p (j s h c) -> p h j s c", j=GT, h=2, s=CORNERS)
                    for h in range(2):
                        for b in range(2):
                            last = V.tensor_tensor(dst[:, h, :, 2 * b:2 * b + 2], rows_[:, h, :, b * K:b * K + 2],
                                                   w[:, h, :, 2 * b:2 * b + 2].unsqueeze(3)
                                                   .broadcast_to([P, GT, 2, D]), ALU.mult)
                    last.then_inc(s_weighted[k], 1)

                def scan(i, k):
                    n = edge_use(c, i)
                    first = isinstance(i, int) and (i, k) == (0, 0)
                    dve.wait_ge(s_turned[k], n + 1)
                    dve.wait_ge(s_keep[k], 32 * (n + 1))
                    wait_for(dve, s_back[k], n)
                    if not first:
                        j, l = before(i, k)
                        dve.wait_ge(s_scanned[l], edge_use(c, j) + 1)
                    init = ((0.0 if MODE[c] == SUM else -BIG) if first
                            else scanned[:, 1 - k, GT * P - 1:GT * P])
                    ops = (ALU.mult, ALU.add) if MODE[c] == SUM else (ALU.min, ALU.max)
                    V.tensor_tensor_scan(scanned[:, k, :], keep[:, k, :], turn_ps[k], init, *ops
                                         ).then_inc(s_scanned[k], 1)

                def edge_step(i, k):
                    if c == 0:
                        hot(i, k)
                    if MODE[c] == MAX:
                        weigh(i, k)
                    if not (isinstance(i, int) and (i, k) == (0, 0)):
                        scan(*before(i, k))

                if c + 1 in TABLE_OF:
                    split_weights(TABLE_OF[c + 1])
                pairs(dve, edge_step, c, GP)
                scan(GP - 1, 1)

                if c == 0:
                    for k in range(2):
                        dve.wait_ge(s_hist[k], GP)
                    found = [1]

                    def find(ins):
                        found[0] += 1
                        ins.then_inc(s_find, 1)
                        dve.wait_ge(s_find, found[0])

                    V.tensor_copy(cnt[:, :], hist_ps).then_inc(s_find, 1)
                    dve.wait_ge(s_pref, 1)
                    find(V.tensor_copy(tot[:, :], scratch_ps[:, P:P + NT]))
                    find(V.tensor_tensor_scan(cum[:, :], ones[:, 0:NT], tot[:, :], 0.0, ALU.mult, ALU.add))
                    find(V.tensor_tensor(cum[:, :], cum[:, :], tot[:, :], ALU.subtract))
                    find(V.tensor_tensor(cum[:, :], cum[:, :], scratch_ps[:, 0:NT], ALU.add))
                    find(V.tensor_scalar(cum[:, :], cum[:, :], 1.0, 0.0, ALU.subtract, ALU.max))
                    find(V.tensor_copy(end_row[:, :], cum[:, :]))
                    find(V.tensor_scalar(nonempty[:, :], cnt[:, :], 0.0, None, ALU.is_gt))
                    find(V.tensor_scalar(tot[:, :], node_id[:, :], cut_dst[:, 0:1], None, ALU.is_equal))
                    find(V.scalar_tensor_tensor(out=straddle[:, :], in0=node_id[:, :], scalar=cut_dst[:, 1:2],
                                                in1=tot[:, :], op0=ALU.is_equal, op1=ALU.mult))
                    find(V.tensor_scalar(straddle_max[:, :], straddle[:, :], 1.0, BIG, ALU.subtract, ALU.mult))
                    dve.sem_inc(s_found, 1)
                    dve.wait_ge(s_x, 32)

                def fix_aggregate(i, k):
                    m = node_use(c, i)
                    step = chained(pre_base, PRE_STEPS - 1, 2 * i + k)
                    dve.wait_ge(s_agg[k], 16 * BT * (m + 1))
                    t = cols(i, k, BT)
                    step(V.tensor_tensor(per_node(pre_a[:, :]), per_node(agg[:, k, :]), over_features(nonempty[:, t]),
                                         ALU.mult))
                    at_cut = (straddle if MODE[c] == SUM else straddle_max)[:, t]
                    step(V.tensor_tensor(per_node(pre_b[:, :]), over_nodes(carry[:, :]), over_features(at_cut),
                                         ALU.mult if MODE[c] == SUM else ALU.add))
                    wait_for(dve, s_zt[k], m)
                    V.tensor_tensor(zin[k].rearrange("p (t c) -> p t c", c=P)[:, :, 0:D], per_node(pre_a[:, :]),
                                    per_node(pre_b[:, :]), ALU.add if MODE[c] == SUM else ALU.max
                                    ).then_inc(s_pre[k], 1)
                    dve.wait_ge(s_pre[k], m + 1)

                def finish_batch(i, k):
                    m, b = node_use(c, i), 2 * i + k
                    step = chained(post_base, POST_STEPS[c], b)
                    dve.wait_ge(s_mm[k], m + 1)
                    if c == 2:
                        end = isinstance(i, int) and (i, k) == (BP - 1, 1)
                        dve.nop(nofuse=True)
                        for g in range(2):
                            w = BW - (NP - N if end and g == 1 else 0)
                            last = V.bn_stats(bn_part[:, bass.ds(2 * b + g, 1), :].rearrange("p g s -> p (g s)"),
                                              u_ps[:, g, 0:w])
                        last.then_inc(s_bst, 1)
                    y, res = y_ps_of[c][k], RES_OF[c][:, cols(i, k, BW)]
                    if c == 2:
                        step(V.tensor_tensor(per_node(res), per_node(y), over_nodes(bias[c][:, :]), ALU.add))
                    else:
                        step(V.tensor_tensor(per_node(tmp_a[:, :]), per_node(y), over_nodes(bias[c][:, :]), ALU.add))
                    if c in (0, 4):
                        step(V.tensor_scalar(res, tmp_a[:, :], 0.0, None, ALU.max))
                    if c in NORMED:
                        step(V.tensor_tensor(tmp_a[:, :], tmp_a[:, :], X[:, cols(i, k, BW)], ALU.add))
                        layer_norm(step, tmp_a[:, :], res, NORMED[c] * BATCHES + b)
                    dve.sem_inc(s_post[k], 1)

                def split_batch(q, i, k):
                    b, parts = 2 * (q * BP + i) + k, x_parts[k]
                    wait_for(dve, s_xt, b - 1)
                    x = per_node(SRC_OF[q][:, cols(i, k, BW)])
                    dve.nop(nofuse=True)

                    def step(n, ins):
                        ins.then_inc(s_split_step, 1)
                        dve.wait_ge(s_split_step, 3 * b + n)

                    step(1, V.tensor_copy(parts[:, :, 0::2, :], x.unsqueeze(2).broadcast_to([P, BT, 2, D])))
                    step(2, V.tensor_tensor(per_node(rest[:, :]), x, parts[:, :, 0, :], ALU.subtract))
                    step(3, V.tensor_copy(parts[:, :, 1, :], per_node(rest[:, :])))
                    V.tensor_tensor(parts[:, :, 3, :], per_node(rest[:, :]), parts[:, :, 1, :], ALU.subtract
                                    ).then_inc(s_xs, 1)
                    dve.wait_ge(s_xs, b + 1)

                def split_weights(q):
                    dve.wait_ge(s_wtab, 32 * (q + 1))
                    if q > 0:
                        for h in range(2):
                            dve.wait_ge(s_tab[h], q * NT)
                    w, n = H[:, 0:TABLE_COLS[q]], TABLE_COLS[q]
                    done = [3 * q]

                    def step(ins):
                        done[0] += 1
                        ins.then_inc(s_wsplit_step, 1)
                        dve.wait_ge(s_wsplit_step, done[0])

                    V.tensor_copy(w_parts[D:P, 2, 0:n], w[D:P, :])
                    step(V.tensor_copy(w_parts[:, 0, 0:n], w))
                    step(V.tensor_tensor(w, w, w_parts[:, 0, 0:n], ALU.subtract))
                    step(V.tensor_copy(w_parts[:, 1, 0:n], w))
                    V.tensor_tensor(w_parts[0:D, 2, 0:n], w[0:D, :], w_parts[0:D, 1, 0:n], ALU.subtract
                                    ).then_inc(s_wsplit, 1)
                    dve.wait_ge(s_wsplit, q + 1)

                def node_step(i, k):
                    fix_aggregate(i, k)
                    if not (isinstance(i, int) and (i, k) == (0, 0)):
                        finish_batch(*before(i, k))
                        if c in ALONG:
                            split_batch(TABLE_OF[c + 1], *before(i, k))

                dve.wait_ge(s_carry, 16 * (c + 1))
                pairs(dve, node_step, c, BP)
                finish_batch(BP - 1, 1)
                if c in ALONG:
                    split_batch(TABLE_OF[c + 1], BP - 1, 1)
                pre_base[0] += (PRE_STEPS - 1) * BATCHES
                post_base[0] += POST_STEPS[c] * BATCHES

                if c == 2:
                    bn = [0]

                    def norm_step(ins):
                        bn[0] += 1
                        ins.then_inc(s_bn, 1)
                        dve.wait_ge(s_bn, bn[0])

                    dve.wait_ge(s_bst, BATCHES)
                    norm_step(V.bn_aggr(bn_all[:, :], bn_part[:, :, :].rearrange("p g s -> p (g s)")))
                    V.tensor_scalar(bn_col[:, 0:1], bn_all[:, 1:2], EPS, None, ALU.add).then_inc(s_bnv, 1)
                    dve.wait_ge(s_bns, 1)
                    norm_step(V.reciprocal(bn_col[:, 2:3], bn_col[:, 1:2]))
                    norm_step(V.tensor_tensor(bn_col[:, 2:3], bn_col[:, 2:3], gamma_col[:, :], ALU.mult))
                    norm_step(V.tensor_tensor(bn_col[:, 3:4], bn_all[:, 0:1], b2_col[:, :], ALU.add))
                    norm_step(V.tensor_scalar(bn_wide[:, 0, :], ones[0:D, :], bn_col[:, 3:4], None, ALU.mult))
                    V.tensor_scalar(bn_wide[:, 1, :], ones[0:D, :], bn_col[:, 2:3], None, ALU.mult).then_inc(s_bnw, 1)
                    dve.wait_ge(s_bnt, 1)
                    norm_step(V.tensor_copy(bn_row[:, :, :].rearrange("p a c -> p (a c)"), scratch_ps[:, 0:2 * D]))

                    def normed_batch(i, k):
                        b = 2 * i + k
                        step = chained(post_base, BN_STEPS, b)
                        step(V.tensor_tensor(per_node(tmp_a[:, :]), per_node(H[:, cols(i, k, BW)]),
                                             over_nodes(bn_row[:, 0, :]), ALU.subtract))
                        step(V.tensor_tensor(per_node(tmp_a[:, :]), per_node(tmp_a[:, :]),
                                             over_nodes(bn_row[:, 1, :]), ALU.mult))
                        step(V.tensor_tensor(per_node(tmp_a[:, :]), per_node(tmp_a[:, :]), over_nodes(beta[:, :]),
                                             ALU.add))
                        step(V.scalar_tensor_tensor(out=tmp_a[:, :], in0=tmp_a[:, :], scalar=0.0,
                                                    in1=X[:, cols(i, k, BW)], op0=ALU.max, op1=ALU.add))
                        layer_norm(step, tmp_a[:, :], X[:, cols(i, k, BW)], NORMED["bn"] * BATCHES + b)
                        dve.sem_inc(s_x2, 1)
                        split_batch(0, i, k)

                    pairs(dve, normed_batch, c, BP)
                    post_base[0] += BN_STEPS * BATCHES


_INS = ['x', 'src', 'dst', 'edge_attr_2', 'edge_type_16', 'L0_gnn_W_rel1', 'L0_gnn_b_rel1', 'L0_gnn_W_root1',
        'L0_gnn_W_rel2', 'L0_gnn_b_rel2', 'L0_gnn_W_root2', 'L1_gnn_W1', 'L1_gnn_b1', 'L1_gnn_W2', 'L1_gnn_b2',
        'L1_gnn_gamma', 'L1_gnn_beta', 'L2_gnn_weight', 'L2_gnn_h_bias', 'L2_gnn_loop_weight', 'L3_gnn_W1',
        'L3_gnn_root1', 'L3_gnn_bias1', 'L3_gnn_W2', 'L3_gnn_root2', 'L3_gnn_bias2']


def kernel(**inputs):
    import numpy as _np
    import concourse.bacc as _bacc
    from concourse import mybir as _mybir
    from concourse.bass_utils import run_bass_kernel_spmd as _run

    nc = _bacc.Bacc("TRN2", target_bir_lowering=False, num_devices=1)
    arrays, args = {}, {}
    for name in _INS:
        a = _np.ascontiguousarray(inputs[name])
        arrays[f"in_{name}_dram"] = a
        args[name] = nc.dram_tensor(f"in_{name}_dram", a.shape, _mybir.dt.from_np(a.dtype), kind="ExternalInput").ap()
    out = nc.dram_tensor("out_0_dram", inputs["x"].shape, _mybir.dt.float32, kind="ExternalOutput").ap()
    build(nc, args, out)
    r = _run(nc, [arrays], core_ids=[0])
    return r.results[0]["out_0_dram"]
```

```python
from contextlib import ExitStack

import concourse.bass as bass
from concourse import mybir

F32 = mybir.dt.float32
BF16 = mybir.dt.bfloat16
I32 = mybir.dt.int32
U32 = mybir.dt.uint32
ALU = mybir.AluOpType
ACT = mybir.ActivationFunctionType
AX = mybir.AxisListType

P = 128
D = 64
N = 12500
E = 200000
RELS = 16
K = 5
KNOTS = K * K
RUN = K + 2
CORNERS = 4
EPS = 1e-5
BIG = 3.3e38

GT = 4
GROUPS = -(-E // (2 * GT * P))
GROUPS += GROUPS % 2
GP = GROUPS // 2
HALF = GROUPS * GT * P
EP = 2 * HALF
TILES = EP // P
NBLK = -(-TILES // P)
NAT = NBLK * P
FULLBLK = E // (P * P)
RESTROWS = (E - FULLBLK * P * P) // P
RESTCOLS = E % P

NT = -(-N // P)
NP = NT * P
LASTROWS = N - (NT - 1) * P
BT = 7
BATCHES = NT // BT
BP = BATCHES // 2
BW = BT * D
HIS = NT
BOX = GT * 2

CONVS = 6
SUM, MAX = 0, 1
MODE = [SUM, SUM, SUM, SUM, MAX, MAX]
ALONG = (3, 4)
RUN_OF = [1, 1, 1, 1, RUN, RUN]
PRE_STEPS = 2
LN_STEPS = 7
POST_STEPS = [2, 2 + LN_STEPS, 1, 2 + LN_STEPS, 2, 2 + LN_STEPS]
BN_STEPS = 4 + LN_STEPS

REL_PARTS = [(0, 6), (6, 11), (11, RELS)]
KNOT_PARTS = [(0, 2), (2, 4), (4, K)]
PARTS = 3
RING = 7
TILES_PER_SLOT = 2 * BT // RING
LAG = 2


def is_pad_tile(g, j):
    return HALF + (g * GT + j) * P >= E


PAD_TILES = [sum(is_pad_tile(GROUPS - 2 + k, j) for j in range(GT)) for k in range(2)]
assert not is_pad_tile(GROUPS - 3, GT - 1)


def wait_for(eng, sem, value):
    if isinstance(value, int) and value <= 0:
        return
    eng.wait_ge(sem, value)


def build(nc, a, out):
    with ExitStack() as ctx:
        def sb(name, shape, dt):
            return ctx.enter_context(nc.sbuf_tensor(name, shape, dt))

        def sem(name):
            return ctx.enter_context(nc.semaphore(name))

        def pair(name):
            return [sem(f"{name}{k}") for k in range(2)]

        def dram(name, shape, dt=F32):
            return nc.dram_tensor(name, shape, dt, kind="Internal").ap()

        rows = dram("scanned_rows", [EP, D])
        h_table = dram("h_table", [NP, D])
        x1_table = dram("x1_table", [NP, D])
        rel_table = dram("rel_table", [NP * RELS, D])
        knot_table = dram("knot_table", [NP * KNOTS, D])
        keep_sum = dram("keep_sum", [EP], BF16)
        keep_max = dram("keep_max", [EP], BF16)

        idx = [sb(f"idx{n}", [P, GROUPS, 2, GT], I32) for n in range(3)]
        basis = sb("basis", [P, GROUPS, BOX, CORNERS], F32)
        X = sb("X", [P, NT * D], F32)
        H = sb("H", [P, NT * D], F32)
        hi_t, lo_t = (H[:, NT * D - (n + 1) * TILES // 2:NT * D - n * TILES // 2].bitcast(BF16)
                      .rearrange("p (g t) -> p g t", t=BOX) for n in range(2))
        ident = sb("ident", [P, P], F32)
        ones = sb("ones", [P, P], F32)
        upto = sb("upto", [P, P], F32)
        iota_row = sb("iota_row", [P, P], BF16)
        node_id = sb("node_id", [P, NT], F32)
        cut_dst_i = sb("cut_dst_i", [P, 2], I32)
        cut_dst = sb("cut_dst", [P, 2], F32)
        cnt = sb("cnt", [P, NT], F32)
        tot = sb("tot", [P, NT], F32)
        cum = sb("cum", [P, NT], F32)
        end_row = sb("end_row", [P, NT], I32)
        nonempty = sb("nonempty", [P, NT], F32)
        straddle = sb("straddle", [P, NT], F32)
        straddle_max = sb("straddle_max", [P, NT], F32)
        carry = sb("carry", [P, D], F32)
        w_pair = [sb(f"w_pair{c}", [P, D], F32) for c in range(CONVS)]
        w2 = sb("w2", [D, D], F32)
        bias_in = ["L0_gnn_b_rel1", "L0_gnn_b_rel2", "L1_gnn_b2", "L2_gnn_h_bias", "L3_gnn_bias1", "L3_gnn_bias2"]
        bias = [sb(f"bias{c}", [P, D], F32) for c in range(CONVS)]
        cols_in = ["L1_gnn_b1", "L1_gnn_b2", "L1_gnn_gamma"]
        b1_col, b2_col, gamma_col = (sb(f"col{n}", [D, 1], F32) for n in range(3))
        beta = sb("beta", [P, D], F32)
        w_parts = sb("w_parts", [P, 3, KNOTS * D], BF16)
        ident_h = sb("ident_h", [P, P], BF16)
        bn_part = sb("bn_part", [D, 2 * BATCHES, 6], F32)
        bn_all = sb("bn_all", [D, 2], F32)
        bn_col = sb("bn_col", [D, 4], F32)
        bn_row = sb("bn_row", [P, 2, D], F32)
        scanned = sb("scanned", [P, 2, GT * P], F32)
        turned_rows = sb("turned_rows", [P, 2, 2, GT * D], F32)
        keep = sb("keep", [P, 2, GT * P], BF16)
        idx_now = sb("idx_now", [P, 2, 2, GT], I32)
        end_now = sb("end_now", [P, 2, BT], I32)
        plain_rows = sb("plain_rows", [P, 2, BOX * D], F32)
        agg = plain_rows[:, :, 0:BW]
        tmp_a = sb("tmp_a", [P, BW], F32)
        tmp_b = sb("tmp_b", [P, BW], F32)
        pre_a, pre_b = tmp_a, tmp_b
        ln_c = sb("ln_c", [P, BW], F32)
        bn_wide = ln_c[0:D, 0:2 * P].rearrange("p (n c) -> p n c", n=2)
        rest = ln_c
        iota_i = tmp_a[:, 0:P].bitcast(I32)
        node_i = tmp_a[:, P:P + NT].bitcast(I32)
        w_raw = ln_c[0:D, 0:4 * D].rearrange("p (n a c) -> p n a c", n=2, a=2)
        ln_s = sb("ln_s", [P, BT], F32)
        ln_m = sb("ln_m", [P, BT], F32)
        ln_v = sb("ln_v", [P, BT], F32)
        ln_e = sb("ln_e", [P, BT], F32)
        ln_d = sb("ln_d", [P, BT], F32)
        ln_r = sb("ln_r", [P, BT], F32)

        arena = sb("arena", [P, RING * KNOTS * D + 3 * BW + 4 * BT * P], F32)
        at = [0]

        def carve(n):
            v = arena[:, at[0]:at[0] + n]
            at[0] += n
            return v

        gathered = [carve(BOX * RUN * D) for _ in range(2)]
        weighted = [carve(BOX * CORNERS * D) for _ in range(2)]
        at = [0]
        ring = [carve(KNOTS * D) for _ in range(RING)]
        x_parts = [carve(3 * BW // 2).bitcast(BF16).rearrange("p (t s c) -> p t s c", s=3, c=D) for _ in range(2)]
        zin = [carve(BT * P) for _ in range(2)]
        zt = [carve(BT * P) for _ in range(2)]
        onehot = [z.bitcast(BF16) for z in zin + zt]
        hi_hot = [o[:, 0:BOX * HIS].rearrange("p (t v) -> p t v", v=HIS) for o in onehot[0:2]]
        lo_hot = [o[:, 0:BOX * P].rearrange("p (t v) -> p t v", v=P) for o in onehot[2:4]]
        nats = [arena[:, n * NAT:(n + 1) * NAT] for n in range(9)]
        keep_nat = [X[:, n * NAT // 2:(n + 1) * NAT // 2].bitcast(BF16) for n in range(2)]
        xt = [v[:, 0:2 * BW].bitcast(BF16).rearrange("p (t s c) -> p t s c", s=2, c=P) for v in
              (scanned.rearrange("p a b -> p (a b)"), turned_rows.rearrange("p a b c -> p (a b c)"))]
        u_t = [w[0:D, 0:BT * P] for w in weighted]

        PS = ctx.enter_context(nc.psum_tensor("PS", [P, 8, 512], F32))
        turn_ps = [PS[:, k, :] for k in range(2)]
        back_ps = [PS[:, 2 + k, :] for k in range(2)]
        hist_ps = PS[:, 4, 0:HIS]
        flip_ps = [PS[:, 5 + k, :] for k in range(2)]
        scratch_ps = PS[:, 7, :]
        zt_ps = [PS[:, 2 * k:2 * k + 2, :].rearrange("p a b -> p (a b)")[:, 0:BT * P] for k in range(2)]
        y_ps = [PS[:, 4 + k, 0:BW] for k in range(2)]
        zt_ps_of = [[zt_ps[0], zt_ps[0]] if c in ALONG + (2,) else zt_ps for c in range(CONVS)]
        y_ps_of = [[PS[:, 7, 0:BW]] * 2 if c in ALONG else y_ps for c in range(CONVS)]
        u_ps, v_ps = PS[0:D, 6:8, 0:BW], PS[0:D, 2:4, 0:BW]
        xt_ps = PS[:, 0:2, :].rearrange("p a b -> p (a b)")[:, 0:2 * BW].bitcast(BF16).rearrange(
            "p (t s c) -> p t s c", s=2, c=P)
        rel_part_ps = [[PS[:, n + h:n + h + 1, 0:(b - a_) * D] for h, (a_, b) in enumerate(REL_PARTS)]
                       for n in (2, 2 + PARTS)]
        knot_part_ps = [PS[:, 2 + a_:2 + b, 0:K * D] for a_, b in KNOT_PARTS]

        def part_ps(q, u, h):
            return knot_part_ps[h] if q else rel_part_ps[u % 2][h]

        PART_COLS = [[(a_ * D, (b - a_) * D) for a_, b in REL_PARTS]] + \
            2 * [[(a_ * K * D, (b - a_) * K * D) for a_, b in KNOT_PARTS]]
        PRODUCTS = [[[(0, a_ * D, b * D)] for a_, b in REL_PARTS]] + \
            2 * [[[(r - a_, r * K * D, (r + 1) * K * D) for r in range(a_, b)] for a_, b in KNOT_PARTS]]

        s_pads = sem("pads_set")
        s_src = sem("src_in")
        s_nat = sem("dst_in")
        s_attr = sem("type_and_attr_in")
        s_consts = sem("constants")
        s_weights = sem("weights_in")
        s_x = sem("x_in")
        s_xpad = sem("x_pad")
        s_setup = sem("setup_steps")
        s_marks = sem("segment_marks")
        s_array = sem("edge_values_ready")
        s_flip = sem("flipped")
        s_flipped = sem("flip_taken")
        s_keep_dram = sem("keep_in_dram")
        s_wt = sem("weights_turned")
        s_wt_taken = sem("turned_weights_taken")
        s_idx = pair("idx_staged")
        s_rows_in = [pair("rows_gathered_a"), pair("rows_gathered_b")]
        s_weighted = pair("rows_weighted")
        s_turned = pair("rows_turned")
        s_keep = pair("keep_in")
        s_scanned = pair("scanned")
        s_back = pair("turned_back")
        s_taken = pair("back_taken")
        s_stored = pair("rows_stored")
        s_onehot = pair("onehots")
        s_hist = pair("counted")
        s_find = sem("last_edges_steps")
        s_pref = sem("prefix_sums")
        s_found = sem("last_edges_found")
        s_carry = sem("carry_in")
        s_end = pair("end_rows_staged")
        s_agg = pair("aggregates_in")
        s_pre_step = sem("pre_steps")
        s_pre = pair("aggregate_fixed")
        s_zx = pair("node_part")
        s_zt = pair("batch_turned")
        s_ztc = pair("turned_batch_taken")
        s_u = sem("hidden")
        s_uc = sem("hidden_taken")
        s_mm = pair("products")
        s_post_step = sem("post_steps")
        s_var = sem("variance")
        s_std = sem("deviation")
        s_post = pair("batch_done")
        s_out = sem("batches_stored")
        s_bn = sem("batch_norm_steps")
        s_bst = sem("batch_statistics")
        s_x2 = sem("normed_batches")
        s_wtab = sem("table_weights_in")
        s_wsplit_step = sem("weight_split_steps")
        s_wsplit = sem("weights_split")
        s_split_step = sem("split_steps")
        s_xs = sem("batch_split")
        s_xt = sem("table_batch_turned")
        s_bnt = sem("batch_norm_totals")
        s_bnv = sem("batch_norm_variance")
        s_bns = sem("batch_norm_deviation")
        s_bnw = sem("batch_norm_columns")
        s_xtc = pair("table_batch_taken")
        s_tab = [sem(f"table_part{h}") for h in range(PARTS)]
        s_tabc = [sem(f"table_part_taken{h}") for h in range(PARTS)]
        s_tabd = [sem(f"table_stored{v}") for v in range(RING)]
        block = ctx.enter_context(nc.Block())

        rows_w = rows.rearrange("(h g p j) c -> p h g (j c)", h=2, g=GROUPS, p=P)
        keeps = [k.rearrange("(h g c) -> h g c", h=2, g=GROUPS) for k in (keep_sum, keep_max)]
        knot_v = knot_table.rearrange("(t p r) c -> t p (r c)", p=P, r=KNOTS)
        rel_v = rel_table.rearrange("(t p r) c -> t p (r c)", p=P, r=RELS)
        h_v = h_table.rearrange("(t p) c -> p t c", p=P)
        x1_v = x1_table.rearrange("(t p) c -> p t c", p=P)
        tables = [a["x"], h_table, x1_table, rel_table, knot_table, knot_table]
        idx_of = [idx[0], idx[0], idx[0], idx[1], idx[2], idx[2]]
        x3d = X[:, :].rearrange("p (t c) -> p t c", c=D)
        TABLE_OF = {3: 0, 4: 1, 5: 2}
        TABLE_COLS = [RELS * D, KNOTS * D, KNOTS * D]
        NORMED = {1: 0, "bn": 1, 3: 2, 5: 3}
        SRC_OF = [X, X, H]
        NODE_OF = [X, H, X, X, X, H]
        RES_OF = [H, X, H, X, H, X]

        def rows_before(c, i, k):
            return 16 * (BOX * edge_use(c % 3, i) - PAD_TILES[k] * (c % 3))

        def rows_with(c, i, k):
            end = isinstance(i, int) and i == GP - 1
            return 16 * (BOX * (edge_use(c % 3, i) + 1) - PAD_TILES[k] * (c % 3 + end))

        def edge_use(c, i):
            return c * GP + i

        def max_use(c, i):
            return (c - MODE.index(MAX)) * GP + i

        def node_use(c, i):
            return c * BP + i

        def pairs(eng, body, c, n, first=0):
            start = first or (1 if c else 2)
            for i in range(start):
                for k in range(2):
                    body(i, k)
            with eng.Fori(start, n - 1) as i:
                for k in range(2):
                    body(i, k)
            for k in range(2):
                body(n - 1, k)

        def before(i, k):
            return (i, 0) if k == 1 else (i - 1, 1)

        def after(i, k):
            return (i, 1) if k == 0 else (i + 1, 0)

        def is_batch(i):
            return not isinstance(i, int) or 0 <= i < BP

        def steps_along(eng, body):
            for k in range(2):
                body(0, k)
            with eng.Fori(1, BP - 1) as i:
                for k in range(2):
                    body(i, k)
            for i in range(BP - 1, BP + 1):
                for k in range(2):
                    body(i, k)

        def cols(i, k, width):
            return bass.ds((2 * i + k) * width, width)

        WEIGHT_DMAS = 2 + 4 + 3 + 3 + CONVS + 1 + 3

        def by_tile(dst):
            return dst.rearrange("p g (h j) -> p g h j", h=2)

        FLIPS = [(nats[6], idx[0]), (nats[2], by_tile(hi_t)), (nats[1], by_tile(lo_t)), (nats[3], idx[1]), (nats[6], idx[2])]
        FLIPS += [(nats[n], by_tile(basis[:, :, :, s])) for s, n in enumerate((0, 8, 1, 3))]
        EARLY = 3
        SETUP_PARTS = 8
        FLIP_IN = {1: (3,), 6: (4,), 7: (5, 6), 8: (7, 8)}
        SETUP_PAIRS = 5
        CHUNKS = [(b, min(4, NBLK - b)) for b in range(0, NBLK, 4)]

        def slot_free(eng, q, i, u):
            wait_for(eng, s_tabd[u % RING], 16 * (TILES_PER_SLOT * (q * BP + i) + u // RING))

        @block.gpsimd
        def _(pool):
            pool.iota(iota_i[:, :], [[1, P]], base=0, channel_multiplier=0).then_inc(s_consts, 1)
            pool.iota(node_i[:, :], [[P, NT]], base=0, channel_multiplier=1).then_inc(s_consts, 1)
            pool.memset(ident[:, :], 0.0).then_inc(s_consts, 1)
            pool.memset(ones[:, :], 1.0).then_inc(s_consts, 1)
            pool.wait_ge(s_consts, 4)
            pool.affine_select(out=ident[:, :], in_=ident[:, :], compare_op=ALU.not_equal, fill=1.0, base=0,
                               pattern=[[-1, P]], channel_multiplier=1).then_inc(s_consts, 1)
            pool.affine_select(out=upto[:, :], in_=ones[:, :], compare_op=ALU.is_ge, fill=0.0, base=0,
                               pattern=[[1, P]], channel_multiplier=-1).then_inc(s_consts, 1)

            for c in range(CONVS):
                width = RUN_OF[c] * D
                if c in (1, 2):
                    pool.wait_ge(s_out, 16 * BATCHES * c)
                if c in TABLE_OF:
                    n = TABLE_OF[c]
                    for v in range(RING):
                        pool.wait_ge(s_tabd[v], 16 * TILES_PER_SLOT * BP * (n + 1))

                def gather_group(i, k):
                    n = edge_use(c, i)
                    pool.wait_ge(s_idx[k], n + 1)
                    if MODE[c] == SUM:
                        wait_for(pool, s_turned[k], n)
                    else:
                        wait_for(pool, s_weighted[k], max_use(c, i))
                    pool.nop(nofuse=True)
                    for j in range(GT):
                        for h in range(2):
                            t = 2 * j + h
                            if isinstance(i, int) and h == 1 and is_pad_tile(2 * i + k, j):
                                continue
                            into = plain_rows[:, k, :] if MODE[c] == SUM else gathered[k]
                            pool.indirect_dma_start(
                                into[:, t * width:(t + 1) * width], None, tables[c],
                                bass.IndirectOffsetOnAxis(ap=idx_now[:, k, h, j:j + 1].bitcast(U32), axis=0),
                            ).then_inc(s_rows_in[c // 3][k], 16)

                pairs(pool, gather_group, c, GP)
                for k in range(2):
                    pool.wait_ge(s_stored[k], 16 * GP * (c + 1))

                def gather_batch(i, k):
                    m = node_use(c, i)
                    pool.wait_ge(s_end[k], m + 1)
                    wait_for(pool, s_pre[k], m)
                    pool.nop(nofuse=True)
                    for t in range(BT):
                        pool.indirect_dma_start(
                            agg[:, k, t * D:(t + 1) * D], None, rows,
                            bass.IndirectOffsetOnAxis(ap=end_now[:, k, t:t + 1].bitcast(U32), axis=0),
                        ).then_inc(s_agg[k], 16)

                pairs(pool, gather_batch, c, BP)

        @block.sync
        def _(sp):
            sp.wait_ge(s_pads, 6)
            def load_edges(tile_, src, w, arrived):
                v = tile_.rearrange("p (b c) -> p b c", b=NBLK)
                n = FULLBLK * P * P
                full = src[0:n * w].rearrange("(b r c) -> r b c", r=P, c=P * w)
                sp.dma_start(v[:, 0:FULLBLK, :], full).then_inc(arrived, 16)
                sp.dma_start(v[0:RESTROWS, FULLBLK, :],
                             src[n * w:(n + RESTROWS * P) * w].rearrange("(r c) -> r c", c=P * w)).then_inc(arrived, 16)
                sp.dma_start(v[RESTROWS:RESTROWS + 1, FULLBLK, 0:RESTCOLS * w],
                             src[(n + RESTROWS * P) * w:E * w].rearrange("(r c) -> r c", r=1)).then_inc(arrived, 16)
            load_edges(nats[0].bitcast(I32), a["src"], 1, s_src)
            load_edges(nats[1].bitcast(I32), a["dst"], 1, s_nat)
            v = nats[2].bitcast(I32).rearrange("p (b c) -> p b c", b=NBLK)
            sp.dma_start(v[0:1, 0, 1:P], a["dst"][0:P - 1].rearrange("(r c) -> r c", r=1)).then_inc(s_nat, 16)
            sp.dma_start(v[1:P, 0, :], a["dst"][P - 1:P * P - 1].rearrange("(r c) -> r c", c=P)).then_inc(s_nat, 16)
            sp.dma_start(v[:, 1:FULLBLK, :], a["dst"][P * P - 1:FULLBLK * P * P - 1].rearrange(
                "(b r c) -> r b c", r=P, c=P)).then_inc(s_nat, 16)
            sp.dma_start(v[0:RESTROWS, FULLBLK, :],
                         a["dst"][FULLBLK * P * P - 1:(FULLBLK * P + RESTROWS) * P - 1].rearrange(
                             "(r c) -> r c", c=P)).then_inc(s_nat, 16)
            sp.dma_start(v[RESTROWS:RESTROWS + 1, FULLBLK, 0:RESTCOLS],
                         a["dst"][(FULLBLK * P + RESTROWS) * P - 1:E - 1].rearrange("(r c) -> r c", r=1)).then_inc(s_nat, 16)
            load_edges(nats[3].bitcast(I32), a["edge_type_16"], 1, s_attr)
            load_edges(arena[:, 4 * NAT:6 * NAT], a["edge_attr_2"].rearrange("e c -> (e c)"), 2, s_attr)
            for h in range(2):
                sp.dma_start(cut_dst_i[:, h:h + 1], a["dst"][HALF - 1 + h:HALF + h].rearrange("(r c) -> r c", r=1)
                             .broadcast_to([P, 1])).then_inc(s_weights, 16)
            for n in range(2):
                sp.dma_start(w_raw[:, n, 0, :], a[f"L0_gnn_W_rel{n + 1}"]).then_inc(s_weights, 16)
                sp.dma_start(w_raw[:, n, 1, :], a[f"L0_gnn_W_root{n + 1}"]).then_inc(s_weights, 16)
            sp.dma_start(w_pair[2][0:D, :], a["L1_gnn_W1"]).then_inc(s_weights, 16)
            sp.dma_start(w_pair[2][D:P, :], a["L1_gnn_W1"]).then_inc(s_weights, 16)
            sp.dma_start(w2[:, :], a["L1_gnn_W2"]).then_inc(s_weights, 16)
            for c, name in ((3, "L2_gnn_loop_weight"), (4, "L3_gnn_root1"), (5, "L3_gnn_root2")):
                sp.dma_start(w_pair[c][D:P, :], a[name]).then_inc(s_weights, 16)
            for c in range(CONVS):
                sp.dma_start(bias[c][:, :], a[bias_in[c]].rearrange("(r c) -> r c", r=1)
                             .broadcast_to([P, D])).then_inc(s_weights, 16)
            sp.dma_start(beta[:, :], a["L1_gnn_beta"].rearrange("(r c) -> r c", r=1)
                         .broadcast_to([P, D])).then_inc(s_weights, 16)
            for col, name in zip((b1_col, b2_col, gamma_col), cols_in):
                sp.dma_start(col[:, :], a[name].rearrange("(r c) -> r c", c=1)).then_inc(s_weights, 16)
            sp.wait_ge(s_marks, 1)
            for n in range(2):
                blocks = TILES // P
                v = keep_nat[n].rearrange("p (b c) -> p b c", b=NBLK)
                dst = (keep_sum, keep_max)[n]
                sp.dma_start(dst[0:blocks * P * P].rearrange("(b r c) -> r b c", r=P, c=P),
                             v[:, 0:blocks, :]).then_inc(s_keep_dram, 16)
                sp.dma_start(dst[blocks * P * P:EP].rearrange("(r c) -> r c", c=P),
                             v[0:TILES - blocks * P, blocks, :]).then_inc(s_keep_dram, 16)
            sp.wait_ge(s_keep_dram, 64)
            def table_weights(c):
                n = TABLE_OF[c]
                w = a["L2_gnn_weight"] if n == 0 else a[f"L3_gnn_W{n}"]
                if n == 1:
                    sp.wait_ge(s_x2, BATCHES)
                for half in range(2):
                    sp.dma_start(H[half * D:(half + 1) * D, 0:TABLE_COLS[n]].rearrange("i (r o) -> i r o", o=D),
                                 w.rearrange("r i o -> i r o")).then_inc(s_wtab, 16)

            for c in range(CONVS):
                marks = keeps[MODE[c]]

                def load_keep(i, k):
                    n = edge_use(c, i)
                    wait_for(sp, s_scanned[k], n)
                    for h in range(2):
                        src = marks[h:h + 1, bass.ds(2 * i + k, 1), :].rearrange("a b c -> (a b) c")
                        sp.dma_start(keep[h * D:(h + 1) * D, k, :], src.broadcast_to([D, GT * P])).then_inc(s_keep[k], 16)

                def store_rows(i, k):
                    n = edge_use(c, i)
                    sp.wait_ge(s_taken[k], n + 1)
                    sp.dma_start(rows_w[:, :, bass.ds(2 * i + k, 1), :].rearrange("p h g c -> p h (g c)"),
                                 turned_rows[:, k, :, :]).then_inc(s_stored[k], 16)

                if c + 1 in TABLE_OF:
                    table_weights(c + 1)
                for k in range(2):
                    load_keep(0, k)
                with sp.Fori(1, GP) as i:
                    for k in range(2):
                        store_rows(i - 1, k)
                        load_keep(i, k)
                for k in range(2):
                    store_rows(GP - 1, k)
                for k in range(2):
                    sp.wait_ge(s_stored[k], 16 * GP * (c + 1))
                sp.dma_start(carry[:, :], rows[HALF - 1:HALF, :].broadcast_to([P, D])).then_inc(s_carry, 16)
                if c in (0, 1, 5):
                    res = RES_OF[c][:, :].rearrange("p (t c) -> p t c", c=D)
                    def store_batch(i, k):
                        m = node_use(c, i)
                        sp.wait_ge(s_post[k], m + 1)
                        t = bass.ds((2 * i + k) * BT, BT)
                        dst = h_v if c == 0 else x1_v
                        if c < 5:
                            sp.dma_start(dst[:, t, :], res[:, t, :]).then_inc(s_out, 16)
                        elif isinstance(i, int) and (i, k) == (BP - 1, 1):
                            t0 = NT - BT
                            sp.dma_start(out[t0 * P:(NT - 1) * P, :].rearrange("(t p) c -> p t c", p=P),
                                         res[:, t0:NT - 1, :]).then_inc(s_out, 16)
                            sp.dma_start(out[(NT - 1) * P:N, :], res[0:LASTROWS, NT - 1, :]).then_inc(s_out, 16)
                        else:
                            sp.dma_start(out[bass.ds((2 * i + k) * BT * P, BT * P), :].rearrange("(t p) c -> p t c", p=P),
                                         res[:, t, :]).then_inc(s_out, 16)
                    pairs(sp, store_batch, c, BP)
                if c + 1 in TABLE_OF:
                    q = TABLE_OF[c + 1]

                    def store_table(i, u):
                        for h in range(PARTS):
                            sp.wait_ge(s_tabc[h], q * NT + 2 * BT * i + u + 1)
                        dst = (rel_v if q == 0 else knot_v)[bass.ds(2 * BT * i + u, 1)].rearrange("t p c -> (t p) c")
                        sp.dma_start(dst, ring[u % RING][:, 0:TABLE_COLS[q]]).then_inc(s_tabd[u % RING], 16)

                    with sp.Fori(0, BP) as i:
                        for u in range(2 * BT):
                            store_table(i, u)
            sp.wait_ge(s_out, 16 * (3 * BATCHES + 1))

        @block.scalar
        def _(act):
            def take_flips(n):
                for q, (b, nb) in enumerate(CHUNKS):
                    f = n * len(CHUNKS) + q
                    act.wait_ge(s_flip, f + 1)
                    done = []
                    for h in range(2):
                        t0, t1 = max(b * P, h * TILES // 2), min((b + nb) * P, (h + 1) * TILES // 2)
                        if t0 < t1:
                            g0, g1 = (t0 - h * TILES // 2) // GT, (t1 - h * TILES // 2) // GT
                            done.append(nc.scalar.copy(
                                FLIPS[n][1][:, g0:g1, h, :],
                                flip_ps[f % 2][:, t0 - b * P:t1 - b * P].rearrange("p (g j) -> p g j", j=GT)))
                    done[-1].then_inc(s_flipped, 1)

            def stage_rows(c, i, k):
                if c == 3 and isinstance(i, int) and i == 0:
                    act.wait_ge(s_rows_in[0][k], rows_with(2, GP - 1, k))
                else:
                    wait_for(act, s_rows_in[c // 3][k], rows_before(c, i, k))
                act.nop(nofuse=True)
                nc.scalar.copy(idx_now[:, k, :, :],
                               idx_of[c][:, bass.ds(2 * i + k, 1), :, :].rearrange("p g h j -> p (g h) j")
                               ).then_inc(s_idx[k], 1)

            take_flips(0)
            act.wait_ge(s_flipped, len(CHUNKS))
            for k in range(2):
                stage_rows(0, 0, k)
            for n in range(1, EARLY):
                take_flips(n)
            act.wait_ge(s_xpad, 1)
            act.dma_start(x3d[:, 0:NT - 1, :], a["x"][0:(NT - 1) * P, :].rearrange("(t p) c -> p t c", p=P)).then_inc(s_x, 16)
            act.dma_start(x3d[0:LASTROWS, NT - 1, :], a["x"][(NT - 1) * P:N, :]).then_inc(s_x, 16)

            for c in range(CONVS):
                def take_back(i, k):
                    n = edge_use(c, i)
                    act.wait_ge(s_back[k], n + 1)
                    wait_for(act, s_stored[k], 16 * n)
                    nc.scalar.copy(turned_rows[:, k, :, :].rearrange("p h (j c) -> p j h c", j=GT),
                                   back_ps[k].rearrange("p (j h c) -> p j h c", j=GT, h=2)).then_inc(s_taken[k], 1)

                def edge_step(i, k):
                    if not (isinstance(i, int) and i == GP - 1):
                        stage_rows(c, i + 1, k)
                    if c == 1 and isinstance(i, int):
                        for n in FLIP_IN.get(2 * i + k, ()):
                            take_flips(n)
                    if not (isinstance(i, int) and (i, k) == (0, 0)):
                        take_back(*before(i, k))

                if c > 0:
                    for k in range(2):
                        stage_rows(c, 0, k)
                pairs(act, edge_step, c, GP, SETUP_PAIRS if c == 1 else 0)
                take_back(GP - 1, 1)

                def stage_ends(i, k):
                    m = node_use(c, i)
                    wait_for(act, s_agg[k], 16 * BT * m)
                    act.nop(nofuse=True)
                    nc.scalar.copy(end_now[:, k, :], end_row[:, cols(i, k, BT)]).then_inc(s_end[k], 1)

                def deviation():
                    nc.scalar.activation(ln_d[:, :], ln_e[:, :], ACT.Sqrt).then_inc(s_std, 1)

                def norm_count(c_, i, k):
                    return c_ * BATCHES + 2 * i + k

                q = TABLE_OF.get(c + 1)

                def take_x(i, k):
                    r = q * BP + i
                    act.wait_ge(s_xt, 2 * r + k + 1)
                    nc.scalar.copy(xt[k], xt_ps).then_inc(s_xtc[k], 1)

                def take_tile(i, k, t):
                    u = k * BT + t
                    slot_free(act, q, i, u)
                    for h in range(PARTS):
                        act.wait_ge(s_tab[h], q * NT + 2 * BT * i + u + 1)
                        v, (start, w) = part_ps(q, u, h), PART_COLS[q][h]
                        nc.scalar.copy(ring[u % RING][:, start:start + w].rearrange("p (r c) -> p r c", r=v.shape[1]),
                                       v).then_inc(s_tabc[h], 1)

                def rel_step(i, k):
                    end = isinstance(i, int) and (i, k) == (BP - 1, 1)
                    for t in range(BT):
                        take_tile(i, k, t)
                        if t == 0 and not end:
                            act.wait_ge(s_var, norm_count(NORMED["bn"], i, k) + 2)
                            deviation()
                        if t == BT - 3 and not end:
                            take_x(*after(i, k))

                def node_part(i, k):
                    m = node_use(c, i)
                    wait_for(act, s_zt[k], m)
                    act.nop(nofuse=True)
                    nc.scalar.copy(zin[k].rearrange("p (t c) -> p t c", c=P)[:, :, D:P],
                                   NODE_OF[c][:, cols(i, k, BW)].rearrange("p (t c) -> p t c", c=D)).then_inc(s_zx[k], 1)

                def take_z(i, k):
                    m = node_use(c, i)
                    act.wait_ge(s_zt[k], m + 1)
                    wait_for(act, s_mm[k], m)
                    nc.scalar.copy(zt[k], zt_ps_of[c][k]).then_inc(s_ztc[k], 1)

                def node_step(i, k):
                    if c != 2:
                        node_part(i, k)
                    elif not (isinstance(i, int) and (i, k) == (BP - 1, 1)):
                        node_part(*after(i, k))
                    if not (isinstance(i, int) and i == BP - 1):
                        stage_ends(i + 1, k)
                    if c != 2:
                        take_z(i, k)
                    else:
                        act.wait_ge(s_u, 2 * i + k + 1)
                        nc.scalar.activation(u_t[k].rearrange("p (a b) -> p a b", a=2), u_ps, ACT.Relu,
                                             bias=b1_col[:, 0:1]).then_inc(s_uc, 1)
                        if not (isinstance(i, int) and (i, k) == (BP - 1, 1)):
                            take_z(*after(i, k))
                    if c in NORMED and not (isinstance(i, int) and (i, k) == (0, 0)):
                        act.wait_ge(s_var, norm_count(NORMED[c], *before(i, k)) + 1)
                        deviation()

                def along_step(i, k):
                    for t in range(BT):
                        if is_batch(i - 1):
                            take_tile(i - 1, k, t)
                        if t == 0:
                            j, l = after(i, k)
                            if is_batch(j):
                                node_part(j, l)
                            if is_batch(i + 1):
                                stage_ends(i + 1, k)
                        if t == 1 and is_batch(i):
                            take_z(i, k)
                        if t == BT - 2:
                            if c in NORMED and is_batch(i):
                                act.wait_ge(s_var, norm_count(NORMED[c], i, k) + 1)
                                deviation()
                            j, l = before(i, k)
                            if is_batch(j):
                                take_x(j, l)

                if c == 0:
                    act.wait_ge(s_found, 1)
                    act.wait_ge(s_x, 32)
                for k in range(2):
                    stage_ends(0, k)
                if c in ALONG:
                    node_part(0, 0)
                    steps_along(act, along_step)
                else:
                    if c == 2:
                        node_part(0, 0)
                        take_z(0, 0)
                    pairs(act, node_step, c, BP)
                    if c in NORMED:
                        act.wait_ge(s_var, norm_count(NORMED[c], BP - 1, 1) + 1)
                        deviation()
                if c == 2:
                    act.wait_ge(s_bnv, 1)
                    nc.scalar.activation(bn_col[:, 1:2], bn_col[:, 0:1], ACT.Sqrt).then_inc(s_bns, 1)
                    act.wait_ge(s_var, norm_count(NORMED["bn"], 0, 0) + 1)
                    deviation()
                    take_x(0, 0)
                    pairs(act, rel_step, c, BP)

        @block.tensor
        def _(pe):
            pe.wait_ge(s_consts, 6)

            def turn_array(n):
                pe.wait_ge(s_array, n + 1)
                for q, (b, nb) in enumerate(CHUNKS):
                    f = n * len(CHUNKS) + q
                    if f >= 2:
                        pe.wait_ge(s_flipped, f - 1)
                    for j in range(nb):
                        last = nc.tensor.transpose(flip_ps[f % 2][:, j * P:(j + 1) * P],
                                                   FLIPS[n][0][:, (b + j) * P:(b + j + 1) * P], ident[:, :])
                    last.then_inc(s_flip, 1)

            for n in range(EARLY):
                turn_array(n)
            pe.wait_ge(s_weights, 16 * WEIGHT_DMAS)
            for n in range(2):
                last = nc.tensor.transpose(scratch_ps[:, n * D:(n + 1) * D],
                                           w_raw[:, n, :, :].rearrange("o a i -> o (a i)"), ident[0:D, 0:D])
            last.then_inc(s_wt, 1)

            for c in range(CONVS):
                def turn(i, k):
                    n = edge_use(c, i)
                    if MODE[c] == SUM:
                        pe.wait_ge(s_rows_in[c // 3][k], rows_with(c, i, k))
                    else:
                        pe.wait_ge(s_weighted[k], max_use(c, i) + 1)
                    wait_for(pe, s_scanned[k], n)
                    pe.nop(nofuse=True)
                    if MODE[c] == SUM:
                        v = plain_rows[:, k, :].rearrange("p (j q) -> p j q", j=GT)
                        for j in range(GT):
                            last = nc.tensor.transpose(turn_ps[k][:, j * P:(j + 1) * P], v[:, j, :], ident[:, :])
                        last.then_inc(s_turned[k], 1)
                    else:
                        v = weighted[k].rearrange("p (j s q) -> p j s q", j=GT, s=CORNERS)
                        for j in range(GT):
                            for s in range(CORNERS):
                                last = nc.tensor.matmul(turn_ps[k][:, j * P:(j + 1) * P], v[:, j, s, :],
                                                        ident[:, :], start=(s == 0), stop=(s == CORNERS - 1))
                        last.then_inc(s_turned[k], 1)

                def count(i, k):
                    pe.wait_ge(s_onehot[k], i + 1)
                    first, end = isinstance(i, int) and (i, k) == (0, 0), isinstance(i, int) and (i, k) == (GP - 1, 1)
                    for t in range(BOX):
                        last = nc.tensor.matmul(hist_ps, lo_hot[k][:, t, :], hi_hot[k][:, t, :],
                                                start=first and t == 0, stop=end and t == BOX - 1,
                                                skip_group_check=True)
                    last.then_inc(s_hist[k], 1)

                def turn_back(i, k):
                    n = edge_use(c, i)
                    pe.wait_ge(s_scanned[k], n + 1)
                    wait_for(pe, s_taken[k], n)
                    pe.nop(nofuse=True)
                    v = scanned[:, k, :].rearrange("q (p j) -> q j p", j=GT)
                    for j in range(GT):
                        last = nc.tensor.transpose(back_ps[k][:, j * P:(j + 1) * P], v[:, j, :], ident[:, :])
                    last.then_inc(s_back[k], 1)

                def edge_step(i, k):
                    turn(i, k)
                    if c == 0:
                        count(i, k)
                    if c == 1 and isinstance(i, int):
                        for n in FLIP_IN.get(2 * i + k, ()):
                            turn_array(n)
                    if not (isinstance(i, int) and (i, k) == (0, 0)):
                        turn_back(*before(i, k))

                pairs(pe, edge_step, c, GP, SETUP_PAIRS if c == 1 else 0)
                turn_back(GP - 1, 1)

                if c == 0:
                    pe.wait_ge(s_wt_taken, 1)
                    pe.wait_ge(s_find, 1)
                    nc.tensor.matmul(scratch_ps[:, 0:NT], upto[:, :], cnt[:, :], start=True, stop=True)
                    nc.tensor.matmul(scratch_ps[:, P:P + NT], ones[:, :], cnt[:, :], start=True,
                                     stop=True).then_inc(s_pref, 1)

                q = TABLE_OF.get(c + 1)

                def turn_x(i, k):
                    r = q * BP + i
                    pe.wait_ge(s_xs, 2 * r + k + 1)
                    wait_for(pe, s_xtc[1 - k], r + k)
                    pe.nop(nofuse=True)
                    for t in range(BT):
                        for s in range(2):
                            last = nc.tensor.transpose(xt_ps[:, t, s, :], x_parts[k][:, t, s:s + 2, :]
                                                       .rearrange("p s c -> p (s c)"), ident_h[:, :])
                    last.then_inc(s_xt, 1)

                def table_tile(i, k, t):
                    if t == 0:
                        pe.wait_ge(s_xtc[k], q * BP + i + 1)
                        if isinstance(i, int) and (i, k) == (0, 0):
                            pe.wait_ge(s_wsplit, q + 1)
                    for h in range(PARTS):
                        wait_for(pe, s_tabc[h], q * NT + 2 * BT * i + k * BT + t - (0 if q else 1))
                        pe.nop(nofuse=True)
                        for n in range(3):
                            for bank, from_, to in PRODUCTS[q][h]:
                                last = nc.tensor.matmul(part_ps(q, k * BT + t, h)[:, bank, :], xt[k][:, t, n // 2, :],
                                                        w_parts[:, n, from_:to], start=(n == 0), stop=(n == 2))
                        last.then_inc(s_tab[h], 1)

                def rel_step(i, k):
                    for t in range(BT):
                        table_tile(i, k, t)
                        if t == BT - 3 and not (isinstance(i, int) and (i, k) == (BP - 1, 1)):
                            turn_x(*after(i, k))

                def turn_z(i, k):
                    m = node_use(c, i)
                    pe.wait_ge(s_pre[k], m + 1)
                    pe.wait_ge(s_zx[k], m + 1)
                    wait_for(pe, s_ztc[k], m)
                    pe.nop(nofuse=True)
                    for t in range(BT):
                        last = nc.tensor.transpose(zt_ps_of[c][k][:, t * P:(t + 1) * P], zin[k][:, t * P:(t + 1) * P],
                                                   ident[:, :])
                    last.then_inc(s_zt[k], 1)

                def multiply(i, k):
                    m = node_use(c, i)
                    pe.wait_ge(s_ztc[k], m + 1)
                    if c not in ALONG:
                        wait_for(pe, s_post[k], m)
                    elif not (isinstance(i, int) and (i, k) == (0, 0)):
                        j, l = before(i, k)
                        pe.wait_ge(s_post[l], node_use(c, j) + 1)
                    pe.nop(nofuse=True)
                    lhs, rhs = zt[k], w_pair[c]
                    if c == 2:
                        for g in range(2):
                            last = nc.tensor.matmul(u_ps[:, g, :], w_pair[2][:, :], zt[k][:, g * BW:(g + 1) * BW],
                                                    start=True, stop=True)
                        last.then_inc(s_u, 1)
                        if not (isinstance(i, int) and (i, k) == (BP - 1, 1)):
                            turn_z(*after(i, k))
                        wait_for(pe, s_bst, 2 * i + k)
                        pe.wait_ge(s_uc, 2 * i + k + 1)
                        pe.nop(nofuse=True)
                        for g in range(2):
                            last = nc.tensor.matmul(v_ps[:, g, :], w2[:, :], u_t[k][:, g * BW:(g + 1) * BW],
                                                    start=True, stop=True)
                        lhs, rhs = u_t[k], w2
                    for t in range(BT):
                        last = nc.tensor.matmul(y_ps_of[c][k][:, t * D:(t + 1) * D], lhs[:, t * P:(t + 1) * P], rhs[:, :],
                                                start=True, stop=True)
                    last.then_inc(s_mm[k], 1)

                def node_step(i, k):
                    if c != 2:
                        turn_z(i, k)
                    multiply(i, k)

                def along_step(i, k):
                    for t in range(BT):
                        if is_batch(i - 1):
                            table_tile(i - 1, k, t)
                        if t == 1 and is_batch(i):
                            turn_z(i, k)
                        if t == 3 and is_batch(i):
                            multiply(i, k)
                        if t == BT - 2:
                            j, l = before(i, k)
                            if is_batch(j):
                                turn_x(j, l)

                if c in ALONG:
                    steps_along(pe, along_step)
                else:
                    if c == 2:
                        turn_z(0, 0)
                    pairs(pe, node_step, c, BP)

                if c == 2:
                    pe.wait_ge(s_bnw, 1)
                    for n in range(2):
                        last = nc.tensor.matmul(scratch_ps[:, n * D:(n + 1) * D], bn_wide[:, n, :], ident[0:D, 0:D],
                                                start=True, stop=True)
                    last.then_inc(s_bnt, 1)
                    turn_x(0, 0)
                    pairs(pe, rel_step, c, BP)

        @block.vector
        def _(dve):
            steps = [0]

            def link(ins):
                steps[0] += 1
                ins.then_inc(s_setup, 1)
                dve.wait_ge(s_setup, steps[0])

            published = [0]

            def publish(ins):
                published[0] += 1
                ins.then_inc(s_array, 1)
                dve.wait_ge(s_array, published[0])

            V = nc.vector
            tail = slice(FULLBLK * P, NAT)
            V.memset(nats[0].bitcast(I32)[:, tail], 0).then_inc(s_pads, 1)
            V.memset(nats[1].bitcast(I32)[:, tail], 1 << 20).then_inc(s_pads, 1)
            V.memset(nats[2].bitcast(I32)[:, tail], -1).then_inc(s_pads, 1)
            V.memset(nats[2].bitcast(I32)[:, 0:1], -1).then_inc(s_pads, 1)
            V.memset(nats[3].bitcast(I32)[:, tail], 0).then_inc(s_pads, 1)
            V.memset(arena[:, 4 * NAT + 2 * FULLBLK * P:6 * NAT], 0.0).then_inc(s_pads, 1)

            src_i, dst_i, prev_i, typ_i = (nats[n].bitcast(I32) for n in range(4))
            attr = arena[:, 4 * NAT:6 * NAT].rearrange("p (e a) -> p e a", a=2)
            dve.wait_ge(s_src, 48)
            publish(V.tensor_copy(nats[6], src_i))
            dve.wait_ge(s_nat, 8 * 16)
            link(V.tensor_tensor(nats[7], dst_i, prev_i, ALU.is_equal))
            link(V.tensor_copy(keep_nat[0], nats[7]))
            link(V.tensor_scalar(nats[8], nats[7], 0.5, BIG, ALU.subtract, ALU.mult))
            link(V.tensor_tensor(keep_nat[1], nats[8], nats[8], ALU.add))
            dve.sem_inc(s_marks, 1)
            link(V.tensor_scalar(prev_i, dst_i, 7, None, ALU.logical_shift_right))
            link(V.tensor_copy(nats[7], prev_i))
            publish(V.tensor_copy(nats[2], nats[7]))
            link(V.tensor_scalar(dst_i, dst_i, P - 1, None, ALU.bitwise_and))
            link(V.tensor_copy(nats[8], dst_i))
            publish(V.tensor_copy(nats[1], nats[8]))

            def setup_part(n):
                v, up, whole, off = nats[7], nats[8], nats[0].bitcast(I32), (nats[2], nats[7])
                cell = (nats[1], nats[3])
                d = (n - 1) // 2
                if n == 0:
                    dve.wait_ge(s_attr, 6 * 16)
                    link(V.tensor_copy(nats[7], typ_i))
                    publish(V.scalar_tensor_tensor(out=nats[3], in0=nats[6], scalar=float(RELS), in1=nats[7],
                                                   op0=ALU.mult, op1=ALU.add))
                elif n in (1, 3):
                    link(V.tensor_scalar(v, attr[:, :, d], float(K - 1), 0.0, ALU.mult, ALU.max))
                    link(V.tensor_scalar(v, v, float(K - 1), None, ALU.min))
                    link(V.tensor_copy(whole, v))
                    dve.wait_ge(s_flipped, len(CHUNKS) * (EARLY + d))
                    link(V.tensor_copy(cell[d], whole))
                elif n in (2, 4):
                    link(V.tensor_tensor(up, cell[d], v, ALU.is_gt))
                    link(V.tensor_tensor(cell[d], cell[d], up, ALU.subtract))
                    link(V.tensor_scalar(cell[d], cell[d], float(K - 2), None, ALU.min))
                    link(V.tensor_tensor(off[d], v, cell[d], ALU.subtract))
                elif n == 5:
                    row = nats[8]
                    link(V.scalar_tensor_tensor(out=row, in0=cell[1], scalar=float(K), in1=cell[0], op0=ALU.mult,
                                                op1=ALU.add))
                    publish(V.scalar_tensor_tensor(out=nats[6], in0=nats[6], scalar=float(KNOTS), in1=row, op0=ALU.mult,
                                                   op1=ALU.add))
                    for d in range(2):
                        link(V.tensor_scalar((nats[4], nats[5])[d], off[d], -1.0, 1.0, ALU.mult, ALU.add))
                else:
                    for s in range(2 * (n - 6), 2 * (n - 5)):
                        publish(V.tensor_tensor(FLIPS[5 + s][0], (nats[4], off[0])[s % 2], (nats[5], off[1])[s // 2],
                                                ALU.mult))

            dve.wait_ge(s_consts, 6)
            link(V.tensor_copy(iota_row[:, :], iota_i[:, :]))
            link(V.tensor_copy(node_id[:, :], node_i[:, :]))
            link(V.tensor_copy(ident_h[:, :], ident[:, :]))
            dve.wait_ge(s_weights, 16 * WEIGHT_DMAS)
            link(V.tensor_copy(cut_dst[:, :], cut_dst_i[:, :]))
            for c in range(3, CONVS):
                link(V.tensor_copy(w_pair[c][0:D, :], ident[0:D, 0:D]))
            dve.wait_ge(s_wt, 1)
            for n in range(2):
                last = V.tensor_copy(w_pair[n][:, :], scratch_ps[:, n * D:(n + 1) * D])
            last.then_inc(s_wt_taken, 1)
            dve.wait_ge(s_keep_dram, 64)
            V.memset(x3d[:, NT - 1, :], 0.0).then_inc(s_xpad, 1)
            dve.wait_ge(s_wt_taken, 1)

            pre_base, post_base = [0], [0]

            def per_node(v):
                return v.rearrange("p (t c) -> p t c", c=D)

            def over_features(v):
                return v.unsqueeze(2).broadcast_to([P, BT, D])

            def over_nodes(v, n=BT):
                return v.unsqueeze(1).broadcast_to([P, n, D])

            def chained(base, per, b):
                done = [0]

                def step(ins):
                    done[0] += 1
                    ins.then_inc(s_post_step if base is post_base else s_pre_step, 1)
                    dve.wait_ge(s_post_step if base is post_base else s_pre_step, base[0] + per * b + done[0])
                    assert done[0] <= per
                return step

            def layer_norm(step, y, res, norm_no):
                step(V.tensor_reduce(ln_s[:, :], per_node(y), AX.X, ALU.add))
                step(V.tensor_scalar(ln_m[:, :], ln_s[:, :], 1.0 / D, None, ALU.mult))
                step(V.tensor_tensor(per_node(ln_c[:, :]), per_node(y), over_features(ln_m[:, :]), ALU.subtract))
                step(V.tensor_tensor(tmp_b[:, :], ln_c[:, :], ln_c[:, :], ALU.mult))
                step(V.tensor_reduce(ln_v[:, :], per_node(tmp_b[:, :]), AX.X, ALU.add))
                V.tensor_scalar(ln_e[:, :], ln_v[:, :], 1.0 / D, EPS, ALU.mult, ALU.add).then_inc(s_var, 1)
                dve.wait_ge(s_std, norm_no + 1)
                step(V.reciprocal(ln_r[:, :], ln_d[:, :]))
                step(V.tensor_tensor(per_node(res), per_node(ln_c[:, :]), over_features(ln_r[:, :]), ALU.mult))

            for c in range(CONVS):
                def hot(i, k):
                    wait_for(dve, s_hist[k], i)
                    g = bass.ds(2 * i + k, 1)
                    for hot_, val, w in ((hi_hot, hi_t, HIS), (lo_hot, lo_t, P)):
                        last = V.tensor_tensor(hot_[k], val[:, g, :].rearrange("p g t -> p (g t)").unsqueeze(2)
                                               .broadcast_to([P, BOX, w]),
                                               iota_row[:, 0:w].unsqueeze(1).broadcast_to([P, BOX, w]), ALU.is_equal)
                    last.then_inc(s_onehot[k], 1)

                def weigh(i, k):
                    n = edge_use(c, i)
                    dve.wait_ge(s_rows_in[c // 3][k], rows_with(c, i, k))
                    wait_for(dve, s_turned[k], n)
                    w = basis[:, bass.ds(2 * i + k, 1), :, :].rearrange("p g (h j) s -> p h (g j) s", h=2)
                    rows_ = gathered[k].rearrange("p (j h s c) -> p h j s c", j=GT, h=2, s=RUN)
                    dst = weighted[k].rearrange("p (j s h c) -> p h j s c", j=GT, h=2, s=CORNERS)
                    for h in range(2):
                        for b in range(2):
                            last = V.tensor_tensor(dst[:, h, :, 2 * b:2 * b + 2], rows_[:, h, :, b * K:b * K + 2],
                                                   w[:, h, :, 2 * b:2 * b + 2].unsqueeze(3)
                                                   .broadcast_to([P, GT, 2, D]), ALU.mult)
                    last.then_inc(s_weighted[k], 1)

                def scan(i, k):
                    n = edge_use(c, i)
                    first = isinstance(i, int) and (i, k) == (0, 0)
                    dve.wait_ge(s_turned[k], n + 1)
                    dve.wait_ge(s_keep[k], 32 * (n + 1))
                    wait_for(dve, s_back[k], n)
                    if not first:
                        j, l = before(i, k)
                        dve.wait_ge(s_scanned[l], edge_use(c, j) + 1)
                    init = ((0.0 if MODE[c] == SUM else -BIG) if first
                            else scanned[:, 1 - k, GT * P - 1:GT * P])
                    ops = (ALU.mult, ALU.add) if MODE[c] == SUM else (ALU.min, ALU.max)
                    V.tensor_tensor_scan(scanned[:, k, :], keep[:, k, :], turn_ps[k], init, *ops
                                         ).then_inc(s_scanned[k], 1)

                def edge_step(i, k):
                    if c == 0:
                        hot(i, k)
                    if MODE[c] == MAX:
                        weigh(i, k)
                    if not (isinstance(i, int) and (i, k) == (0, 0)):
                        scan(*before(i, k))
                    if c == 1 and isinstance(i, int) and 2 * i + k < SETUP_PARTS:
                        setup_part(2 * i + k)

                if c + 1 in TABLE_OF:
                    split_weights(TABLE_OF[c + 1])
                pairs(dve, edge_step, c, GP, SETUP_PAIRS if c == 1 else 0)
                scan(GP - 1, 1)

                if c == 0:
                    for k in range(2):
                        dve.wait_ge(s_hist[k], GP)
                    found = [1]

                    def find(ins):
                        found[0] += 1
                        ins.then_inc(s_find, 1)
                        dve.wait_ge(s_find, found[0])

                    V.tensor_copy(cnt[:, :], hist_ps).then_inc(s_find, 1)
                    dve.wait_ge(s_pref, 1)
                    find(V.tensor_copy(tot[:, :], scratch_ps[:, P:P + NT]))
                    find(V.tensor_tensor_scan(cum[:, :], ones[:, 0:NT], tot[:, :], 0.0, ALU.mult, ALU.add))
                    find(V.tensor_tensor(cum[:, :], cum[:, :], tot[:, :], ALU.subtract))
                    find(V.tensor_tensor(cum[:, :], cum[:, :], scratch_ps[:, 0:NT], ALU.add))
                    find(V.tensor_scalar(cum[:, :], cum[:, :], 1.0, 0.0, ALU.subtract, ALU.max))
                    find(V.tensor_copy(end_row[:, :], cum[:, :]))
                    find(V.tensor_scalar(nonempty[:, :], cnt[:, :], 0.0, None, ALU.is_gt))
                    find(V.tensor_scalar(tot[:, :], node_id[:, :], cut_dst[:, 0:1], None, ALU.is_equal))
                    find(V.scalar_tensor_tensor(out=straddle[:, :], in0=node_id[:, :], scalar=cut_dst[:, 1:2],
                                                in1=tot[:, :], op0=ALU.is_equal, op1=ALU.mult))
                    find(V.tensor_scalar(straddle_max[:, :], straddle[:, :], 1.0, BIG, ALU.subtract, ALU.mult))
                    dve.sem_inc(s_found, 1)
                    dve.wait_ge(s_x, 32)

                def fix_aggregate(i, k):
                    m = node_use(c, i)
                    step = chained(pre_base, PRE_STEPS, 2 * i + k)
                    dve.wait_ge(s_agg[k], 16 * BT * (m + 1))
                    t = cols(i, k, BT)
                    step(V.tensor_tensor(per_node(pre_a[:, :]), per_node(agg[:, k, :]), over_features(nonempty[:, t]),
                                         ALU.mult))
                    at_cut = (straddle if MODE[c] == SUM else straddle_max)[:, t]
                    step(V.tensor_tensor(per_node(pre_b[:, :]), over_nodes(carry[:, :]), over_features(at_cut),
                                         ALU.mult if MODE[c] == SUM else ALU.add))
                    wait_for(dve, s_zt[k], m)
                    V.tensor_tensor(zin[k].rearrange("p (t c) -> p t c", c=P)[:, :, 0:D], per_node(pre_a[:, :]),
                                    per_node(pre_b[:, :]), ALU.add if MODE[c] == SUM else ALU.max
                                    ).then_inc(s_pre[k], 1)
                    dve.wait_ge(s_pre[k], m + 1)

                def finish_batch(i, k):
                    m, b = node_use(c, i), 2 * i + k
                    step = chained(post_base, POST_STEPS[c], b)
                    dve.wait_ge(s_mm[k], m + 1)
                    if c == 2:
                        end = isinstance(i, int) and (i, k) == (BP - 1, 1)
                        dve.nop(nofuse=True)
                        for g in range(2):
                            w = BW - (NP - N if end and g == 1 else 0)
                            last = V.bn_stats(bn_part[:, bass.ds(2 * b + g, 1), :].rearrange("p g s -> p (g s)"),
                                              v_ps[:, g, 0:w])
                        last.then_inc(s_bst, 1)
                    y, res = y_ps_of[c][k], RES_OF[c][:, cols(i, k, BW)]
                    if c == 2:
                        step(V.tensor_tensor(per_node(res), per_node(y), over_nodes(bias[c][:, :]), ALU.add))
                    else:
                        step(V.tensor_tensor(per_node(tmp_a[:, :]), per_node(y), over_nodes(bias[c][:, :]), ALU.add))
                    if c in (0, 4):
                        step(V.tensor_scalar(res, tmp_a[:, :], 0.0, None, ALU.max))
                    if c in NORMED:
                        step(V.tensor_tensor(tmp_a[:, :], tmp_a[:, :], X[:, cols(i, k, BW)], ALU.add))
                        layer_norm(step, tmp_a[:, :], res, NORMED[c] * BATCHES + b)
                    dve.sem_inc(s_post[k], 1)

                def split_batch(q, i, k):
                    b, parts = 2 * (q * BP + i) + k, x_parts[k]
                    wait_for(dve, s_xt, b - 1)
                    x = per_node(SRC_OF[q][:, cols(i, k, BW)])
                    dve.nop(nofuse=True)

                    def step(n, ins):
                        ins.then_inc(s_split_step, 1)
                        dve.wait_ge(s_split_step, 3 * b + n)

                    step(1, V.tensor_copy(parts[:, :, 1, :], x))
                    step(2, V.tensor_tensor(per_node(rest[:, :]), x, parts[:, :, 1, :], ALU.subtract))
                    step(3, V.tensor_copy(parts[:, :, 0, :], per_node(rest[:, :])))
                    V.tensor_tensor(parts[:, :, 2, :], per_node(rest[:, :]), parts[:, :, 0, :], ALU.subtract
                                    ).then_inc(s_xs, 1)
                    dve.wait_ge(s_xs, b + 1)

                def split_weights(q):
                    dve.wait_ge(s_wtab, 32 * (q + 1))
                    if q > 0:
                        for h in range(PARTS):
                            dve.wait_ge(s_tab[h], q * NT)
                    w, n = H[:, 0:TABLE_COLS[q]], TABLE_COLS[q]
                    done = [3 * q]

                    def step(ins):
                        done[0] += 1
                        ins.then_inc(s_wsplit_step, 1)
                        dve.wait_ge(s_wsplit_step, done[0])

                    V.tensor_copy(w_parts[D:P, 2, 0:n], w[D:P, :])
                    step(V.tensor_copy(w_parts[:, 0, 0:n], w))
                    step(V.tensor_tensor(w, w, w_parts[:, 0, 0:n], ALU.subtract))
                    step(V.tensor_copy(w_parts[:, 1, 0:n], w))
                    V.tensor_tensor(w_parts[0:D, 2, 0:n], w[0:D, :], w_parts[0:D, 1, 0:n], ALU.subtract
                                    ).then_inc(s_wsplit, 1)
                    dve.wait_ge(s_wsplit, q + 1)

                def node_step(i, k):
                    fix_aggregate(i, k)
                    if not (isinstance(i, int) and (i, k) == (0, 0)):
                        finish_batch(*before(i, k))
                        if c in ALONG:
                            split_batch(TABLE_OF[c + 1], *before(i, k))

                dve.wait_ge(s_carry, 16 * (c + 1))
                pairs(dve, node_step, c, BP)
                finish_batch(BP - 1, 1)
                if c in ALONG:
                    split_batch(TABLE_OF[c + 1], BP - 1, 1)
                pre_base[0] += PRE_STEPS * BATCHES
                post_base[0] += POST_STEPS[c] * BATCHES

                if c == 2:
                    bn = [0]

                    def norm_step(ins):
                        bn[0] += 1
                        ins.then_inc(s_bn, 1)
                        dve.wait_ge(s_bn, bn[0])

                    dve.wait_ge(s_bst, BATCHES)
                    norm_step(V.bn_aggr(bn_all[:, :], bn_part[:, :, :].rearrange("p g s -> p (g s)")))
                    V.tensor_scalar(bn_col[:, 0:1], bn_all[:, 1:2], EPS, None, ALU.add).then_inc(s_bnv, 1)
                    dve.wait_ge(s_bns, 1)
                    norm_step(V.reciprocal(bn_col[:, 2:3], bn_col[:, 1:2]))
                    norm_step(V.tensor_tensor(bn_col[:, 2:3], bn_col[:, 2:3], gamma_col[:, :], ALU.mult))
                    norm_step(V.tensor_tensor(bn_col[:, 3:4], bn_all[:, 0:1], b2_col[:, :], ALU.add))
                    norm_step(V.tensor_scalar(bn_wide[:, 0, :], ones[0:D, :], bn_col[:, 3:4], None, ALU.mult))
                    V.tensor_scalar(bn_wide[:, 1, :], ones[0:D, :], bn_col[:, 2:3], None, ALU.mult).then_inc(s_bnw, 1)
                    dve.wait_ge(s_bnt, 1)
                    norm_step(V.tensor_copy(bn_row[:, :, :].rearrange("p a c -> p (a c)"), scratch_ps[:, 0:2 * D]))

                    def normed_batch(i, k):
                        b = 2 * i + k
                        step = chained(post_base, BN_STEPS, b)
                        step(V.tensor_tensor(per_node(tmp_a[:, :]), per_node(H[:, cols(i, k, BW)]),
                                             over_nodes(bn_row[:, 0, :]), ALU.subtract))
                        step(V.tensor_tensor(per_node(tmp_a[:, :]), per_node(tmp_a[:, :]),
                                             over_nodes(bn_row[:, 1, :]), ALU.mult))
                        step(V.tensor_tensor(per_node(tmp_a[:, :]), per_node(tmp_a[:, :]), over_nodes(beta[:, :]),
                                             ALU.add))
                        step(V.scalar_tensor_tensor(out=tmp_a[:, :], in0=tmp_a[:, :], scalar=0.0,
                                                    in1=X[:, cols(i, k, BW)], op0=ALU.max, op1=ALU.add))
                        layer_norm(step, tmp_a[:, :], X[:, cols(i, k, BW)], NORMED["bn"] * BATCHES + b)
                        dve.sem_inc(s_x2, 1)
                        split_batch(0, i, k)

                    pairs(dve, normed_batch, c, BP)
                    post_base[0] += BN_STEPS * BATCHES


_INS = ['x', 'src', 'dst', 'edge_attr_2', 'edge_type_16', 'L0_gnn_W_rel1', 'L0_gnn_b_rel1', 'L0_gnn_W_root1',
        'L0_gnn_W_rel2', 'L0_gnn_b_rel2', 'L0_gnn_W_root2', 'L1_gnn_W1', 'L1_gnn_b1', 'L1_gnn_W2', 'L1_gnn_b2',
        'L1_gnn_gamma', 'L1_gnn_beta', 'L2_gnn_weight', 'L2_gnn_h_bias', 'L2_gnn_loop_weight', 'L3_gnn_W1',
        'L3_gnn_root1', 'L3_gnn_bias1', 'L3_gnn_W2', 'L3_gnn_root2', 'L3_gnn_bias2']


def kernel(**inputs):
    import numpy as _np
    import concourse.bacc as _bacc
    from concourse import mybir as _mybir
    from concourse.bass_utils import run_bass_kernel_spmd as _run

    nc = _bacc.Bacc("TRN2", target_bir_lowering=False, num_devices=1)
    arrays, args = {}, {}
    for name in _INS:
        a = _np.ascontiguousarray(inputs[name])
        arrays[f"in_{name}_dram"] = a
        args[name] = nc.dram_tensor(f"in_{name}_dram", a.shape, _mybir.dt.from_np(a.dtype), kind="ExternalInput").ap()
    out = nc.dram_tensor("out_0_dram", inputs["x"].shape, _mybir.dt.float32, kind="ExternalOutput").ap()
    build(nc, args, out)
    r = _run(nc, [arrays], core_ids=[0])
    return r.results[0]["out_0_dram"]
```
